# Optimizing a Trainium2 kernel written in Bass

```python
import numpy as np
import jax
import jax.numpy as jnp

def _softmax(x, axis=-1):
    return jax.nn.softmax(x, axis=axis)

def _gelu(x):
    return jax.nn.gelu(x, approximate=True)

def _silu(x):
    return jax.nn.silu(x)

def _sigmoid(x):
    return jax.nn.sigmoid(x)

def _layernorm(x, axis=-1, eps=1e-05):
    m = jnp.mean(x, axis=axis, keepdims=True)
    v = jnp.var(x, axis=axis, keepdims=True)
    return (x - m) / jnp.sqrt(v + eps)

def _scatter_add(tgt, idx, src, axis=0):
    return tgt.at[idx].add(src)

def _segment_sum(src, seg, n):
    return jax.ops.segment_sum(src, seg, n)
kernel_name = 'mk_sandwich_d2_jaxref_r8_3ded7b'

def setup_inputs(seed: int=0):
    np.random.seed(seed)
    _w = jnp.asarray

    def _L0_attn_setup():
        import jax, jax.numpy as jnp
        import numpy as np
        from functools import partial
        BATCH, SEQ = (2, 256)
        D_MODEL, D_INNER, D_XB = (256, 512, 128)
        HEADDIM, D_STATE = (64, 64)
        NHEADS = D_INNER // HEADDIM
        NKV = D_XB // HEADDIM
        REP = NHEADS // NKV
        INTER = 1024
        EPS = 1e-05
        D_IN_PROJ = D_INNER + D_XB + D_XB + D_INNER + NHEADS

        def _layernorm(x, w, b):
            mu = x.mean(-1, keepdims=True)
            var = ((x - mu) ** 2).mean(-1, keepdims=True)
            return (x - mu) * jax.lax.rsqrt(var + EPS) * w + b

        def _ssd_scan(xh, dt, A, Bh, Ch):
            dA = jnp.exp(dt * A)
            to_l = lambda t: jnp.moveaxis(t, 1, 0)

            def step(state, inp):
                dA_t, dt_t, x_t, B_t, C_t = inp
                state = state * dA_t[:, :, None, None] + jnp.einsum('bh,bhp,bhn->bhpn', dt_t, x_t, B_t)
                y = jnp.einsum('bhpn,bhn->bhp', state, C_t)
                return (state, y)
            state0 = jnp.zeros((xh.shape[0], NHEADS, HEADDIM, D_STATE), xh.dtype)
            _, ys = jax.lax.scan(step, state0, (to_l(dA), to_l(dt), to_l(xh), to_l(Bh), to_l(Ch)))
            return jnp.moveaxis(ys, 0, 1)
        key = jax.random.key(seed)
        ks = jax.random.split(key, 8)
        g = lambda k, shape, s: jax.random.normal(k, shape, jnp.float32) * s
        return {'hidden_states': g(ks[0], (BATCH, SEQ, D_MODEL), 1.0), 'ln_w': jnp.ones((D_MODEL,), jnp.float32), 'ln_b': jnp.zeros((D_MODEL,), jnp.float32), 'in_proj_w': g(ks[1], (D_IN_PROJ, D_MODEL), 0.02), 'dt_bias': jax.random.uniform(ks[2], (NHEADS,), jnp.float32, -4.0, 0.0), 'A_log': jnp.log(jnp.arange(1, NHEADS + 1, dtype=jnp.float32)), 'Dp': jnp.ones((NHEADS,), jnp.float32), 'norm_w': jnp.ones((D_INNER,), jnp.float32), 'out_proj_w': g(ks[3], (D_MODEL, D_INNER), 0.02), 'fc1_w': g(ks[4], (INTER, D_MODEL), 0.02), 'fc1_b': jnp.zeros((INTER,), jnp.float32), 'fc2_w': g(ks[5], (D_MODEL, INTER), 0.02), 'fc2_b': jnp.zeros((D_MODEL,), jnp.float32)}
    _L0_attn_in = _L0_attn_setup()

    def _L0_ffn_setup():
        import jax, jax.numpy as jnp
        import numpy as np
        TOPK = 2
        N_EXPERTS = 8
        ROUTE_SCALE = 1.0
        key = jax.random.key(seed)
        ks = jax.random.split(key, 7)
        B, T, C = (4, 256, 256)
        H = 176
        HS = 352
        E = N_EXPERTS
        s = 0.02
        return {'x': jax.random.normal(ks[0], (B, T, C), jnp.float32), 'gate_w': jax.random.normal(ks[1], (E, C), jnp.float32) * s, 'gate_bias': jnp.zeros((E,), jnp.float32), 'shared_gw': jax.random.normal(ks[2], (2 * HS, C), jnp.float32) * s, 'shared_dw': jax.random.normal(ks[3], (C, HS), jnp.float32) * s, 'up_w': jax.random.normal(ks[4], (E, 2 * H, C), jnp.float32) * s, 'down_w': jax.random.normal(ks[5], (E, C, H), jnp.float32) * s}
    _L0_ffn_in = _L0_ffn_setup()

    def _L1_attn_setup():
        import jax, jax.numpy as jnp
        import numpy as np
        EMBED_DIM = 256
        NUM_HEADS = 16
        HEAD_DIM = EMBED_DIM // NUM_HEADS
        SCALE = EMBED_DIM ** (-0.5)
        key = jax.random.key(seed)
        ks = jax.random.split(key, 9)
        d = EMBED_DIM
        s = 1.0 / np.sqrt(d)
        inp = {'x': jax.random.normal(ks[0], (2, 256, d), dtype=jnp.float32), 'wq': jax.random.uniform(ks[1], (d, d), jnp.float32, -s, s), 'bq': jnp.zeros((d,), jnp.float32), 'wk': jax.random.uniform(ks[2], (d, d), jnp.float32, -s, s), 'bk': jnp.zeros((d,), jnp.float32), 'wv': jax.random.uniform(ks[3], (d, d), jnp.float32, -s, s), 'bv': jnp.zeros((d,), jnp.float32), 'wo': jax.random.uniform(ks[4], (d, d), jnp.float32, -s, s), 'bo': jnp.zeros((d,), jnp.float32)}
        return inp
    _L1_attn_in = _L1_attn_setup()

    def _L1_ffn_setup():
        import jax, jax.numpy as jnp
        import numpy as np
        B, S, D, E, I, TOP_K = (2, 512, 256, 8, 512, 2)
        key = jax.random.key(seed)
        k1, k2, k3, k4 = jax.random.split(key, 4)
        return {'hidden_states': jax.random.normal(k1, (B, S, D), dtype=jnp.float32), 'router_weight': jax.random.normal(k2, (E, D), dtype=jnp.float32) * 0.02, 'ws': jax.random.normal(k3, (E, 2 * I, D), dtype=jnp.float32) * 0.02, 'w2s': jax.random.normal(k4, (E, D, I), dtype=jnp.float32) * 0.02}
    _L1_ffn_in = _L1_ffn_setup()
    _d = {'L0_attn_hidden_states': _L0_attn_in['hidden_states'], 'L0_attn_ln_w': _L0_attn_in['ln_w'], 'L0_attn_ln_b': _L0_attn_in['ln_b'], 'L0_attn_in_proj_w': _L0_attn_in['in_proj_w'], 'L0_attn_dt_bias': _L0_attn_in['dt_bias'], 'L0_attn_A_log': _L0_attn_in['A_log'], 'L0_attn_Dp': _L0_attn_in['Dp'], 'L0_attn_norm_w': _L0_attn_in['norm_w'], 'L0_attn_out_proj_w': _L0_attn_in['out_proj_w'], 'L0_attn_fc1_w': _L0_attn_in['fc1_w'], 'L0_attn_fc1_b': _L0_attn_in['fc1_b'], 'L0_attn_fc2_w': _L0_attn_in['fc2_w'], 'L0_attn_fc2_b': _L0_attn_in['fc2_b'], 'L0_ffn_gate_w': _L0_ffn_in['gate_w'], 'L0_ffn_gate_bias': _L0_ffn_in['gate_bias'], 'L0_ffn_shared_gw': _L0_ffn_in['shared_gw'], 'L0_ffn_shared_dw': _L0_ffn_in['shared_dw'], 'L0_ffn_up_w': _L0_ffn_in['up_w'], 'L0_ffn_down_w': _L0_ffn_in['down_w'], 'L1_attn_wq': _L1_attn_in['wq'], 'L1_attn_bq': _L1_attn_in['bq'], 'L1_attn_wk': _L1_attn_in['wk'], 'L1_attn_bk': _L1_attn_in['bk'], 'L1_attn_wv': _L1_attn_in['wv'], 'L1_attn_bv': _L1_attn_in['bv'], 'L1_attn_wo': _L1_attn_in['wo'], 'L1_attn_bo': _L1_attn_in['bo'], 'L1_ffn_router_weight': _L1_ffn_in['router_weight'], 'L1_ffn_ws': _L1_ffn_in['ws'], 'L1_ffn_w2s': _L1_ffn_in['w2s']}
    _x0 = _d['L0_attn_hidden_states']
    _d['L0_attn_hidden_states'] = jax.random.normal(jax.random.fold_in(jax.random.key(seed), 1), (4, 1024, 256), dtype=_x0.dtype)
    del _x0
    return _d

def reference(L0_attn_hidden_states, L0_attn_ln_w, L0_attn_ln_b, L0_attn_in_proj_w, L0_attn_dt_bias, L0_attn_A_log, L0_attn_Dp, L0_attn_norm_w, L0_attn_out_proj_w, L0_attn_fc1_w, L0_attn_fc1_b, L0_attn_fc2_w, L0_attn_fc2_b, L0_ffn_gate_w, L0_ffn_gate_bias, L0_ffn_shared_gw, L0_ffn_shared_dw, L0_ffn_up_w, L0_ffn_down_w, L1_attn_wq, L1_attn_bq, L1_attn_wk, L1_attn_bk, L1_attn_wv, L1_attn_bv, L1_attn_wo, L1_attn_bo, L1_ffn_router_weight, L1_ffn_ws, L1_ffn_w2s):

    def _L0_attn_ref(hidden_states, ln_w, ln_b, in_proj_w, dt_bias, A_log, Dp, norm_w, out_proj_w, fc1_w, fc1_b, fc2_w, fc2_b):
        import jax, jax.numpy as jnp
        import numpy as np
        from functools import partial
        BATCH, SEQ = (2, 256)
        D_MODEL, D_INNER, D_XB = (256, 512, 128)
        HEADDIM, D_STATE = (64, 64)
        NHEADS = D_INNER // HEADDIM
        NKV = D_XB // HEADDIM
        REP = NHEADS // NKV
        INTER = 1024
        EPS = 1e-05
        D_IN_PROJ = D_INNER + D_XB + D_XB + D_INNER + NHEADS

        def _layernorm(x, w, b):
            mu = x.mean(-1, keepdims=True)
            var = ((x - mu) ** 2).mean(-1, keepdims=True)
            return (x - mu) * jax.lax.rsqrt(var + EPS) * w + b

        def _ssd_scan(xh, dt, A, Bh, Ch):
            dA = jnp.exp(dt * A)
            to_l = lambda t: jnp.moveaxis(t, 1, 0)

            def step(state, inp):
                dA_t, dt_t, x_t, B_t, C_t = inp
                state = state * dA_t[:, :, None, None] + jnp.einsum('bh,bhp,bhn->bhpn', dt_t, x_t, B_t)
                y = jnp.einsum('bhpn,bhn->bhp', state, C_t)
                return (state, y)
            state0 = jnp.zeros((xh.shape[0], NHEADS, HEADDIM, D_STATE), xh.dtype)
            _, ys = jax.lax.scan(step, state0, (to_l(dA), to_l(dt), to_l(xh), to_l(Bh), to_l(Ch)))
            return jnp.moveaxis(ys, 0, 1)
        residual = hidden_states
        h = _layernorm(hidden_states, ln_w, ln_b)
        zxbcdt = h @ in_proj_w.T
        z, x, Bm, Cm, dt = jnp.split(zxbcdt, np.cumsum([D_INNER, D_XB, D_XB, D_INNER]).tolist(), axis=-1)
        b, l = (h.shape[0], h.shape[1])
        dt = jax.nn.softplus(dt + dt_bias)
        A = -jnp.exp(A_log)
        xh = jnp.repeat(x.reshape(b, l, NKV, HEADDIM), REP, axis=2)
        Bh = jnp.repeat(Bm.reshape(b, l, NKV, D_STATE), REP, axis=2)
        Ch = Cm.reshape(b, l, NHEADS, D_STATE)
        y = _ssd_scan(xh, dt, A, Bh, Ch) + Dp[None, None, :, None] * xh
        yf = y.reshape(b, l, D_INNER)
        yf = yf * jax.nn.silu(z)
        yf = yf * jax.lax.rsqrt((yf * yf).mean(-1, keepdims=True) + EPS) * norm_w
        mamba_out = yf @ out_proj_w.T
        mlp = jax.nn.gelu(h @ fc1_w.T + fc1_b, approximate=True) @ fc2_w.T + fc2_b
        return mamba_out + mlp + residual

    def _L0_ffn_ref(x, gate_w, gate_bias, shared_gw, shared_dw, up_w, down_w):
        import jax, jax.numpy as jnp
        import numpy as np
        TOPK = 2
        N_EXPERTS = 8
        ROUTE_SCALE = 1.0
        B, T, C = x.shape
        xf = x.reshape(-1, C)
        yg = xf @ shared_gw.T
        y, g = jnp.split(yg, 2, axis=-1)
        shared = jax.nn.silu(g) * y @ shared_dw.T
        scores = jax.nn.sigmoid(xf @ gate_w.T)
        _, topk_idx = jax.lax.top_k(scores + gate_bias, TOPK)
        w = jnp.take_along_axis(scores, topk_idx, axis=-1)
        w = w / jnp.sum(w, axis=-1, keepdims=True) * ROUTE_SCALE
        out = jnp.zeros_like(xf)
        for e in range(N_EXPERTS):
            we = jnp.sum(jnp.where(topk_idx == e, w, 0.0), axis=-1)
            gu = xf @ up_w[e].T
            g_e, u_e = jnp.split(gu, 2, axis=-1)
            h = jax.nn.silu(g_e) * u_e
            out = out + h @ down_w[e].T * we[:, None]
        return (shared + out).reshape(B, T, C)

    def _L1_attn_ref(x, wq, bq, wk, bk, wv, bv, wo, bo):
        import jax, jax.numpy as jnp
        import numpy as np
        EMBED_DIM = 256
        NUM_HEADS = 16
        HEAD_DIM = EMBED_DIM // NUM_HEADS
        SCALE = EMBED_DIM ** (-0.5)
        b, t, d = x.shape
        h, hd = (NUM_HEADS, HEAD_DIM)
        q = (x @ wq + bq).reshape(b, t, h, hd).transpose(0, 2, 1, 3)
        k = (x @ wk + bk).reshape(b, t, h, hd).transpose(0, 2, 1, 3)
        v = (x @ wv + bv).reshape(b, t, h, hd).transpose(0, 2, 1, 3)
        scores = jnp.einsum('bhqd,bhkd->bhqk', q, k) * SCALE
        probs = jax.nn.softmax(scores, axis=-1)
        attn = jnp.einsum('bhqk,bhkd->bhqd', probs, v)
        attn = attn.transpose(0, 2, 1, 3).reshape(b, t, d)
        return attn @ wo + bo

    def _L1_ffn_ref(hidden_states, router_weight, ws, w2s):
        import jax, jax.numpy as jnp
        import numpy as np
        B, S, D, E, I, TOP_K = (2, 512, 256, 8, 512, 2)
        b, s, d = hidden_states.shape
        n_experts = ws.shape[0]
        inter = w2s.shape[2]
        h = hidden_states.reshape(-1, d)
        T = h.shape[0]
        logits = h @ router_weight.T
        probs = jax.nn.softmax(logits, axis=-1)
        topk_vals, topk_ids = jax.lax.top_k(probs, TOP_K)
        combine = jnp.zeros((T, n_experts), dtype=h.dtype)
        combine = combine.at[jnp.arange(T)[:, None], topk_ids].add(topk_vals)
        out = jnp.zeros_like(h)
        for e in range(n_experts):
            gu = h @ ws[e].T
            act = jax.nn.silu(gu[:, :inter]) * gu[:, inter:]
            out = out + combine[:, e:e + 1] * (act @ w2s[e].T)
        return out.reshape(b, s, d)
    x = L0_attn_hidden_states
    x = x + _layernorm(_L0_attn_ref(_layernorm(x, axis=-1), L0_attn_ln_w, L0_attn_ln_b, L0_attn_in_proj_w, L0_attn_dt_bias, L0_attn_A_log, L0_attn_Dp, L0_attn_norm_w, L0_attn_out_proj_w, L0_attn_fc1_w, L0_attn_fc1_b, L0_attn_fc2_w, L0_attn_fc2_b), axis=-1)
    x = x + _layernorm(_L0_ffn_ref(_layernorm(x, axis=-1), L0_ffn_gate_w, L0_ffn_gate_bias, L0_ffn_shared_gw, L0_ffn_shared_dw, L0_ffn_up_w, L0_ffn_down_w), axis=-1)
    x = x + _layernorm(_L1_attn_ref(_layernorm(x, axis=-1), L1_attn_wq, L1_attn_bq, L1_attn_wk, L1_attn_bk, L1_attn_wv, L1_attn_bv, L1_attn_wo, L1_attn_bo), axis=-1)
    x = x + _layernorm(_L1_ffn_ref(_layernorm(x, axis=-1), L1_ffn_router_weight, L1_ffn_ws, L1_ffn_w2s), axis=-1)
    return x

_drawn_inputs = setup_inputs


def setup_inputs(seed=0):
    import zlib

    import numpy as np

    out = dict(_drawn_inputs(seed))
    spreads = {'L0_attn_ln_w': (1.0, 0.2),
     'L0_attn_ln_b': (0.0, 0.1),
     'L0_attn_Dp': (1.0, 0.2),
     'L0_attn_norm_w': (1.0, 0.2),
     'L0_attn_fc1_b': (0.0, 0.1),
     'L0_attn_fc2_b': (0.0, 0.1),
     'L0_ffn_gate_bias': (0.0, 0.1),
     'L1_attn_bq': (0.0, 1.325),
     'L1_attn_bk': (0.0, 2.0),
     'L1_attn_bv': (0.0, 0.1),
     'L1_attn_bo': (0.0, 0.1)}
    factors = {}
    for name, (base, spread) in spreads.items():
        noise = np.random.default_rng([zlib.crc32(name.encode()), seed]).standard_normal(out[name].shape)
        drawn = base * np.exp(spread * noise) if base else spread * noise
        out[name] = jnp.asarray(drawn.astype(out[name].dtype))
    for name, factor in factors.items():
        out[name] = (out[name] * factor).astype(out[name].dtype)
    return out
```

```python
import concourse.bass as bass
from concourse import mybir
from contextlib import ExitStack

F32 = mybir.dt.float32
F32R = mybir.dt.float32r
BF16 = mybir.dt.bfloat16
I32 = mybir.dt.int32
U32 = mybir.dt.uint32
ALU = mybir.AluOpType
ACT = mybir.ActivationFunctionType
AX = mybir.AxisListType

P = 128
BATCH, SEQ, D = 4, 1024, 256
TOKENS = BATCH * SEQ
TILES = TOKENS // P
GT = 4
GROUP = GT * P
GROUPS = TILES // GT
KD = D // P
EPS = 1e-5


class Scope:

    def __init__(self, nc, ctx, stage):
        self.nc, self.ctx, self.stage = nc, ctx, stage
        self.sems = []
        ctx.callback(self.release)

    def sb(self, name, shape, dt=F32):
        return self.ctx.enter_context(self.nc.sbuf_tensor(f"{self.stage}_{name}", shape, dt))

    def pb(self, name, shape, dt=F32):
        return self.ctx.enter_context(self.nc.psum_tensor(f"{self.stage}_{name}", shape, dt))

    def sem(self, name):
        self.sems.append(self.nc.alloc_semaphore(name=f"{self.stage}_{name}"))
        return self.sems[-1]

    def release(self):
        self.nc.clear_and_free_semaphores(self.sems)
        self.nc.all_engine_barrier()


def chain_of(eng, sem, at=0):
    n = [0]

    def link(ins, wait=True):
        n[0] += 1
        ins.then_inc(sem, 1)
        if wait:
            eng.wait_ge(sem, at + n[0])
    link.n = n
    return link


D_INNER, D_XB, HEADDIM, D_STATE = 512, 128, 64, 64
HEADS = D_INNER // HEADDIM
KV = D_XB // HEADDIM
REP = HEADS // KV
INTER = 1024
CZ, CX = 0, D_INNER
CB = CX + D_XB
CDT = CB + 2 * D_XB
CC = CDT + HEADS
CEND = CC + D_INNER
XBD = CC - CX
FC1_TILES = INTER // P
Z_TILES = D_INNER // P


def mamba_stage(nc, X, x_dram, w_in, ln_w, ln_b, dt_bias, a_log, d_skip, norm_w, w_out,
                w_fc1, b_fc1, w_fc2, b_fc2, ident_d, tri_d, mask_d, sel_d, keep_d, xs_zero):
    with ExitStack() as ctx:
        s = Scope(nc, ctx, "mb")
        sb, pb, sem = s.sb, s.pb, s.sem
        WIN = sb("WIN", [P, KD, CEND])
        WF1 = sb("WF1", [P, KD, INTER])
        WF2 = sb("WF2", [P, FC1_TILES, D])
        WOUT = sb("WOUT", [P, Z_TILES, D])
        IDENT = sb("IDENT", [P, P])
        TRI = sb("TRI", [P, P])
        ONES = sb("ONES", [P, P])
        MASKF = sb("MASKF", [P, GROUP])
        MASKB = sb("MASKB", [P, GROUP], BF16)
        IDENTB = sb("IDENTB", [P, P], BF16)
        SEL = sb("SEL", [GT * HEADS, GT * HEADS, P])
        LNW = sb("LNW", [P, KD])
        LNB = sb("LNB", [P, KD])
        NORMW = sb("NORMW", [P, Z_TILES])
        BF1 = sb("BF1", [P, FC1_TILES])
        BF2 = sb("BF2", [P, D])
        DTB = sb("DTB", [P, HEADS])
        AH = sb("AH", [P, HEADS])
        NEGA = sb("NEGA", [P, HEADS])
        DSK = sb("DSK", [P, HEADS])
        KEEP = sb("KEEP", [P, GROUPS])
        MHALF = sb("MHALF", [P, GT])
        EPSC = sb("EPSC", [P, GT])
        PAUSE = sb("PAUSE", [P, 1])
        ZERO = sb("ZERO", [P, 2048])
        STAT = sb("STAT", [P, GT, 6])
        MV = [sb(f"MV{n}", [P, GT, 2]) for n in range(3)]
        VE = sb("VE", [P, GT])
        RSTD = [sb(f"RSTD{n}", [P, GT]) for n in range(3)]
        XN = sb("XN", [P, GT, D])
        XNB = sb("XNB", [P, GT, D])
        H = sb("H", [P, GT, D])
        HT = sb("HT", [P, KD, GROUP])
        BT = sb("BT", [P, KV, GROUP])
        CT = sb("CT", [P, HEADS // 2, GROUP])
        XB = sb("XB", [P, GT, XBD])
        ZS = sb("ZS", [P, GT, D_INNER])
        A1 = sb("A1", [P, FC1_TILES, GROUP])
        DTR = sb("DTR", [P, GT, HEADS])
        DTE = sb("DTE", [P, GT, HEADS])
        DTL = sb("DTL", [P, GT, HEADS])
        DT = sb("DT", [P, GT, HEADS])
        DA = sb("DA", [P, GT * HEADS])
        LT = sb("LT", [GT * HEADS, P])
        CAT = sb("CAT", [P, 3, GT * HEADS])
        EXPS = sb("EXPS", [P, 3, GT * HEADS])
        NEGL = sb("NEGL", [P, GT * HEADS])
        EDEC = sb("EDEC", [P, HEADS, P])
        W = sb("W", [P, HEADS, P])
        XDT = sb("XDT", [P, HEADS, HEADDIM])
        XEND = sb("XEND", [P, HEADS, HEADDIM])
        XSKIP = sb("XSKIP", [P, HEADS, HEADDIM])
        STATE = sb("STATE", [P, HEADS, HEADDIM])
        Y1 = sb("Y1", [P, D_INNER])
        Y2 = sb("Y2", [P, D_INNER])
        G1 = sb("G1", [P, D_INNER])
        SQ = sb("SQ", [P, D_INNER])
        SSQ = sb("SSQ", [P, GT])
        RMSV = sb("RMSV", [P, 1])
        RMS = sb("RMS", [P, GT])
        G1T = sb("G1T", [P, Z_TILES, P])
        U = sb("U", [P, GT, D])
        UN = sb("UN", [P, GT, D])

        PP = [pb(f"PP{n}", [P, GROUP]) for n in range(2)]
        PGL = pb("PGL", [P, 4 * GROUP])
        PG, PL = PGL[:, 0:2 * GROUP], PGL[:, 2 * GROUP:4 * GROUP]
        PT = pb("PT", [P, GROUP])
        PO = pb("PO", [P, GROUP])
        PST = PGL[:, 0:GROUP]
        PYI = PGL[:, GROUP:3 * GROUP].rearrange("p (q n) -> p q n", q=2)
        PY = PGL[:, 3 * GROUP:4 * GROUP]
        POUT = PO[:, 0:D]
        N32 = GT * HEADS
        PCUM = PO[:, D:D + 2 * N32]
        PLT = PO[0:N32, D + 2 * N32:D + 2 * N32 + P]

        c_load = sem("c_load")
        prep = sem("prep")
        act_prep = sem("act_prep")
        x_in = sem("x_in")
        vec = sem("vec")
        scal = sem("scal")
        gps = sem("gps")
        stats = sem("stats")
        rstd = sem("rstd")
        h_ready = sem("h_ready")
        pp_full = sem("pp_full")
        pp_read = [sem(f"pp_read{n}") for n in range(2)]
        dt_in = sem("dt_in")
        dt_log = sem("dt_log")
        da_ready = sem("da_ready")
        cum_ready = sem("cum_ready")
        lt_ready = sem("lt_ready")
        cat_ready = sem("cat_ready")
        exps_ready = sem("exps_ready")
        xnb_ready = sem("xnb_ready")
        lb_ready = sem("lb_ready")
        g_ready = sem("g_ready")
        decay_done = sem("decay_done")
        w_done = sem("w_done")
        xdt_done = sem("xdt_done")
        xend_done = sem("xend_done")
        xskip_done = sem("xskip_done")
        y_ready = sem("y_ready")
        kept = sem("kept")
        s_done = sem("s_done")
        y_used = sem("y_used")
        g1_ready = sem("g1_ready")
        ssq_done = sem("ssq_done")
        rms_done = sem("rms_done")
        g1T_full = sem("g1T_full")
        g1T_ready = sem("g1T_ready")
        out_full = sem("out_full")
        out_used = sem("out_used")
        un_ready = sem("un_ready")
        x_done = sem("x_done")
        z_fill = sem("z_fill")
        UNITS = 28

        def read(eng, i, u):
            eng.wait_ge(pp_read[u % 2], i * (UNITS // 2) + u // 2 + 1)
        LOADS = 16 * 18

        block = ctx.enter_context(nc.Block())

        @block.sync
        def _(sp):
            for dst, src in ((IDENT[:, :], ident_d), (LNW[:, :], ln_w), (LNB[:, :], ln_b),
                             (WIN[:, :, :], w_in.rearrange("(k p) n -> p k n", p=P)),
                             (DTB[:, :], dt_bias), (AH[:, :], a_log), (DSK[:, :], d_skip),
                             (TRI[:, :], tri_d), (MASKF[:, :], mask_d),
                             (SEL[:, :, :], sel_d), (KEEP[:, :], keep_d),
                             (NORMW[:, :], norm_w), (BF1[:, :], b_fc1), (BF2[:, :], b_fc2),
                             (WF1[:, :, :], w_fc1.rearrange("(k p) n -> p k n", p=P)),
                             (WF2[:, :, :], w_fc2.rearrange("(k p) n -> p k n", p=P)),
                             (WOUT[:, :, :], w_out.rearrange("(k p) n -> p k n", p=P))):
                sp.dma_start(dst, src).then_inc(c_load, 16)
            with sp.Fori(0, GROUPS) as i:
                sp.wait_ge(x_in, i * 16)
                sp.dma_start(X[:, i, :, :], x_dram[i]).then_inc(x_in, 16)
            sp.wait_ge(prep, 7)
            with sp.Fori(0, xs_zero.shape[0]) as i:
                sp.dma_start(xs_zero[i], ZERO[:, :]).then_inc(z_fill, 16)
            sp.wait_ge(z_fill, 16 * xs_zero.shape[0])
            sp.wait_ge(c_load, 16 * 17)

        @block.vector
        def _(v):
            nc.vector.memset(ONES[:, :], 1.0).then_inc(prep, 1)
            nc.vector.memset(ZERO[:, :], 0.0).then_inc(prep, 1)
            nc.vector.memset(STATE[:, :, :], 0.0).then_inc(prep, 1)
            nc.vector.memset(MHALF[:, :], -0.5).then_inc(prep, 1)
            nc.vector.memset(EPSC[:, :], EPS).then_inc(prep, 1)
            v.wait_ge(c_load, 16 * 17)
            nc.vector.tensor_copy(MASKB[:, :], MASKF[:, :]).then_inc(prep, 1)
            nc.vector.tensor_copy(IDENTB[:, :], IDENT[:, :]).then_inc(prep, 1)
            v.wait_ge(act_prep, 1)
            nc.vector.tensor_scalar(NEGA[:, :], AH[:, :], -1.0, None, ALU.mult).then_inc(prep, 1)
            for k in range(Z_TILES):
                nc.vector.tensor_scalar(WOUT[:, k, :], WOUT[:, k, :], NORMW[:, k:k + 1], None,
                                        ALU.mult).then_inc(prep, 1)
            v.wait_ge(prep, 12)
            VEC = 3 * (GT + 1) + 1 + 1 + 2 + 3 * GT
            with v.Fori(0, GROUPS) as i:
                link = chain_of(v, vec, i * VEC)
                xi = [X[:, i, c, :] for c in range(GT)]

                def layer_stats(src, n):
                    for c in range(GT):
                        nc.vector.bn_stats(STAT[:, c, :], src[c]).then_inc(vec, 1)
                    link.n[0] += GT
                    v.wait_ge(vec, i * VEC + link.n[0])
                    link(nc.vector.memset(PAUSE[:, :], 0.0), wait=False)
                    for c in range(GT):
                        nc.vector.bn_aggr(MV[n][:, c, :], STAT[:, c, :]).then_inc(stats, 1)
                    v.wait_ge(rstd, i * 3 + n + 1)

                v.wait_ge(x_in, i * 16 + 16)
                layer_stats(xi, 0)
                v.wait_ge(xnb_ready, i * 1)
                for c in range(GT):
                    ins = nc.vector.tensor_scalar(XN[:, c, :], xi[c], MV[0][:, c, 0:1],
                                                  RSTD[0][:, c:c + 1], ALU.subtract, ALU.mult)
                    if c == GT - 1:
                        link(ins)
                layer_stats([XN[:, c, :] for c in range(GT)], 1)
                for c in range(GT):
                    nc.vector.tensor_scalar(H[:, c, :], XN[:, c, :], MV[1][:, c, 0:1],
                                            RSTD[1][:, c:c + 1], ALU.subtract, ALU.mult
                                            ).then_inc(h_ready, 1)
                for u, dst in ((2, BT[:, 0, :]), (4, CT[:, 0, :]), (6, CT[:, 2, :])):
                    v.wait_ge(pp_full, i * UNITS + u + 1)
                    nc.vector.tensor_copy(dst, PP[0][:, :]).then_inc(pp_read[0], 1)
                for c in range(GT):
                    v.wait_ge(pp_full, i * UNITS + 9 + c)
                    nc.vector.tensor_copy(XB[:, c, :], PP[c % 2][:, 0:XBD]
                                          ).then_inc(pp_read[c % 2], 1)
                read(v, i, 10)
                read(v, i, 11)
                nc.vector.tensor_tensor(
                    DTR[:, :, :], XB[:, :, CDT - CX:XBD],
                    DTB[:, :].unsqueeze(1).to_broadcast([P, GT, HEADS]), ALU.add
                ).then_inc(dt_in, 1)
                v.wait_ge(dt_log, i + 1)
                link(nc.vector.scalar_tensor_tensor(out=DT[:, :, :], in0=DTR[:, :, :], scalar=0.0,
                                                    in1=DTL[:, :, :], op0=ALU.max, op1=ALU.add))
                nc.vector.tensor_tensor(
                    DA[:, :].rearrange("p (c h) -> p c h", c=GT), DT[:, :, :],
                    NEGA[:, :].unsqueeze(1).to_broadcast([P, GT, HEADS]), ALU.mult
                ).then_inc(da_ready, 1)
                v.wait_ge(cum_ready, i + 1)
                nc.vector.tensor_copy(LT[:, :], PLT).then_inc(lt_ready, 1)
                link(nc.vector.tensor_copy(CAT[:, 0:2, :], PCUM.rearrange("p (a n) -> p a n", a=2)))
                link(nc.vector.tensor_scalar(NEGL[:, :], CAT[:, 0, :], -1.0, None, ALU.mult))
                nc.vector.tensor_tensor(CAT[:, 2, :], CAT[:, 1, :], CAT[:, 0, :],
                                        ALU.subtract).then_inc(cat_ready, 1)
                nc.vector.tensor_scalar(STATE[:, :, :], STATE[:, :, :], KEEP[:, bass.ds(i, 1)],
                                        None, ALU.mult).then_inc(kept, 1)
                v.wait_ge(kept, i + 1)
                for c in range(GT):
                    cs = slice(c * HEADS, (c + 1) * HEADS)
                    wide = [P, HEADS, HEADDIM]
                    v.wait_ge(decay_done, i * GT + c + 1)
                    v.wait_ge(g_ready, i * GT + c + 1)
                    nc.vector.tensor_tensor(
                        W[:, :, :].rearrange("p (m q) t -> p m q t", q=2),
                        EDEC[:, :, :].rearrange("p (m q) t -> p m q t", q=2),
                        PG[:, :].rearrange("p (q m t) -> p m q t", q=2, t=P), ALU.mult
                    ).then_inc(w_done, 1)
                    v.wait_ge(y_ready, i * GT + c + 1)
                    v.wait_ge(exps_ready, i + 1)
                    link(nc.vector.tensor_tensor(
                        STATE[:, :, :], STATE[:, :, :],
                        EXPS[:, 1, cs].unsqueeze(2).to_broadcast(wide), ALU.mult))
                    nc.vector.tensor_tensor(
                        STATE[:, :, :], STATE[:, :, :],
                        PST.rearrange("p (h d) -> p h d", h=HEADS), ALU.add).then_inc(s_done, 1)
                    for q in range(2):
                        ins = nc.vector.tensor_tensor(
                            Y1[:, :].rearrange("p (m q d) -> p q m d", q=2, d=HEADDIM)[:, q],
                            PYI[:, q, 0:D].rearrange("p (m d) -> p m d", d=HEADDIM),
                            EXPS[:, 0, cs].rearrange("p (m q) -> p q m", q=2)[:, q].unsqueeze(2)
                            .to_broadcast([P, HEADS // 2, HEADDIM]), ALU.mult)
                    link(ins)
                    nc.vector.tensor_tensor(Y2[:, :], PY, Y1[:, :], ALU.add).then_inc(y_used, 1)
                    v.wait_ge(y_used, i * GT + c + 1)
                    v.wait_ge(xskip_done, i * GT + c + 1)
                    link(nc.vector.tensor_tensor(
                        Y1[:, :], Y2[:, :], XSKIP[:, :, :].rearrange("p h d -> p (h d)"), ALU.add))
                    read(v, i, 12 + c)
                    v.wait_ge(ssq_done, i * GT + c)
                    v.wait_ge(g1T_full, i * GT + c)
                    nc.vector.tensor_tensor(G1[:, :], Y1[:, :], ZS[:, c, :],
                                            ALU.mult).then_inc(g1_ready, 1)
                    if c == 0:
                        v.wait_ge(xnb_ready, i + 1)
                    v.wait_ge(pp_full, i * UNITS + 25 + c)
                    nc.vector.tensor_tensor(U[:, c, :], PP[c % 2][:, 0:D], XNB[:, c, :],
                                            ALU.add).then_inc(pp_read[c % 2], 1)
                    read(v, i, 24 + c)
                    v.wait_ge(rms_done, i * GT + c + 1)
                    v.wait_ge(out_full, i * GT + c + 1)
                    nc.vector.scalar_tensor_tensor(
                        out=U[:, c, :], in0=POUT, scalar=RMS[:, c:c + 1], in1=U[:, c, :],
                        op0=ALU.mult, op1=ALU.add).then_inc(out_used, 1)
                v.wait_ge(out_used, i * GT + GT)
                layer_stats([U[:, c, :] for c in range(GT)], 2)
                v.wait_ge(x_done, i * GT)
                for c in range(GT):
                    nc.vector.tensor_scalar(UN[:, c, :], U[:, c, :], MV[2][:, c, 0:1],
                                            RSTD[2][:, c:c + 1], ALU.subtract, ALU.mult
                                            ).then_inc(un_ready, 1)
                assert link.n[0] == VEC, link.n[0]
            v.wait_ge(un_ready, GROUPS * GT)

        @block.gpsimd
        def _(g):
            g.wait_ge(prep, 12)
            with g.Fori(0, GROUPS) as i:
                link = chain_of(g, gps, i * (3 + GT))

                def inverse_std(n):
                    g.wait_ge(stats, i * 3 * GT + GT * (n + 1))
                    link(nc.gpsimd.tensor_tensor(VE[:, :], MV[n][:, :, 1], EPSC[:, :], ALU.add))
                    nc.gpsimd.tensor_tensor(RSTD[n][:, :], VE[:, :], MHALF[:, :],
                                            ALU.pow).then_inc(rstd, 1)
                    g.wait_ge(rstd, i * 3 + n + 1)

                inverse_std(0)
                inverse_std(1)
                g.wait_ge(h_ready, i * GT + GT)
                nc.gpsimd.tensor_tensor(XNB[:, :, :], XN[:, :, :],
                                        BF2[:, :].unsqueeze(1).to_broadcast([P, GT, D]),
                                        ALU.add).then_inc(xnb_ready, 1)
                g.wait_ge(da_ready, i + 1)
                g.wait_ge(cat_ready, i + 1)
                for c in range(GT):
                    cs = slice(c * HEADS, (c + 1) * HEADS)

                    def by_head(t):
                        return t.rearrange("p (k r) d -> p k r d", k=KV)
                    xt = XB[:, c, 0:D_XB].rearrange("p (k d) -> p k d", k=KV).unsqueeze(2) \
                        .to_broadcast([P, KV, REP, HEADDIM])

                    def weight(w):
                        return w.unsqueeze(2).to_broadcast([P, HEADS, HEADDIM])
                    g.wait_ge(y_ready, i * GT + c)
                    g.wait_ge(y_used, i * GT + c)
                    for r in range(KV):
                        ins = nc.gpsimd.tensor_tensor(
                            XDT[:, r * REP:(r + 1) * REP, :],
                            XB[:, c, r * HEADDIM:(r + 1) * HEADDIM].unsqueeze(1)
                            .to_broadcast([P, REP, HEADDIM]),
                            DT[:, c, r * REP:(r + 1) * REP].unsqueeze(2)
                            .to_broadcast([P, REP, HEADDIM]), ALU.mult)
                    ins.then_inc(xdt_done, 1)
                    g.wait_ge(xdt_done, i * GT + c + 1)
                    g.wait_ge(exps_ready, i + 1)
                    nc.gpsimd.tensor_tensor(XEND[:, :, :], XDT[:, :, :],
                                            weight(EXPS[:, 2, cs]), ALU.mult).then_inc(xend_done, 1)
                    g.wait_ge(g1_ready, i * GT + c)
                    for r in range(KV):
                        ins = nc.gpsimd.tensor_tensor(
                            XSKIP[:, r * REP:(r + 1) * REP, :],
                            XB[:, c, r * HEADDIM:(r + 1) * HEADDIM].unsqueeze(1)
                            .to_broadcast([P, REP, HEADDIM]),
                            DSK[:, r * REP:(r + 1) * REP].unsqueeze(2)
                            .to_broadcast([P, REP, HEADDIM]), ALU.mult)
                    ins.then_inc(xskip_done, 1)
                    g.wait_ge(ssq_done, i * GT + c + 1)
                    link(nc.gpsimd.tensor_tensor(RMSV[:, :], SSQ[:, c:c + 1], EPSC[:, 0:1],
                                                 ALU.add))
                    nc.gpsimd.tensor_tensor(RMS[:, c:c + 1], RMSV[:, :], MHALF[:, 0:1],
                                            ALU.pow).then_inc(rms_done, 1)
                    g.wait_ge(rms_done, i * GT + c + 1)
                inverse_std(2)
                for c in range(GT):
                    g.wait_ge(un_ready, i * GT + c + 1)
                    nc.gpsimd.tensor_tensor(X[:, i, c, :], X[:, i, c, :], UN[:, c, :],
                                            ALU.add).then_inc(x_done, 1)
            g.wait_ge(x_done, GROUPS * GT)

        @block.scalar
        def _(a):
            a.wait_ge(c_load, 16 * 17)
            nc.scalar.activation(AH[:, :], AH[:, :], ACT.Exp).then_inc(act_prep, 1)
            a.wait_ge(act_prep, 1)
            with a.Fori(0, GROUPS) as i:
                link = chain_of(a, scal, i * (1 + 1))
                for k in range(KD):
                    a.wait_ge(pp_full, i * UNITS + k + 1)
                    nc.scalar.activation(HT[:, k, :], PP[k][:, :], ACT.Identity,
                                         bias=LNB[:, k:k + 1], scale=LNW[:, k:k + 1]
                                         ).then_inc(pp_read[k], 1)
                for u, dst in ((3, BT[:, 1, :]), (5, CT[:, 1, :]), (7, CT[:, 3, :])):
                    a.wait_ge(pp_full, i * UNITS + u + 1)
                    nc.scalar.activation(dst, PP[1][:, :], ACT.Copy).then_inc(pp_read[1], 1)
                a.wait_ge(dt_in, i + 1)
                link(nc.scalar.activation(DTE[:, :, :], DTR[:, :, :], ACT.Abs))
                link(nc.scalar.activation(DTE[:, :, :], DTE[:, :, :], ACT.Exp, scale=-1.0))
                nc.scalar.activation(DTL[:, :, :], DTE[:, :, :], ACT.Ln, bias=1.0
                                     ).then_inc(dt_log, 1)
                for c in range(GT):
                    a.wait_ge(pp_full, i * UNITS + 13 + c)
                    nc.scalar.activation(ZS[:, c, :], PP[c % 2][:, :], ACT.Silu
                                         ).then_inc(pp_read[c % 2], 1)
                for m in range(FC1_TILES):
                    a.wait_ge(pp_full, i * UNITS + 17 + m)
                    nc.scalar.activation(A1[:, m, :], PP[m % 2][:, :], ACT.Gelu_apprx_tanh,
                                         bias=BF1[:, m:m + 1]).then_inc(pp_read[m % 2], 1)
                a.wait_ge(cat_ready, i + 1)
                nc.scalar.activation(EXPS[:, :, :], CAT[:, :, :], ACT.Exp).then_inc(exps_ready, 1)

                def square_and_turn(c):
                    a.wait_ge(g1_ready, i * GT + c + 1)
                    a.wait_ge(rms_done, i * GT + c)
                    a.wait_ge(ssq_done, i * GT + c)
                    nc.scalar.activation(SQ[:, :], G1[:, :], ACT.Square,
                                         scale=D_INNER ** -0.5,
                                         accum_out=SSQ[:, c:c + 1]).then_inc(ssq_done, 1)
                    a.wait_ge(g1T_full, i * GT + c + 1)
                    nc.scalar.activation(G1T[:, :, :].rearrange("p m t -> p (m t)"), PT[:, :],
                                         ACT.Copy).then_inc(g1T_ready, 1)

                for c in range(GT):
                    a.wait_ge(lb_ready, i * GT + c + 1)
                    a.wait_ge(w_done, i * GT + c)
                    for h in range(HEADS):
                        n = c * HEADS + h
                        ins = nc.scalar.activation(EDEC[:, h, :], PL[:, h * P:(h + 1) * P], ACT.Exp,
                                                   bias=NEGL[:, n:n + 1])
                    ins.then_inc(decay_done, 1)
                    if c:
                        square_and_turn(c - 1)
                square_and_turn(GT - 1)
            a.wait_ge(g1T_ready, GROUPS * GT)

        @block.tensor
        def _(pe):
            pe.wait_ge(prep, 12)
            with pe.Fori(0, GROUPS) as i:
                def unit(u):
                    pe.wait_ge(pp_read[u % 2], i * (UNITS // 2) + u // 2)
                    return PP[u % 2]

                def wide(u, lhsT_of, rhs_of, ks, cols):
                    out = unit(u)
                    for k in range(ks):
                        ins = nc.tensor.matmul(out[:, 0:cols], lhsT_of(k), rhs_of(k),
                                               start=(k == 0), stop=(k == ks - 1))
                    ins.then_inc(pp_full, 1)

                for k in range(KD):
                    out = unit(k)
                    for c in range(GT):
                        pe.wait_ge(h_ready, i * GT + c + 1)
                        ins = nc.tensor.transpose(out[:, c * P:(c + 1) * P],
                                                  H[:, c, k * P:(k + 1) * P], IDENT[:, :])
                    ins.then_inc(pp_full, 1)
                read(pe, i, 0)
                read(pe, i, 1)
                for u, col in enumerate([CB, CB + P] + [CC + m * P for m in range(Z_TILES)]):
                    wide(2 + u, lambda k: WIN[:, k, col:col + P], lambda k: HT[:, k, :], KD, GROUP)
                for c in range(GT):
                    wide(8 + c, lambda k: HT[:, k, c * P:(c + 1) * P],
                         lambda k: WIN[:, k, CX:CC], KD, XBD)
                for c in range(GT):
                    wide(12 + c, lambda k: HT[:, k, c * P:(c + 1) * P],
                         lambda k: WIN[:, k, CZ:CZ + D_INNER], KD, D_INNER)
                pe.wait_ge(da_ready, i + 1)
                pe.wait_ge(out_used, i * GT)
                nc.tensor.matmul(PCUM[:, 0:N32], TRI[:, :], DA[:, :], start=True, stop=True)
                nc.tensor.matmul(PCUM[:, N32:2 * N32], ONES[:, :], DA[:, :], start=True, stop=True)
                nc.tensor.matmul(PLT, DA[:, :], TRI[:, :], start=True, stop=True
                                 ).then_inc(cum_ready, 1)
                for m in range(FC1_TILES):
                    wide(16 + m, lambda k: WF1[:, k, m * P:(m + 1) * P], lambda k: HT[:, k, :],
                         KD, GROUP)
                pe.wait_ge(lt_ready, i + 1)

                def out_projection(c):
                    pe.wait_ge(g1_ready, i * GT + c + 1)
                    pe.wait_ge(g1T_ready, i * GT + c)
                    for m in range(Z_TILES):
                        ins = nc.tensor.transpose(PT[:, m * P:(m + 1) * P],
                                                  G1[:, m * P:(m + 1) * P], IDENT[:, :])
                    ins.then_inc(g1T_full, 1)
                    pe.wait_ge(g1T_ready, i * GT + c + 1)
                    pe.wait_ge(cat_ready, i + 1)
                    pe.wait_ge(out_used, i * GT + c)
                    for m in range(Z_TILES):
                        ins = nc.tensor.matmul(POUT, G1T[:, m, :], WOUT[:, m, :], start=(m == 0),
                                               stop=(m == Z_TILES - 1))
                    ins.then_inc(out_full, 1)

                for c in range(GT):
                    t = slice(c * P, (c + 1) * P)
                    pe.wait_ge(y_used, i * GT + c)
                    for half in range(2):
                        bank = PL[:, half * GROUP:(half + 1) * GROUP]
                        for n in range(GT):
                            h = half * GT + n
                            nc.tensor.matmul(bank[:, n * P:(n + 1) * P],
                                             SEL[:, c * HEADS + h, :], LT[:, :],
                                             start=(n == 0), stop=False, skip_group_check=True)
                        ins = nc.tensor.matmul(bank, IDENTB[:, :], MASKB[:, :], start=False,
                                               stop=True, skip_group_check=True)
                    ins.then_inc(lb_ready, 1)
                    pe.wait_ge(w_done, i * GT + c)
                    pe.wait_ge(s_done, i * GT + c)
                    for q in range(2):
                        row = slice(64 * q, 64 * q + 64)
                        for k in range(KV):
                            at = q * GROUP + k * 2 * P
                            ins = nc.tensor.matmul(PG[:, at:at + 2 * P], BT[row, k, t],
                                                   CT[row, 2 * k:2 * k + 2, t], start=True,
                                                   stop=True)
                    ins.then_inc(g_ready, 1)
                    if c == 0:
                        read(pe, i, 22)
                        read(pe, i, 23)
                    wide(24 + c, lambda m: A1[:, m, t], lambda m: WF2[:, m, :], FC1_TILES, D)
                    if c:
                        out_projection(c - 1)
                    pe.wait_ge(w_done, i * GT + c + 1)
                    pe.wait_ge(xdt_done, i * GT + c + 1)
                    pe.wait_ge(decay_done, i * GT + c + 1)
                    for k in range(KV):
                        pe.wait_ge(xend_done, i * GT + c + 1)
                        ins = nc.tensor.matmul(
                            PST[:, k * 2 * P:(k + 1) * 2 * P],
                            XB[:, c, D_XB + k * P:D_XB + (k + 1) * P],
                            XEND[:, k * REP:(k + 1) * REP, :].rearrange("p h d -> p (h d)"),
                            start=True, stop=True)
                    for h in range(HEADS):
                        nc.tensor.matmul(PY[:, h * HEADDIM:(h + 1) * HEADDIM], W[:, h, :],
                                         XDT[:, h, :], start=True, stop=True)
                    if c == 0:
                        pe.wait_ge(kept, i + 1)
                    for h in range(HEADS):
                        row = slice(64 * (h % 2), 64 * (h % 2) + 64)
                        at = (h // 2) * HEADDIM
                        ins = nc.tensor.matmul(PYI[:, h % 2, at:at + HEADDIM],
                                               CT[row, h // 2, t], STATE[row, h, :], start=True,
                                               stop=True)
                    ins.then_inc(y_ready, 1)
                out_projection(GT - 1)

EXPERTS, TOPK = 8, 2
ETILES = TOKENS * TOPK // P + EXPERTS
XS_TILES = ETILES + 8
BIG = 3.0e38


def route_stage(nc, X, XN, LOG, SHARED, w_router, ident_d, w_sgate, w_sdown, hs):
    with ExitStack() as ctx:
        s = Scope(nc, ctx, f"rt{hs}")
        sb, pb, sem = s.sb, s.pb, s.sem
        IDENT = sb("IDENT", [P, P])
        WR = sb("WR", [P, KD, EXPERTS])
        MHALF = sb("MHALF", [P, GT])
        STAT = sb("STAT", [P, GT, 6])
        MV = sb("MV", [P, GT, 2])
        VE = sb("VE", [P, GT])
        RSTD = sb("RSTD", [P, GT])
        EPSC = sb("EPSC", [P, GT])
        PAUSE = sb("PAUSE", [P, 1])
        H = sb("H", [P, GT, D])
        HT = sb("HT", [P, KD, GROUP])
        PP = [pb(f"PP{n}", [P, GROUP]) for n in range(2)]
        PR = pb("PR", [P, GT, EXPERTS])
        HSC = [min(P, hs - P * m) for m in range(-(-hs // P))]
        NS = len(HSC)
        if hs:
            WSG = sb("WSG", [P, KD, 2 * hs])
            WSD = sb("WSD", [P, NS, D])
            SG = [sb(f"SG{n}", [P, GROUP]) for n in range(2)]
            HS = sb("HS", [P, NS, GROUP])
            PY = [pb(f"PY{n}", [P, GROUP]) for n in range(2)]
            PGT = [pb(f"PGT{n}", [P, GROUP]) for n in range(2)]
        c_load = sem("c_load")
        prep = sem("prep")
        vec = sem("vec")
        gps = sem("gps")
        stats = sem("stats")
        rstd = sem("rstd")
        h_ready = sem("h_ready")
        pp_full = sem("pp_full")
        pp_read = [sem(f"pp_read{n}") for n in range(2)]
        r_full = sem("r_full")
        r_read = sem("r_read")
        xn_kept = sem("xn_kept")
        hid_full = sem("hid_full")
        sg_ready = sem("sg_ready")
        hs_ready = sem("hs_ready")
        UNITS = 6 if hs else 2
        LOADS = 16 * (2 + (1 + NS if hs else 0))
        block = ctx.enter_context(nc.Block())

        def read(eng, i, u):
            eng.wait_ge(pp_read[u % 2], i * (UNITS // 2) + u // 2 + 1)

        @block.sync
        def _(sp):
            sp.dma_start(IDENT[:, :], ident_d).then_inc(c_load, 16)
            sp.dma_start(WR[:, :, :], w_router.rearrange("(k p) n -> p k n", p=P)
                         ).then_inc(c_load, 16)
            if hs:
                sp.dma_start(WSG[:, :, :], w_sgate.rearrange("(k p) n -> p k n", p=P)
                             ).then_inc(c_load, 16)
                for m, rows in enumerate(HSC):
                    sp.dma_start(WSD[0:rows, m, :], w_sdown[m * P:m * P + rows, :]
                                 ).then_inc(c_load, 16)
            sp.wait_ge(c_load, LOADS)

        @block.vector
        def _(v):
            nc.vector.memset(MHALF[:, :], -0.5).then_inc(prep, 1)
            nc.vector.memset(EPSC[:, :], EPS).then_inc(prep, 1)
            VEC = GT + 1
            with v.Fori(0, GROUPS) as i:
                link = chain_of(v, vec, i * VEC)
                for c in range(GT):
                    link(nc.vector.bn_stats(STAT[:, c, :], X[:, i, c, :]), wait=False)
                v.wait_ge(vec, i * VEC + GT)
                link(nc.vector.memset(PAUSE[:, :], 0.0), wait=False)
                for c in range(GT):
                    nc.vector.bn_aggr(MV[:, c, :], STAT[:, c, :]).then_inc(stats, 1)
                v.wait_ge(rstd, i + 1)
                v.wait_ge(xn_kept, i)
                for c in range(GT):
                    nc.vector.tensor_scalar(H[:, c, :], X[:, i, c, :], MV[:, c, 0:1],
                                            RSTD[:, c:c + 1], ALU.subtract, ALU.mult
                                            ).then_inc(h_ready, 1)
                v.wait_ge(pp_full, i * UNITS + 1)
                nc.vector.tensor_copy(HT[:, 0, :], PP[0][:, :]).then_inc(pp_read[0], 1)
                v.wait_ge(r_full, i + 1)
                nc.vector.tensor_copy(LOG[:, i, :, :], PR[:, :, :]).then_inc(r_read, 1)
                for m in range(NS):
                    v.wait_ge(sg_ready, i * NS + m + 1)
                    nc.vector.tensor_tensor(HS[0:HSC[m], m, :], SG[m % 2][0:HSC[m], :],
                                            PY[m % 2][0:HSC[m], :], ALU.mult
                                            ).then_inc(hs_ready, 1)
                if hs:
                    for c in range(0, GT, 2):
                        v.wait_ge(pp_full, i * UNITS + 3 + c)
                        nc.vector.tensor_copy(SHARED[:, i, c, :], PP[0][:, 0:D]
                                              ).then_inc(pp_read[0], 1)
            v.wait_ge(r_read, GROUPS)
            read(v, GROUPS - 1, UNITS - 2)

        @block.gpsimd
        def _(g):
            g.wait_ge(prep, 2)
            with g.Fori(0, GROUPS) as i:
                g.wait_ge(stats, i * GT + GT)
                nc.gpsimd.tensor_tensor(VE[:, :], MV[:, :, 1], EPSC[:, :], ALU.add
                                        ).then_inc(gps, 1)
                g.wait_ge(gps, i + 1)
                nc.gpsimd.tensor_tensor(RSTD[:, :], VE[:, :], MHALF[:, :], ALU.pow
                                        ).then_inc(rstd, 1)
                g.wait_ge(h_ready, i * GT + GT)
                nc.gpsimd.tensor_copy(XN[:, i, :, :], H[:, :, :]).then_inc(xn_kept, 1)
            g.wait_ge(xn_kept, GROUPS)

        @block.scalar
        def _(a):
            with a.Fori(0, GROUPS) as i:
                a.wait_ge(pp_full, i * UNITS + 2)
                nc.scalar.activation(HT[:, 1, :], PP[1][:, :], ACT.Copy).then_inc(pp_read[1], 1)
                for m in range(NS):
                    a.wait_ge(hid_full, i * NS + m + 1)
                    if m >= 2:
                        a.wait_ge(hs_ready, i * NS + m - 1)
                    else:
                        a.wait_ge(hs_ready, i * NS)
                    nc.scalar.activation(SG[m % 2][0:HSC[m], :], PGT[m % 2][0:HSC[m], :], ACT.Silu
                                         ).then_inc(sg_ready, 1)
                if hs:
                    for c in range(1, GT, 2):
                        a.wait_ge(pp_full, i * UNITS + 3 + c)
                        nc.scalar.activation(SHARED[:, i, c, :], PP[1][:, 0:D], ACT.Copy
                                             ).then_inc(pp_read[1], 1)
            read(a, GROUPS - 1, UNITS - 1)

        @block.tensor
        def _(pe):
            pe.wait_ge(c_load, LOADS)
            with pe.Fori(0, GROUPS) as i:
                for k in range(KD):
                    pe.wait_ge(pp_read[k], i * (UNITS // 2))
                    for c in range(GT):
                        pe.wait_ge(h_ready, i * GT + c + 1)
                        ins = nc.tensor.transpose(PP[k][:, c * P:(c + 1) * P],
                                                  H[:, c, k * P:(k + 1) * P], IDENT[:, :])
                    ins.then_inc(pp_full, 1)
                read(pe, i, 0)
                read(pe, i, 1)
                pe.wait_ge(r_read, i)
                for c in range(GT):
                    for k in range(KD):
                        ins = nc.tensor.matmul(PR[:, c, :], HT[:, k, c * P:(c + 1) * P],
                                               WR[:, k, :], start=(k == 0), stop=(k == KD - 1))
                ins.then_inc(r_full, 1)
                for m in range(NS):
                    if m >= 2:
                        pe.wait_ge(hs_ready, i * NS + m - 1)
                    else:
                        pe.wait_ge(hs_ready, i * NS)
                    for bank, off in ((PY, 0), (PGT, hs)):
                        for k in range(KD):
                            at = off + m * P
                            ins = nc.tensor.matmul(bank[m % 2][0:HSC[m], :],
                                                   WSG[:, k, at:at + HSC[m]], HT[:, k, :],
                                                   start=(k == 0), stop=(k == KD - 1))
                    ins.then_inc(hid_full, 1)
                if hs:
                    pe.wait_ge(hs_ready, i * NS + NS)
                    for c in range(GT):
                        pe.wait_ge(pp_read[c % 2], i * (UNITS // 2) + 1 + c // 2)
                        for m in range(NS):
                            ins = nc.tensor.matmul(PP[c % 2][:, 0:D],
                                                   HS[0:HSC[m], m, c * P:(c + 1) * P],
                                                   WSD[0:HSC[m], m, :], start=(m == 0),
                                                   stop=(m == NS - 1))
                        ins.then_inc(pp_full, 1)


def dispatch_stage(nc, XN, LOG, POS, WT, EXP_OF, gate_bias, tri_d, rev_d, tile_d, step_d, xs, hs):
    sigmoid = hs > 0
    with ExitStack() as ctx:
        s = Scope(nc, ctx, f"dp{hs}")
        sb, pb, sem = s.sb, s.pb, s.sem
        TRI = sb("TRI", [P, P])
        ONES = sb("ONES", [P, P])
        REV = sb("REV", [P, EXPERTS])
        TIDX = sb("TIDX", [P, ETILES])
        STEP = sb("STEP", [P, TILES])
        GB = sb("GB", [P, EXPERTS])
        te = [P, TILES, EXPERTS]
        SC, SEL, EQ, T, POSF = (sb(n, te) for n in ("SC", "SEL", "EQ", "T", "POSF"))
        O = [sb(f"O{n}", te) for n in range(TOPK)]
        RUN = [sb(f"RUN{n}", te) for n in range(2)]
        M = sb("M", [P, TILES])
        R = sb("R", [P, TILES])
        PF = sb("PF", [P, TILES])
        WSUM = sb("WSUM", [P, TILES])
        CMP = sb("CMP", [P, EXPERTS, TILES])
        TE = sb("TE", [P, EXPERTS])
        CE = [sb(f"CE{n}", [P, EXPERTS]) for n in range(2)]
        BASE = sb("BASE", [P, EXPERTS])
        CMT = sb("CMT", [P, ETILES, EXPERTS - 1])
        EXF = sb("EXF", [P, ETILES])
        PC = pb("PC", [P, 2, TILES * EXPERTS])
        c_load = sem("c_load")
        vec = sem("vec")
        scores_in = sem("scores_in")
        scored = sem("scored")
        picked = sem("picked")
        counted = sem("counted")
        placed = sem("placed")
        scattered = sem("scattered")
        block = ctx.enter_context(nc.Block())
        flat = LOG[:, :, :, :].rearrange("p g c e -> p (g c) e")
        V = nc.vector

        def over_e(t):
            return t.unsqueeze(2).to_broadcast(te)

        def over_t(t):
            return t.unsqueeze(1).to_broadcast(te)

        @block.sync
        def _(sp):
            for dst, src in ((TRI, tri_d), (REV, rev_d), (TIDX, tile_d), (STEP, step_d),
                             (GB, gate_bias)):
                sp.dma_start(dst[:, :], src).then_inc(c_load, 16)
            sp.wait_ge(c_load, 80)

        @block.scalar
        def _(a):
            if sigmoid:
                nc.scalar.activation(SC[:, :, :], flat, ACT.Sigmoid).then_inc(scored, 1)
            else:
                a.wait_ge(scores_in, 1)
                nc.scalar.activation(SC[:, :, :], T[:, :, :], ACT.Exp).then_inc(scored, 1)

        @block.vector
        def _(v):
            link = chain_of(v, vec)
            link(V.memset(ONES[:, :], 1.0))
            v.wait_ge(c_load, 80)
            if sigmoid:
                v.wait_ge(scored, 1)
                link(V.tensor_tensor(SEL[:, :, :], SC[:, :, :], over_t(GB[:, :]), ALU.add))
            else:
                link(V.tensor_reduce(M[:, :], flat, AX.X, ALU.max))
                V.tensor_tensor(T[:, :, :], flat, over_e(M[:, :]), ALU.subtract
                                ).then_inc(scores_in, 1)
                v.wait_ge(scored, 1)
                link(V.tensor_reduce(M[:, :], SC[:, :, :], AX.X, ALU.add))
                link(V.reciprocal(R[:, :], M[:, :]))
                link(V.tensor_tensor(SC[:, :, :], SC[:, :, :], over_e(R[:, :]), ALU.mult))
                link(V.tensor_copy(SEL[:, :, :], SC[:, :, :]))
            for n in range(TOPK):
                link(V.tensor_reduce(M[:, :], SEL[:, :, :], AX.X, ALU.max))
                link(V.tensor_tensor(EQ[:, :, :], SEL[:, :, :], over_e(M[:, :]), ALU.is_equal))
                link(V.tensor_tensor(T[:, :, :], EQ[:, :, :], over_t(REV[:, :]), ALU.mult))
                link(V.tensor_reduce(R[:, :], T[:, :, :], AX.X, ALU.max))
                link(V.tensor_tensor(O[n][:, :, :], over_t(REV[:, :]), over_e(R[:, :]),
                                     ALU.is_equal))
                link(V.tensor_tensor(T[:, :, :], O[n][:, :, :], SC[:, :, :], ALU.mult))
                link(V.tensor_reduce(WT[:, n, :], T[:, :, :], AX.X, ALU.add))
                if n < TOPK - 1:
                    link(V.scalar_tensor_tensor(out=SEL[:, :, :], in0=O[n][:, :, :], scalar=-BIG,
                                                in1=SEL[:, :, :], op0=ALU.mult, op1=ALU.add))
            if sigmoid:
                link(V.tensor_tensor(WSUM[:, :], WT[:, 0, :], WT[:, 1, :], ALU.add))
                link(V.reciprocal(R[:, :], WSUM[:, :]))
                for n in range(TOPK):
                    link(V.tensor_tensor(WT[:, n, :], WT[:, n, :], R[:, :], ALU.mult))
            V.tensor_tensor(EQ[:, :, :], O[0][:, :, :], O[1][:, :, :], ALU.add
                            ).then_inc(picked, 1)
            v.wait_ge(counted, 1)
            total = PC[:, 1, :].rearrange("p (t e) -> p t e", e=EXPERTS)
            link(V.tensor_copy(RUN[0][:, :, :], total))
            src, d = 0, 1
            while d < TILES:
                link(V.tensor_copy(RUN[1 - src][:, 0:d, :], RUN[src][:, 0:d, :]))
                link(V.tensor_tensor(RUN[1 - src][:, d:, :], RUN[src][:, d:, :],
                                     RUN[src][:, 0:TILES - d, :], ALU.add))
                src, d = 1 - src, 2 * d
            run, other = RUN[src], RUN[1 - src]
            link(V.tensor_tensor(CMP[:, :, :],
                                 run[:, TILES - 1, :].unsqueeze(2)
                                 .to_broadcast([P, EXPERTS, TILES]),
                                 STEP[:, :].unsqueeze(1).to_broadcast([P, EXPERTS, TILES]),
                                 ALU.is_gt))
            link(V.tensor_reduce(TE[:, :], CMP[:, :, :], AX.X, ALU.add))
            link(V.tensor_copy(CE[0][:, :], TE[:, :]))
            ce, d = 0, 1
            while d < EXPERTS:
                link(V.tensor_copy(CE[1 - ce][:, 0:d], CE[ce][:, 0:d]))
                link(V.tensor_tensor(CE[1 - ce][:, d:], CE[ce][:, d:],
                                     CE[ce][:, 0:EXPERTS - d], ALU.add))
                ce, d = 1 - ce, 2 * d
            link(V.tensor_tensor(BASE[:, :], CE[ce][:, :], TE[:, :], ALU.subtract))
            link(V.tensor_scalar(BASE[:, :], BASE[:, :], float(P), -1.0, ALU.mult, ALU.add))
            link(V.tensor_tensor(other[:, :, :], run[:, :, :], total, ALU.subtract))
            link(V.tensor_tensor(POSF[:, :, :], other[:, :, :],
                                 PC[:, 0, :].rearrange("p (t e) -> p t e", e=EXPERTS), ALU.add))
            link(V.tensor_tensor(POSF[:, :, :], POSF[:, :, :], over_t(BASE[:, :]), ALU.add))
            for n in range(TOPK):
                link(V.tensor_tensor(T[:, :, :], POSF[:, :, :], O[n][:, :, :], ALU.mult))
                link(V.tensor_reduce(PF[:, :], T[:, :, :], AX.X, ALU.add))
                V.tensor_copy(POS[:, n, :], PF[:, :]).then_inc(placed, 1)
            shape = [P, ETILES, EXPERTS - 1]
            link(V.tensor_tensor(CMT[:, :, :], TIDX[:, :].unsqueeze(2).to_broadcast(shape),
                                 CE[ce][:, 0:EXPERTS - 1].unsqueeze(1).to_broadcast(shape),
                                 ALU.is_ge))
            link(V.tensor_reduce(EXF[:, :], CMT[:, :, :], AX.X, ALU.add))
            link(V.memset(EXP_OF[:, :], 0))
            link(V.tensor_copy(EXP_OF[:, 0:ETILES], EXF[:, :]))

        @block.tensor
        def _(pe):
            pe.wait_ge(picked, 1)
            picks = EQ[:, :, :].rearrange("p t e -> p (t e)")
            nc.tensor.matmul(PC[:, 0, :], TRI[:, :], picks, start=True, stop=True)
            nc.tensor.matmul(PC[:, 1, :], ONES[:, :], picks, start=True, stop=True
                             ).then_inc(counted, 1)

        @block.gpsimd
        def _(g):
            for n in range(TOPK):
                g.wait_ge(placed, n + 1)
                for t in range(TILES):
                    g.indirect_dma_start(
                        out=xs, out_offset=bass.IndirectOffsetOnAxis(ap=POS[:, n, t:t + 1], axis=0),
                        in_=XN[:, t // GT, t % GT, :], in_offset=None).then_inc(scattered, 16)
            g.wait_ge(scattered, 16 * TOPK * TILES)


def expert_stage(nc, EXP_OF, xs, ys, w_up, w_down, ident_d, hid):
    with ExitStack() as ctx:
        s = Scope(nc, ctx, f"ex{hid}")
        sb, pb, sem = s.sb, s.pb, s.sem
        HC = hid // P if hid % P == 0 else 2
        HP = hid // HC
        IDENT = sb("IDENT", [P, P])
        WU = sb("WU", [P, EXPERTS, KD, 2 * hid])
        WD = sb("WD", [P, EXPERTS, HC, D])
        XG = [sb(f"XG{n}", [P, D]) for n in range(2)]
        XT = [sb(f"XT{n}", [P, KD, P]) for n in range(2)]
        SG = [sb(f"SG{n}", [P, hid]) for n in range(2)]
        HH = [sb(f"HH{n}", [P, hid]) for n in range(2)]
        HT = [sb(f"HT{n}", [P, HC, P]) for n in range(2)]
        YO = [sb(f"YO{n}", [P, D]) for n in range(2)]
        PX = pb("PX", [P, GROUP])
        PGA = [pb(f"PGA{n}", [P, GROUP]) for n in range(2)]
        PUP = [pb(f"PUP{n}", [P, GROUP]) for n in range(2)]
        PH = pb("PH", [P, GROUP])
        PY = [pb(f"PY{n}", [P, GROUP]) for n in range(2)]
        c_load = sem("c_load")
        w_load = sem("w_load")
        x_load = [sem(f"x_load{n}") for n in range(2)]
        xt_full = sem("xt_full")
        xt_read = sem("xt_read")
        gate_full = sem("gate_full")
        up_full = sem("up_full")
        sg_ready = sem("sg_ready")
        hh_ready = sem("hh_ready")
        ht_full = sem("ht_full")
        ht_read = sem("ht_read")
        y_full = sem("y_full")
        y_read = sem("y_read")
        stored = [sem(f"stored{n}") for n in range(2)]
        block = ctx.enter_context(nc.Block())
        PAIRS = ETILES // 2

        @block.sync
        def _(sp):
            sp.dma_start(IDENT[:, :], ident_d).then_inc(c_load, 16)

            def load(t, n):
                sp.dma_start(XG[n][:, :], xs[t]).then_inc(x_load[n], 16)
            load(0, 0)
            load(1, 1)
            for e in range(EXPERTS):
                sp.dma_start(WU[:, e, :, :], w_up[e].rearrange("(k p) n -> p k n", p=P)
                             ).then_inc(w_load, 16)
                sp.dma_start(WD[0:HP, e, :, :], w_down[e].rearrange("(k p) n -> p k n", p=HP)
                             ).then_inc(w_load, 16)
            with sp.Fori(0, PAIRS) as i:
                for n in range(2):
                    sp.wait_ge(xt_full, i * 2 + n + 1)
                    load(i * 2 + n + 2, n)
            sp.wait_ge(x_load[0], 16 * (PAIRS + 1))
            sp.wait_ge(x_load[1], 16 * (PAIRS + 1))
            sp.wait_ge(w_load, 32 * EXPERTS)
            sp.wait_ge(c_load, 16)

        @block.gpsimd
        def _(g):
            with g.Fori(0, PAIRS) as i:
                for n in range(2):
                    g.wait_ge(y_read, i * 2 + n + 1)
                    g.dma_start(ys[i * 2 + n], YO[n][:, :]).then_inc(stored[n], 16)
            g.wait_ge(stored[0], 16 * PAIRS)
            g.wait_ge(stored[1], 16 * PAIRS)

        @block.scalar
        def _(a):
            with a.Fori(0, PAIRS) as i:
                for n in range(2):
                    t = i * 2 + n
                    a.wait_ge(gate_full, t + 1)
                    a.wait_ge(sg_ready, t)
                    nc.scalar.activation(SG[n][:, :], PGA[n][:, 0:hid], ACT.Silu
                                         ).then_inc(sg_ready, 1)
                    a.wait_ge(ht_full, t + 1)
                    nc.scalar.activation(HT[n][0:HP, :, :].rearrange("p c t -> p (c t)"),
                                         PH[0:HP, 0:HC * P], ACT.Copy).then_inc(ht_read, 1)

        @block.vector
        def _(v):
            def turned(t, n):
                v.wait_ge(xt_full, t + 1)
                nc.vector.tensor_copy(XT[n][:, :, :].rearrange("p k t -> p (k t)"), PX[:, 0:D]
                                      ).then_inc(xt_read, 1)
            turned(0, 0)
            turned(1, 1)
            with v.Fori(0, PAIRS) as i:
                for n in range(2):
                    t = i * 2 + n
                    v.wait_ge(sg_ready, t + 1)
                    v.wait_ge(up_full, t + 1)
                    nc.vector.tensor_tensor(HH[n][:, :], SG[n][:, :], PUP[n][:, 0:hid], ALU.mult
                                            ).then_inc(hh_ready, 1)
                    turned(t + 2, n)
                    v.wait_ge(y_full, t + 1)
                    v.wait_ge(stored[n], i * 16)
                    nc.vector.tensor_copy(YO[n][:, :], PY[n][:, 0:D]).then_inc(y_read, 1)

        @block.tensor
        def _(pe):
            def turn(t, n, loads):
                pe.wait_ge(x_load[n], loads * 16)
                pe.wait_ge(xt_read, t)
                for k in range(KD):
                    ins = nc.tensor.transpose(PX[:, k * P:(k + 1) * P],
                                              XG[n][:, k * P:(k + 1) * P], IDENT[:, :])
                ins.then_inc(xt_full, 1)

            def project(n, bank, e, at, full):
                for k in range(KD):
                    ins = nc.tensor.matmul(bank[n][:, 0:hid], XT[n][:, k, :],
                                           WU[:, e, k, at:at + hid], start=(k == 0),
                                           stop=(k == KD - 1))
                ins.then_inc(full, 1)

            def expert(t):
                return pe.value_load(EXP_OF[0:1, bass.ds(t, 1)], min_val=0, max_val=EXPERTS - 1)

            pe.wait_ge(c_load, 16)
            turn(0, 0, 1)
            pe.wait_ge(w_load, 32 * EXPERTS)
            first = pe.value_load(EXP_OF[0:1, 0:1], min_val=0, max_val=EXPERTS - 1)
            pe.wait_ge(xt_read, 1)
            project(0, PGA, first, 0, gate_full)
            project(0, PUP, first, hid, up_full)
            turn(1, 1, 1)
            with pe.Fori(0, PAIRS) as i:
                for n in range(2):
                    t = i * 2 + n
                    m = 1 - n
                    here = expert(t)
                    ahead = expert(t + 1)
                    pe.wait_ge(xt_read, t + 2)
                    pe.wait_ge(sg_ready, t)
                    project(m, PGA, ahead, 0, gate_full)
                    pe.wait_ge(hh_ready, t + 1)
                    pe.wait_ge(ht_read, t)
                    for c in range(HC):
                        ins = nc.tensor.transpose(PH[0:HP, c * P:(c + 1) * P],
                                                  HH[n][:, c * HP:(c + 1) * HP], IDENT[:, :])
                    ins.then_inc(ht_full, 1)
                    project(m, PUP, ahead, hid, up_full)
                    turn(t + 2, n, i + 2)
                    pe.wait_ge(ht_read, t + 1)
                    if n:
                        pe.wait_ge(y_read, i * 2)
                    else:
                        pe.wait_ge(y_read, i * 2)
                    for c in range(HC):
                        ins = nc.tensor.matmul(PY[n][:, 0:D], HT[n][0:HP, c, :],
                                               WD[0:HP, here, c, :], start=(c == 0),
                                               stop=(c == HC - 1))
                    ins.then_inc(y_full, 1)


def combine_stage(nc, X, POS, WT, SHARED, ys, out, hs):
    with ExitStack() as ctx:
        s = Scope(nc, ctx, f"cb{hs}")
        sb, sem = s.sb, s.sem
        GY = [[sb(f"GY{c}_{n}", [P, D]) for n in range(TOPK)] for c in range(GT)]
        MHALF = sb("MHALF", [P, GT])
        STAT = sb("STAT", [P, GT, 6])
        MV = sb("MV", [P, GT, 2])
        VE = sb("VE", [P, GT])
        RSTD = sb("RSTD", [P, GT])
        EPSC = sb("EPSC", [P, GT])
        PAUSE = sb("PAUSE", [P, 1])
        U = sb("U", [P, GT, D])
        UN = sb("UN", [P, GT, D])
        gathered = [sem(f"gathered{c}") for c in range(GT)]
        used = sem("used")
        prep = sem("prep")
        vec = sem("vec")
        act = sem("act")
        sqrt_done = sem("sqrt_done")
        stats = sem("stats")
        x_done = sem("x_done")
        stored = sem("stored")
        block = ctx.enter_context(nc.Block())

        @block.gpsimd
        def _(g):
            for t in range(TILES):
                c = t % GT
                if t >= GT:
                    g.wait_ge(used, t - GT + 1)
                for n in range(TOPK):
                    g.indirect_dma_start(
                        out=GY[c][n][:, :], out_offset=None, in_=ys,
                        in_offset=bass.IndirectOffsetOnAxis(ap=POS[:, n, t:t + 1], axis=0)
                    ).then_inc(gathered[c], 16)

        @block.vector
        def _(v):
            V = nc.vector
            PER = GT * (3 if hs else 2) + 3 + GT
            with v.Fori(0, GROUPS) as i:
                link = chain_of(v, vec, i * PER)
                for c in range(GT):
                    v.wait_ge(gathered[c], (i + 1) * 16 * TOPK)
                    link(V.tensor_scalar(U[:, c, :], GY[c][0][:, :], WT[:, 0, bass.ds(i * GT + c, 1)],
                                         None, ALU.mult))
                    ins = V.scalar_tensor_tensor(
                        out=U[:, c, :], in0=GY[c][1][:, :], scalar=WT[:, 1, bass.ds(i * GT + c, 1)],
                        in1=U[:, c, :], op0=ALU.mult, op1=ALU.add)
                    ins.then_inc(used, 1)
                    v.wait_ge(used, i * GT + c + 1)
                    if hs:
                        link(V.tensor_tensor(U[:, c, :], U[:, c, :], SHARED[:, i, c, :], ALU.add))
                    link(V.bn_stats(STAT[:, c, :], U[:, c, :]))
                link(V.memset(PAUSE[:, :], 0.0), wait=False)
                for c in range(GT):
                    ins = V.bn_aggr(MV[:, c, :], STAT[:, c, :])
                link(ins)
                V.tensor_scalar(VE[:, :], MV[:, :, 1], EPS, None, ALU.add).then_inc(stats, 1)
                v.wait_ge(sqrt_done, i + 1)
                link(V.reciprocal(RSTD[:, :], RSTD[:, :]))
                for c in range(GT):
                    link(V.tensor_scalar(UN[:, c, :], U[:, c, :], MV[:, c, 0:1], RSTD[:, c:c + 1],
                                         ALU.subtract, ALU.mult))
                V.tensor_tensor(X[:, i, :, :], X[:, i, :, :], UN[:, :, :], ALU.add
                                ).then_inc(x_done, 1)
                assert link.n[0] == PER
            v.wait_ge(x_done, GROUPS)

        @block.scalar
        def _(a):
            with a.Fori(0, GROUPS) as i:
                a.wait_ge(stats, i + 1)
                nc.scalar.activation(RSTD[:, :], VE[:, :], ACT.Sqrt).then_inc(sqrt_done, 1)

        if out is not None:
            @block.sync
            def _(sp):
                with sp.Fori(0, GROUPS) as i:
                    sp.wait_ge(x_done, i + 1)
                    sp.dma_start(out[i], X[:, i, :, :]).then_inc(stored, 16)
                sp.wait_ge(stored, 16 * GROUPS)


def moe_layer(nc, X, xs, ys, w_router, gate_bias, w_up, w_down, w_sgate, w_sdown, hs, hid,
              consts, out):
    xs_tiles = xs.rearrange("(t p) d -> t p d", p=P)
    ys_tiles = ys.rearrange("(t p) d -> t p d", p=P)
    tag = f"moe{hs}_"
    with ExitStack() as ctx:
        def keep(name, shape, dt=F32):
            return ctx.enter_context(nc.sbuf_tensor(tag + name, shape, dt))
        POS = keep("POS", [P, TOPK, TILES], U32)
        WT = keep("WT", [P, TOPK, TILES])
        EXP_OF = keep("EXP_OF", [P, XS_TILES], I32)
        SHARED = keep("SHARED", [P, GROUPS, GT, D]) if hs else None
        with nc.sbuf_tensor(tag + "XN", [P, GROUPS, GT, D], F32) as XN, \
                nc.sbuf_tensor(tag + "LOG", [P, GROUPS, GT, EXPERTS], F32) as LOG:
            route_stage(nc, X, XN, LOG, SHARED, w_router, consts["ident"], w_sgate, w_sdown, hs)
            dispatch_stage(nc, XN, LOG, POS, WT, EXP_OF, gate_bias, consts["tri"], consts["rev"],
                           consts["tidx"], consts["step"], xs, hs)
        expert_stage(nc, EXP_OF, xs_tiles, ys_tiles, w_up, w_down, consts["ident"], hid)
        combine_stage(nc, X, POS, WT, SHARED, ys, out, hs)

AH_HEADS, AH_DIM = 16, 16
SCALE = float(D) ** -0.5
AT = SEQ // P
HALVES = SEQ // GROUP
PAIRED = AH_HEADS // 2
QUADS = AH_HEADS // 4
VP = 32
SHIFT_ROW = 32
SROWS = 49


def attention_stage(nc, X, wq, bq, wk, bk, wv, bv, wo, bo, ident_d, stack_d, one_row_d):
    with ExitStack() as ctx:
        s = Scope(nc, ctx, "at")
        sb, pb, sem = s.sb, s.pb, s.sem
        IDENT = sb("IDENT", [P, P])
        IDENTR = sb("IDENTR", [P, P], F32R)
        WQ = sb("WQ", [P, KD, D])
        WK = sb("WK", [P, KD, D])
        WV = sb("WV", [P, KD, AH_HEADS * VP])
        WO = sb("WO", [P, KD, D])
        BQ = sb("BQ", [P, KD])
        BK = sb("BK", [P, KD])
        BV = sb("BV", [P, AH_HEADS * VP])
        BO = sb("BO", [P, D])
        STACK = sb("STACK", [P, 4, 4, P], F32R)
        ONE_ROW = sb("ONE_ROW", [P, 1])
        MHALF = sb("MHALF", [P, GT])
        STAT = sb("STAT", [P, GT, 6])
        MV = sb("MV", [P, GT, 2])
        VE = sb("VE", [P, GT])
        RSTD = sb("RSTD", [P, GT])
        EPSC = sb("EPSC", [P, GT])
        PAUSE = sb("PAUSE", [P, 1])
        H = sb("H", [P, GT, D])
        HT = sb("HT", [P, KD, GROUP])
        F = [sb(f"F{n}", [P, KD, GROUP]) for n in range(2)]
        HI = [sb(f"HI{n}", [P, KD, GROUP], F32R) for n in range(2)]
        LO = [sb(f"LO{n}", [P, KD, GROUP], F32R) for n in range(2)]
        QS = sb("QS", [P, PAIRED, SEQ], F32R)
        KS = sb("KS", [P, PAIRED, SEQ], F32R)
        VS = sb("VS", [P, AT, AH_HEADS * VP])
        M2 = sb("M2", [P, 4, AT, HALVES])
        MP = sb("MP", [P, AT, 2, P], F32R)
        PBUF = 8
        PB = [sb(f"PB{n}", [P, GROUP]) for n in range(PBUF)]
        OS = sb("OS", [P, GROUP])
        RS = sb("RS", [P, GT, 4])
        ATT = sb("ATT", [P, AT, D])
        ATTT = [sb(f"ATTT{n}", [P, D]) for n in range(2)]
        U = H
        UN = HT[:, :, :].rearrange("p k (a d) -> p (k a) d", d=D)
        NR, NM = 4, 3
        RING = [pb(f"RING{n}", [P, GROUP]) for n in range(NR)]
        MRING = [pb(f"MRING{n}", [P, GROUP]) for n in range(NM)]
        PO = pb("PO", [P, GROUP])

        c_load = sem("c_load")
        prep = sem("prep")
        vec = sem("vec")
        gps = sem("gps")
        stats = sem("stats")
        rstd = sem("rstd")
        h_ready = sem("h_ready")
        r_full = sem("r_full")
        r_vec = sem("r_vec")
        r_act = sem("r_act")
        m_full = sem("m_full")
        m_read = sem("m_read")
        hi_ready = sem("hi_ready")
        lo_ready = sem("lo_ready")
        max_ready = sem("max_ready")
        pv_done = sem("pv_done")
        o_read = sem("o_read")
        x_done = sem("x_done")

        plan = []
        for g in range(HALVES):
            plan += [(("T", g, 0), "v"), (("T", g, 1), "a")]
            plan += [(("F", g, n, k), "v") for n in range(2) for k in range(KD)]
            plan += [(("V", g, c), "v") for c in range(GT)]
            plan += [(("ST", g, n, c), "va"[c % 2]) for n in range(2) for c in range(PAIRED)]
        for quad in range(QUADS):
            for g in range(HALVES):
                for kt in range(AT):
                    plan += [(("S", quad, g, kt, j), "a") for j in range(4)]
                    if kt == 1 and (quad or g):
                        before = (quad, g - 1) if g else (quad - 1, HALVES - 1)
                        plan += [(("OT",) + before, "v")]
        plan += [(("OT", QUADS - 1, HALVES - 1), "v")]
        for t in range(AT):
            plan += [(("AT", t), "a"), (("Y", t), "v")]
        while len(plan) % NR:
            plan += [(("pad", len(plan)), "v")]
        NUNITS = len(plan)
        seat, readers = {}, {"v": 0, "a": 0}
        for u, (name, who) in enumerate(plan):
            readers[who] += 1
            seat[name] = (u, who, readers[who])
        ring_read = {"v": r_vec, "a": r_act}
        NMU = QUADS * (4 * AT * HALVES + 2 * HALVES)
        NGROUPS = QUADS * HALVES * AT

        def wait_read(eng, i, u):
            _, who, n = seat[plan[u][0]]
            eng.wait_ge(ring_read[who], i * readers[who] + n)

        block = ctx.enter_context(nc.Block())

        @block.sync
        def _(sp):
            loads = ((IDENT[:, :], ident_d), (WQ[:, :, :], wq.rearrange("(k p) n -> p k n", p=P)),
                     (WK[:, :, :], wk.rearrange("(k p) n -> p k n", p=P)),
                     (WV[:, :, :], wv.rearrange("(k p) n -> p k n", p=P)),
                     (WO[:, :, :], wo.rearrange("(k p) n -> p k n", p=P)),
                     (BQ[:, :], bq), (BK[:, :], bk), (BV[:, :], bv), (BO[:, :], bo),
                     (ONE_ROW[:, :], one_row_d),
                     (VS[:, 0:4, :], stack_d))
            for dst, src in loads:
                sp.dma_start(dst, src).then_inc(c_load, 16)
            sp.wait_ge(c_load, 16 * len(loads))
        CLOAD = 16 * 11

        @block.gpsimd
        def _(g):
            g.wait_ge(prep, 2)
            with g.Fori(0, BATCH) as i:
                for n in range(2 * HALVES):
                    at = i * 2 * HALVES + n
                    g.wait_ge(stats, at * GT + GT)
                    nc.gpsimd.tensor_tensor(VE[:, :], MV[:, :, 1], EPSC[:, :], ALU.add
                                            ).then_inc(gps, 1)
                    g.wait_ge(gps, at + 1)
                    nc.gpsimd.tensor_tensor(RSTD[:, :], VE[:, :], MHALF[:, :], ALU.pow
                                            ).then_inc(rstd, 1)
            g.wait_ge(rstd, BATCH * 2 * HALVES)

        @block.vector
        def _(v):
            V = nc.vector
            V.memset(MHALF[:, :], -0.5).then_inc(prep, 1)
            V.memset(EPSC[:, :], EPS).then_inc(prep, 1)
            V.memset(MP[:, :, :, :].bitcast(F32), 0.0).then_inc(prep, 1)
            v.wait_ge(c_load, CLOAD)
            V.tensor_copy(STACK[:, :, :, :].rearrange("p a b c -> p (a b c)"),
                          VS[:, 0:4, :].rearrange("p a b -> p (a b)")
                          ).then_inc(prep, 1)
            V.tensor_copy(IDENTR[:, :], IDENT[:, :]).then_inc(prep, 1)
            V.tensor_scalar(BQ[:, :], BQ[:, :], SCALE, None, ALU.mult).then_inc(prep, 1)
            v.wait_ge(prep, 6)
            PER = 2 * HALVES * (GT + 1) + QUADS * HALVES + HALVES
            with v.Fori(0, BATCH) as i:
                link = chain_of(v, vec, i * PER)
                m_at = [0]

                def take(name):
                    u, who, _ = seat[name]
                    v.wait_ge(r_full, i * NUNITS + u + 1)
                    return RING[u % NR]

                def mtake():
                    v.wait_ge(m_full, i * NMU + m_at[0] + 1)
                    m_at[0] += 1
                    return MRING[(m_at[0] - 1) % NM]

                def normed(src, dst, n, done):
                    for c in range(GT):
                        link(V.bn_stats(STAT[:, c, :], src[c]), wait=False)
                    v.wait_ge(vec, i * PER + link.n[0])
                    link(V.memset(PAUSE[:, :], 0.0), wait=False)
                    for c in range(GT):
                        V.bn_aggr(MV[:, c, :], STAT[:, c, :]).then_inc(stats, 1)
                    v.wait_ge(rstd, i * 2 * HALVES + n + 1)
                    for c in range(GT):
                        ins = V.tensor_scalar(dst[:, c, :], src[c], MV[:, c, 0:1],
                                              RSTD[:, c:c + 1], ALU.subtract, ALU.mult)
                        if done is not None:
                            ins.then_inc(done, 1)
                    return ins

                for g in range(HALVES):
                    normed([X[:, i * HALVES + g, c, :] for c in range(GT)], H, g, h_ready)
                    V.tensor_copy(HT[:, 0, :], take(("T", g, 0))[:, :]).then_inc(r_vec, 1)
                    for n, bias in ((0, BQ), (1, BK)):
                        for k in range(KD):
                            bank = take(("F", g, n, k))
                            V.tensor_scalar(F[n][:, k, :], bank[:, :], 1.0 if n else SCALE,
                                            bias[:, k:k + 1], ALU.mult, ALU.add
                                            ).then_inc(r_vec, 1)
                    for c in range(GT):
                        bank = take(("V", g, c))
                        V.tensor_tensor(VS[:, g * GT + c, :], bank[:, :], BV[:, :], ALU.add
                                        ).then_inc(r_vec, 1)
                    for n in range(2):
                        v.wait_ge(hi_ready, (i * HALVES + g) * 2 + n + 1)
                        V.tensor_tensor(LO[n][:, :, :], F[n][:, :, :],
                                        HI[n][:, :, :].bitcast(F32), ALU.subtract
                                        ).then_inc(lo_ready, 1)
                    for n, dst in ((0, QS), (1, KS)):
                        for c in range(0, PAIRED, 2):
                            bank = take(("ST", g, n, c))
                            out = dst[:, c, g * GROUP:(g + 1) * GROUP]
                            if n:
                                ins = V.tensor_scalar(out, bank[:, :], ONE_ROW[:, 0:1], None,
                                                      ALU.add)
                            else:
                                ins = V.tensor_copy(out, bank[:, :])
                            ins.then_inc(r_vec, 1)

                def maxima(n):
                    j, qt, half = n // (AT * HALVES), n // HALVES % AT, n % HALVES
                    bank = mtake()
                    V.tensor_reduce(M2[:, j, qt, half:half + 1], bank[:, :], AX.X, ALU.max
                                    ).then_inc(m_read, 1)

                def shifts(quad):
                    v.wait_ge(m_read, i * NMU + m_at[0])
                    for j in range(4):
                        at = SHIFT_ROW + 64 * (j % 2)
                        V.tensor_reduce(MP[:, :, j // 2, at:at + 1], M2[:, j, :, :], AX.X, ALU.max,
                                        negate=True).then_inc(max_ready, 1)
                    for cc in range(2):
                        for half in range(HALVES):
                            bank = mtake()
                            q = QS[:, quad * 2 + cc, half * GROUP:(half + 1) * GROUP]
                            V.tensor_tensor(q, q.bitcast(F32), bank[:, :], ALU.add
                                            ).then_inc(m_read, 1)

                def normalise(quad, g):
                    bank = take(("OT", quad, g))
                    o = bank[:, :].rearrange("p (t j d) -> p t j d", t=GT, j=4)
                    link(V.reciprocal(RS[:, :, :].unsqueeze(3), o[:, :, :, AH_DIM:AH_DIM + 1]))
                    out = ATT[:, g * GT:(g + 1) * GT, quad * 64:(quad + 1) * 64]
                    V.tensor_tensor(out.rearrange("p t (j d) -> p t j d", j=4),
                                    o[:, :, :, 0:AH_DIM],
                                    RS[:, :, :].unsqueeze(3).to_broadcast([P, GT, 4, AH_DIM]),
                                    ALU.mult).then_inc(r_vec, 1)

                UNITS1 = 4 * AT * HALVES
                for n in range(UNITS1):
                    maxima(n)
                shifts(0)
                for quad in range(QUADS):
                    for step in range(HALVES * AT):
                        if quad < QUADS - 1:
                            for n in range(4 * step, 4 * step + 4):
                                maxima(n)
                        g, kt = step // AT, step % AT
                        if kt == 1 and (quad or g):
                            normalise(*((quad, g - 1) if g else (quad - 1, HALVES - 1)))
                    if quad < QUADS - 1:
                        shifts(quad + 1)
                normalise(QUADS - 1, HALVES - 1)
                for g in range(HALVES):
                    for c in range(GT):
                        bank = take(("Y", g * GT + c))
                        V.tensor_tensor(U[:, c, :], bank[:, 0:D], BO[:, :], ALU.add
                                        ).then_inc(r_vec, 1)
                    wait_read(v, i, seat[("Y", g * GT + GT - 1)][0])
                    link(normed([U[:, c, :] for c in range(GT)], UN, HALVES + g, None))
                    x = X[:, i * HALVES + g, :, :]
                    V.tensor_tensor(x, x, UN[:, :, :], ALU.add).then_inc(x_done, 1)
                for name, _ in plan:
                    if name[0] == "pad":
                        take(name)
                        V.tensor_copy(RS[:, 0, 0:1], MHALF[:, 0:1]).then_inc(r_vec, 1)
                        v.wait_ge(r_vec, i * readers["v"] + seat[name][2])
                v.wait_ge(x_done, i * HALVES + HALVES)
                assert m_at[0] == NMU
                assert link.n[0] == PER, link.n[0]

        @block.scalar
        def _(a):
            a.wait_ge(prep, 6)
            with a.Fori(0, BATCH) as i:
                def take(name):
                    u, who, _ = seat[name]
                    a.wait_ge(r_full, i * NUNITS + u + 1)
                    return RING[u % NR]
                for g in range(HALVES):
                    nc.scalar.activation(HT[:, 1, :], take(("T", g, 1))[:, :], ACT.Copy
                                         ).then_inc(r_act, 1)
                    for n in range(2):
                        wait_read(a, i, seat[("F", g, n, KD - 1)][0])
                        nc.scalar.activation(HI[n][:, :, :], F[n][:, :, :], ACT.Copy
                                             ).then_inc(hi_ready, 1)
                    for n, dst in ((0, QS), (1, KS)):
                        for c in range(1, PAIRED, 2):
                            bank = take(("ST", g, n, c))
                            out = dst[:, c, g * GROUP:(g + 1) * GROUP]
                            if n:
                                ins = nc.scalar.activation(out, bank[:, :], ACT.Identity,
                                                           bias=ONE_ROW[:, 0:1])
                            else:
                                ins = nc.scalar.activation(out, bank[:, :], ACT.Copy)
                            ins.then_inc(r_act, 1)
                for quad in range(QUADS):
                    for g in range(HALVES):
                        for kt in range(AT):
                            step = (quad * HALVES + g) * AT + kt
                            if step >= PBUF // 4:
                                a.wait_ge(pv_done, i * NGROUPS + step - PBUF // 4 + 1)
                            for j in range(4):
                                bank = take(("S", quad, g, kt, j))
                                nc.scalar.activation(PB[(step * 4 + j) % PBUF][:, :], bank[:, :],
                                                     ACT.Exp).then_inc(r_act, 1)
                            if kt == 0 and (quad or g):
                                n = quad * HALVES + g
                                a.wait_ge(pv_done, i * NGROUPS + n * AT)
                                nc.scalar.activation(OS[:, :], PO[:, :], ACT.Copy
                                                     ).then_inc(o_read, 1)
                a.wait_ge(pv_done, i * NGROUPS + NGROUPS)
                a.wait_ge(o_read, i * QUADS * HALVES + QUADS * HALVES - 1)
                nc.scalar.activation(OS[:, :], PO[:, :], ACT.Copy).then_inc(o_read, 1)
                for t in range(AT):
                    nc.scalar.activation(ATTT[t % 2][:, :], take(("AT", t))[:, 0:D], ACT.Copy
                                         ).then_inc(r_act, 1)

        @block.tensor
        def _(pe):
            T = nc.tensor
            pe.wait_ge(prep, 6)
            with pe.Fori(0, BATCH) as i:
                m_at = [0]
                order = [0]

                def put(name):
                    u, _, _ = seat[name]
                    assert u == order[0], (name, u, order[0])
                    order[0] += 1
                    if u >= NR:
                        wait_read(pe, i, u - NR)
                    return RING[u % NR]

                def mput():
                    n = m_at[0]
                    m_at[0] += 1
                    pe.wait_ge(m_read, i * NMU + max(0, n - NM + 1))
                    return MRING[n % NM]

                pe.wait_ge(r_vec, i * readers["v"])
                pe.wait_ge(r_act, i * readers["a"])
                for g in range(HALVES):
                    for k in range(KD):
                        bank = put(("T", g, k))
                        for c in range(GT):
                            pe.wait_ge(h_ready, (i * HALVES + g) * GT + c + 1)
                            ins = T.transpose(bank[:, c * P:(c + 1) * P],
                                              H[:, c, k * P:(k + 1) * P], IDENT[:, :])
                        ins.then_inc(r_full, 1)
                    wait_read(pe, i, seat[("T", g, 0)][0])
                    wait_read(pe, i, seat[("T", g, 1)][0])
                    for n, w in ((0, WQ), (1, WK)):
                        for m in range(KD):
                            bank = put(("F", g, n, m))
                            for k in range(KD):
                                ins = T.matmul(bank[:, :], w[:, k, m * P:(m + 1) * P], HT[:, k, :],
                                               start=(k == 0), stop=(k == KD - 1))
                            ins.then_inc(r_full, 1)
                    for c in range(GT):
                        bank = put(("V", g, c))
                        for k in range(KD):
                            ins = T.matmul(bank[:, :], HT[:, k, c * P:(c + 1) * P], WV[:, k, :],
                                           start=(k == 0), stop=(k == KD - 1))
                        ins.then_inc(r_full, 1)
                    for n in range(2):
                        pe.wait_ge(lo_ready, (i * HALVES + g) * 2 + n + 1)
                        for c in range(PAIRED):
                            bank = put(("ST", g, n, c))
                            k, cc = c // 4, c % 4
                            T.matmul(bank[:, :], STACK[:, 2 * n, cc, :], HI[n][:, k, :],
                                     start=True, stop=False)
                            T.matmul(bank[:, :], STACK[:, 2 * n + 1, cc, :], LO[n][:, k, :],
                                     start=False, stop=True).then_inc(r_full, 1)
                wait_read(pe, i, seat[("ST", HALVES - 1, 1, PAIRED - 1)][0])
                wait_read(pe, i, seat[("ST", HALVES - 1, 1, PAIRED - 2)][0])

                def rows(j):
                    return slice(64 * (j % 2), 64 * (j % 2) + SROWS)

                def maxima(quad, n):
                    j, qt, half = n // (AT * HALVES), n // HALVES % AT, n % HALVES
                    c = quad * 2 + j // 2
                    T.matmul(mput()[:, :], QS[rows(j), c, qt * P:(qt + 1) * P],
                             KS[rows(j), c, half * GROUP:(half + 1) * GROUP], start=True,
                             stop=True).then_inc(m_full, 1)

                def shifts(quad):
                    pe.wait_ge(max_ready, i * QUADS * 4 + quad * 4 + 4)
                    for cc in range(2):
                        for half in range(HALVES):
                            bank = mput()
                            for t in range(GT):
                                ins = T.matmul(bank[:, t * P:(t + 1) * P],
                                               MP[:, half * GT + t, cc, :], IDENTR[:, :],
                                               start=True, stop=True)
                            ins.then_inc(m_full, 1)

                def with_values(step):
                    quad, g, kt = step // (HALVES * AT), step // AT % HALVES, step % AT
                    n = quad * HALVES + g
                    wait_read(pe, i, seat[("S", quad, g, kt, 3)][0])
                    if kt == 0:
                        pe.wait_ge(o_read, i * QUADS * HALVES + n)
                    for j in range(4):
                        head = quad * 4 + j
                        ins = T.matmul(PO[VP * j:VP * (j + 1), :],
                                       VS[:, kt, head * VP:(head + 1) * VP],
                                       PB[(step * 4 + j) % PBUF][:, :], start=(kt == 0),
                                       stop=(kt == AT - 1))
                    ins.then_inc(pv_done, 1)

                def turn_output(quad, g):
                    pe.wait_ge(o_read, i * QUADS * HALVES + quad * HALVES + g + 1)
                    bank = put(("OT", quad, g))
                    for t in range(GT):
                        ins = T.transpose(bank[:, t * P:(t + 1) * P], OS[:, t * P:(t + 1) * P],
                                          IDENT[:, :])
                    ins.then_inc(r_full, 1)

                for n in range(4 * AT * HALVES):
                    maxima(0, n)
                shifts(0)
                for quad in range(QUADS):
                    pe.wait_ge(m_read, i * NMU + m_at[0])
                    for step in range(HALVES * AT):
                        g, kt = step // AT, step % AT
                        whole = quad * HALVES * AT + step
                        for j in range(4):
                            c = quad * 2 + j // 2
                            T.matmul(put(("S", quad, g, kt, j))[:, :],
                                     KS[rows(j), c, kt * P:(kt + 1) * P],
                                     QS[rows(j), c, g * GROUP:(g + 1) * GROUP], start=True,
                                     stop=True).then_inc(r_full, 1)
                            if quad < QUADS - 1:
                                maxima(quad + 1, 4 * step + j)
                        if whole:
                            with_values(whole - 1)
                        if kt == 1 and (quad or g):
                            turn_output(*((quad, g - 1) if g else (quad - 1, HALVES - 1)))
                    if quad < QUADS - 1:
                        shifts(quad + 1)
                with_values(QUADS * HALVES * AT - 1)
                turn_output(QUADS - 1, HALVES - 1)
                wait_read(pe, i, seat[("OT", QUADS - 1, HALVES - 1)][0])
                for t in range(AT):
                    bank = put(("AT", t))
                    for k in range(KD):
                        ins = T.transpose(bank[:, k * P:(k + 1) * P],
                                          ATT[:, t, k * P:(k + 1) * P], IDENT[:, :])
                    ins.then_inc(r_full, 1)
                    wait_read(pe, i, seat[("AT", t)][0])
                    bank = put(("Y", t))
                    for k in range(KD):
                        ins = T.matmul(bank[:, 0:D], ATTT[t % 2][:, k * P:(k + 1) * P], WO[:, k, :],
                                       start=(k == 0), stop=(k == KD - 1))
                    ins.then_inc(r_full, 1)
                for name, _ in plan:
                    if name[0] == "pad":
                        T.transpose(put(name)[:, 0:P], IDENT[:, :], IDENT[:, :]
                                    ).then_inc(r_full, 1)


def whole_program(nc, a, out):
    xs = nc.dram_tensor("routed_rows", (XS_TILES * P, D), F32, kind="Internal").ap()
    ys = nc.dram_tensor("expert_rows", (ETILES * P, D), F32, kind="Internal").ap()
    with nc.sbuf_tensor("X", [P, GROUPS, GT, D], F32) as X:
        mamba_stage(nc, X, a["x"], a["w_in"], a["ln_w"], a["ln_b"], a["dt_bias"], a["a_log"],
                    a["d_skip"], a["norm_w"], a["w_out"], a["w_fc1"], a["b_fc1"], a["w_fc2"],
                    a["b_fc2"], a["ident"], a["tri"], a["mask"], a["sel"], a["keep"],
                    xs.rearrange("(t p r) d -> t p (r d)", p=P, r=8))
        moe_layer(nc, X, xs, ys, a["router0"], a["gate_bias"], a["up0"], a["down0"],
                  a["shared_up"], a["shared_down"], 352, 176, a, None)
        attention_stage(nc, X, a["wq"], a["bq"], a["wk"], a["bk"], a["wv"], a["bv"], a["wo"],
                        a["bo"], a["ident"], a["stack"], a["one_row"])
        moe_layer(nc, X, xs, ys, a["router1"], a["gate_bias"], a["up1"], a["down1"], None, None,
                  0, 512, a, out)


def _constants(np):
    t = np.arange(P)
    full = lambda v: np.ascontiguousarray(np.broadcast_to(np.asarray(v, np.float32), (P, len(v))))
    c = {
        "ident": np.eye(P, dtype=np.float32),
        "tri": (t[:, None] <= t[None, :]).astype(np.float32),
        "mask": np.tile(np.where(t[:, None] <= t[None, :], 0, -1e30).astype(np.float32), (1, GT)),
        "sel": np.repeat(np.eye(GT * HEADS, dtype=np.float32)[:, :, None], P, axis=2),
        "keep": full(np.arange(GROUPS) % (SEQ // GROUP) != 0),
        "rev": full(EXPERTS - np.arange(EXPERTS)),
        "tidx": full(np.arange(ETILES)),
        "step": full(P * np.arange(TILES)),
    }
    stack = np.zeros((P, 4, 4, P), np.float32)
    d = np.arange(AH_DIM)
    for cc in range(4):
        for pair in range(2):
            src, at = (2 * cc + pair) * AH_DIM + d, 64 * pair
            stack[src, 0, cc, at + d] = 1
            stack[src, 0, cc, at + SHIFT_ROW + 1 + d] = 1
            stack[src, 1, cc, at + AH_DIM + d] = 1
            stack[src, 2, cc, at + d] = 1
            stack[src, 2, cc, at + AH_DIM + d] = 1
            stack[src, 3, cc, at + SHIFT_ROW + 1 + d] = 1
    c["stack"] = stack.reshape(P, 4, GROUP)
    c["one_row"] = np.isin(t, (SHIFT_ROW, 64 + SHIFT_ROW)).astype(np.float32)[:, None]
    return c


def _layout(np, v):
    def turned(name):
        return np.swapaxes(v[name], -1, -2)

    def chunked(name):
        return v[name].reshape(-1, P).T

    def rows(name):
        return np.broadcast_to(v[name], (P, v[name].shape[-1]))
    w = turned("L0_attn_in_proj_w")
    cut = np.cumsum([D_INNER, D_XB, HEADDIM, HEADDIM, D_INNER])
    z, x, b0, b1, c, dt = np.split(w, cut, axis=1)
    wv = np.zeros((D, AH_HEADS, VP), np.float32)
    wv[:, :, 0:AH_DIM] = v["L1_attn_wv"].reshape(D, AH_HEADS, AH_DIM)
    bv = np.zeros((AH_HEADS, VP), np.float32)
    bv[:, 0:AH_DIM] = v["L1_attn_bv"].reshape(AH_HEADS, AH_DIM)
    bv[:, AH_DIM] = 1
    a = {
        "x": v["L0_attn_hidden_states"].reshape(GROUPS, GT, P, D).transpose(0, 2, 1, 3),
        "w_in": np.concatenate([z, x, b0, b0, b1, b1, dt, c], axis=1),
        "ln_w": chunked("L0_attn_ln_w"), "ln_b": chunked("L0_attn_ln_b"),
        "dt_bias": rows("L0_attn_dt_bias"), "a_log": rows("L0_attn_A_log"),
        "d_skip": rows("L0_attn_Dp"), "norm_w": chunked("L0_attn_norm_w"),
        "w_out": turned("L0_attn_out_proj_w"), "w_fc1": turned("L0_attn_fc1_w"),
        "b_fc1": chunked("L0_attn_fc1_b"), "w_fc2": turned("L0_attn_fc2_w"),
        "b_fc2": rows("L0_attn_fc2_b"),
        "router0": turned("L0_ffn_gate_w"), "gate_bias": rows("L0_ffn_gate_bias"),
        "shared_up": turned("L0_ffn_shared_gw"), "shared_down": turned("L0_ffn_shared_dw"),
        "up0": turned("L0_ffn_up_w"), "down0": turned("L0_ffn_down_w"),
        "wq": v["L1_attn_wq"], "wk": v["L1_attn_wk"], "wo": v["L1_attn_wo"],
        "wv": wv.reshape(D, AH_HEADS * VP), "bq": chunked("L1_attn_bq"),
        "bk": chunked("L1_attn_bk"),
        "bv": np.broadcast_to(bv.reshape(-1), (P, AH_HEADS * VP)), "bo": rows("L1_attn_bo"),
        "router1": turned("L1_ffn_router_weight"), "up1": turned("L1_ffn_ws"),
        "down1": turned("L1_ffn_w2s"),
    }
    return {k: np.ascontiguousarray(x) for k, x in a.items()}


def kernel(**inputs):
    import numpy as np
    import concourse.bacc as bacc
    from concourse.bass_utils import run_bass_kernel_spmd

    arrays = _layout(np, {k: np.asarray(x) for k, x in inputs.items()})
    arrays.update(_constants(np))
    nc = bacc.Bacc("TRN2", target_bir_lowering=False, num_devices=1)
    aps = {k: nc.dram_tensor(f"in_{k}", x.shape, mybir.dt.from_np(x.dtype),
                             kind="ExternalInput").ap() for k, x in arrays.items()}
    out = nc.dram_tensor("out", (GROUPS, P, GT, D), F32, kind="ExternalOutput").ap()
    whole_program(nc, aps, out)
    r = run_bass_kernel_spmd(nc, [{f"in_{k}": x for k, x in arrays.items()}], core_ids=[0])
    y = r.results[0]["out"]
    return y.transpose(0, 2, 1, 3).reshape(BATCH, SEQ, D)
```

```python
import concourse.bass as bass
from concourse import mybir
from contextlib import ExitStack

F32 = mybir.dt.float32
F32R = mybir.dt.float32r
BF16 = mybir.dt.bfloat16
I32 = mybir.dt.int32
U32 = mybir.dt.uint32
ALU = mybir.AluOpType
ACT = mybir.ActivationFunctionType
AX = mybir.AxisListType

P = 128
BATCH, SEQ, D = 4, 1024, 256
TOKENS = BATCH * SEQ
TILES = TOKENS // P
GT = 4
GROUP = GT * P
GROUPS = TILES // GT
KD = D // P
EPS = 1e-5


class Scope:

    def __init__(self, nc, ctx, stage):
        self.nc, self.ctx, self.stage = nc, ctx, stage
        self.sems = []
        ctx.callback(self.release)

    def sb(self, name, shape, dt=F32):
        return self.ctx.enter_context(self.nc.sbuf_tensor(f"{self.stage}_{name}", shape, dt))

    def pb(self, name, shape, dt=F32):
        return self.ctx.enter_context(self.nc.psum_tensor(f"{self.stage}_{name}", shape, dt))

    def sem(self, name):
        self.sems.append(self.nc.alloc_semaphore(name=f"{self.stage}_{name}"))
        return self.sems[-1]

    def release(self):
        self.nc.clear_and_free_semaphores(self.sems)
        self.nc.all_engine_barrier()


def chain_of(eng, sem, at=0):
    n = [0]

    def link(ins, wait=True):
        n[0] += 1
        ins.then_inc(sem, 1)
        if wait:
            eng.wait_ge(sem, at + n[0])
    link.n = n
    return link


def wait(eng, sem, value):
    if not isinstance(value, int) or value > 0:
        eng.wait_ge(sem, value)


D_INNER, D_XB, HEADDIM, D_STATE = 512, 128, 64, 64
HEADS = D_INNER // HEADDIM
KV = D_XB // HEADDIM
REP = HEADS // KV
INTER = 1024
CZ, CX = 0, D_INNER
CB = CX + D_XB
CDT = CB + 2 * D_XB
CC = CDT + HEADS
CEND = CC + D_INNER
XBD = CC - CX
FC1_TILES = INTER // P
Z_TILES = D_INNER // P


HALF = (slice(0, 64), slice(64, 128))


def mamba_stage(nc, X, x_dram, w_in, ln_w, ln_b, dt_bias, a_log, d_skip, norm_w, w_out,
                w_fc1, b_fc1, w_fc2, b_fc2, ident_d, tri_d, mask_d, sel_d, sel2_d, keep_d,
                xs_zero):
    with ExitStack() as ctx:
        s = Scope(nc, ctx, "mb")
        sb, pb, sem = s.sb, s.pb, s.sem
        N32 = GT * HEADS
        WIN = sb("WIN", [P, KD, CEND])
        WF1 = sb("WF1", [P, KD, INTER])
        WF2 = sb("WF2", [P, FC1_TILES, D])
        WOUT = sb("WOUT", [P, Z_TILES, D])
        IDENT = sb("IDENT", [P, P])
        TRI = sb("TRI", [P, P])
        ONES = sb("ONES", [P, P])
        MASKB = sb("MASKB", [P, GROUP], BF16)
        IDENTB = sb("IDENTB", [P, P], BF16)
        SEL = sb("SEL", [P, N32, P], F32R)
        SEL2 = sb("SEL2", [P, N32 // 2, P], F32R)
        LNW = sb("LNW", [P, KD])
        LNB = sb("LNB", [P, KD])
        NORMW = sb("NORMW", [P, Z_TILES])
        BF1 = sb("BF1", [P, FC1_TILES])
        BF2 = sb("BF2", [P, D])
        DTB = sb("DTB", [P, HEADS])
        AH = sb("AH", [P, HEADS])
        NEGA = sb("NEGA", [P, HEADS])
        DSK = sb("DSK", [P, HEADS])
        KEEP = sb("KEEP", [P, GROUPS])
        MHALF = sb("MHALF", [P, GT])
        EPSC = sb("EPSC", [P, GT])
        PAUSE = sb("PAUSE", [P, 1])
        ZERO = sb("ZERO", [P, 1024])
        STAT = sb("STAT", [P, GT, 6])
        MV = [sb(f"MV{n}", [P, GT, 2]) for n in range(3)]
        VE = sb("VE", [P, GT])
        RSTD = [sb(f"RSTD{n}", [P, GT]) for n in range(3)]
        XN = sb("XN", [P, GT, D])
        XNB = sb("XNB", [P, GT, D])
        H = sb("H", [P, GT, D])
        HT = sb("HT", [P, KD, GROUP])
        BT = sb("BT", [P, KV, 2, GROUP])
        CT = sb("CT", [P, HEADS // 2, GROUP])
        XB = sb("XB", [P, GT, XBD])
        ZS = sb("ZS", [P, GT, D_INNER])
        A1 = sb("A1", [P, FC1_TILES, GROUP])
        DTR = sb("DTR", [P, GT, HEADS])
        DTE = sb("DTE", [P, GT, HEADS])
        DTL = sb("DTL", [P, GT, HEADS])
        DT = sb("DT", [P, GT, HEADS])
        DA = sb("DA", [P, 2, N32])
        LT = sb("LT", [P, P], F32R)
        CAT = sb("CAT", [P, 3, N32])
        EXPS = sb("EXPS", [P, 3, N32])
        NEGL = sb("NEGL", [P, N32])
        EDEC = sb("EDEC", [P, HEADS, P])
        ECT = sb("ECT", [P, HEADS // 2, P])
        W = [sb(f"W{n}", [P, HEADS, P]) for n in range(2)]
        CTS = [sb(f"CTS{n}", [P, HEADS // 2, P]) for n in range(2)]
        XDT = [sb(f"XDT{n}", [P, HEADS, HEADDIM]) for n in range(2)]
        XEND = [sb(f"XEND{n}", [P, HEADS, HEADDIM]) for n in range(2)]
        XSKIP = [sb(f"XSKIP{n}", [P, D_INNER]) for n in range(2)]
        STATE = sb("STATE", [P, HEADS, HEADDIM])
        Y1 = sb("Y1", [P, D_INNER])
        G1 = sb("G1", [P, D_INNER])
        SQ = sb("SQ", [P, D_INNER])
        MASKF = SQ
        SSQ = sb("SSQ", [P, GT])
        RMSV = sb("RMSV", [P, 1])
        RMS = sb("RMS", [P, GT])
        G1T = sb("G1T", [P, Z_TILES, P])
        U = sb("U", [P, GT, D])
        UN = sb("UN", [P, GT, D])

        PP = [pb(f"PP{n}", [P, GROUP]) for n in range(2)]
        PL = pb("PL", [P, 2 * GROUP])
        PG = pb("PG", [P, 2 * GROUP])
        PST = pb("PST", [P, GROUP])
        PY = pb("PY", [P, GROUP])

        c_first = sem("c_first")
        c_rest = sem("c_rest")
        prep = sem("prep")
        act_prep = sem("act_prep")
        x_in = sem("x_in")
        ln_vec = sem("ln_vec")
        vec = sem("vec")
        un_vec = sem("un_vec")
        scal = sem("scal")
        ln_gps = sem("ln_gps")
        rms_gps = sem("rms_gps")
        un_gps = sem("un_gps")
        stats = sem("stats")
        rstd = sem("rstd")
        u_stats = sem("u_stats")
        u_rstd = sem("u_rstd")
        xn_ready = sem("xn_ready")
        h_ready = sem("h_ready")
        pp_full = sem("pp_full")
        pp_read = [sem(f"pp_read{n}") for n in range(2)]
        dt_in = sem("dt_in")
        dt_log = sem("dt_log")
        da_ready = sem("da_ready")
        lt_ready = sem("lt_ready")
        cat_ready = sem("cat_ready")
        exps_ready = sem("exps_ready")
        xnb_ready = sem("xnb_ready")
        lb_ready = sem("lb_ready")
        g_ready = sem("g_ready")
        decay_done = sem("decay_done")
        w_done = sem("w_done")
        xdt_done = sem("xdt_done")
        xend_done = sem("xend_done")
        cts_done = sem("cts_done")
        xskip_done = sem("xskip_done")
        y_ready = sem("y_ready")
        kept = sem("kept")
        s_done = sem("s_done")
        y_used = sem("y_used")
        g1_ready = sem("g1_ready")
        ssq_done = sem("ssq_done")
        rms_done = sem("rms_done")
        un_ready = sem("un_ready")
        x_done = sem("x_done")
        z_fill = sem("z_fill")

        plan = [("T", k) for k in range(KD)]
        plan += [("B", k) for k in range(KV)]
        plan += [("C", m) for m in range(HEADS // 2)]
        plan += [("X", c) for c in range(GT)]
        plan += [("Z", c) for c in range(GT)]
        plan += [("CUM", 0)]
        plan += [("F1", m) for m in range(FC1_TILES)]
        plan += [(n, c) for n, c in
                 (("E", 0), ("F2", 0), ("E", 1), ("F2", 1), ("E", 2), ("F2", 2), ("GT", 0),
                  ("O", 0), ("E", 3), ("F2", 3), ("GT", 1), ("O", 1), ("GT", 2), ("O", 2),
                  ("GT", 3), ("O", 3))]
        plan += [("PAD", 0)]
        UNITS = len(plan)
        assert UNITS % 2 == 0
        seat = {name: u for u, name in enumerate(plan)}

        def read(eng, i, *name):
            u = seat[name]
            wait(eng, pp_read[u % 2], i * (UNITS // 2) + u // 2 + 1)

        def take(eng, i, *name):
            u = seat[name]
            eng.wait_ge(pp_full, i * UNITS + u + 1)
            return PP[u % 2], pp_read[u % 2]
        PREPARED = 18

        block = ctx.enter_context(nc.Block())

        @block.sync
        def _(sp):
            for dst, src in ((IDENT[:, :], ident_d), (LNW[:, :], ln_w), (LNB[:, :], ln_b),
                             (WIN[:, :, :], w_in.rearrange("(k p) n -> p k n", p=P)),
                             (DTB[:, :], dt_bias), (AH[:, :], a_log)):
                sp.dma_start(dst, src).then_inc(c_first, 16)
            sp.dma_start(X[:, 0, :, :], x_dram[0]).then_inc(x_in, 16)
            for dst, src in ((DSK[:, :], d_skip), (TRI[:, :], tri_d), (MASKF[:, :], mask_d),
                             (ZS[0:64, :, :].rearrange("p a b -> p (a b)"), sel2_d),
                             (A1[0:64, :, :].rearrange("p a b -> p (a b)"), sel_d),
                             (KEEP[:, :], keep_d),
                             (NORMW[:, :], norm_w), (BF1[:, :], b_fc1), (BF2[:, :], b_fc2),
                             (WOUT[:, :, :], w_out.rearrange("(k p) n -> p k n", p=P)),
                             (WF1[:, :, :], w_fc1.rearrange("(k p) n -> p k n", p=P)),
                             (WF2[:, :, :], w_fc2.rearrange("(k p) n -> p k n", p=P))):
                sp.dma_start(dst, src).then_inc(c_rest, 16)
            with sp.Fori(1, GROUPS) as i:
                sp.wait_ge(x_in, i * 16)
                sp.dma_start(X[:, i, :, :], x_dram[i]).then_inc(x_in, 16)
            sp.wait_ge(prep, 9)
            with sp.Fori(0, xs_zero.shape[0]) as i:
                sp.dma_start(xs_zero[i], ZERO[:, :]).then_inc(z_fill, 16)
            sp.wait_ge(z_fill, 16 * xs_zero.shape[0])
        C_FIRST, C_REST = 16 * 6, 16 * 12

        @block.vector
        def _(v):
            V = nc.vector

            def moments(src, mv, chain, at, done):
                for c in range(GT):
                    V.bn_stats(STAT[:, c, :], src[c]).then_inc(chain, 1)
                v.wait_ge(chain, at + GT)
                V.memset(PAUSE[:, :], 0.0).then_inc(chain, 1)
                for c in range(GT):
                    V.bn_aggr(mv[:, c, :], STAT[:, c, :]).then_inc(done, 1)

            LN_CHAIN = 2 * (GT + 1)

            def norm_x(j):
                v.wait_ge(x_in, j * 16 + 16)
                moments([X[:, j, c, :] for c in range(GT)], MV[0], ln_vec, j * LN_CHAIN, stats)

            def norm_h(j):
                v.wait_ge(rstd, j * 2 + 1)
                wait(v, xnb_ready, j * 1)
                for c in range(GT):
                    V.tensor_scalar(XN[:, c, :], X[:, j, c, :], MV[0][:, c, 0:1],
                                    RSTD[0][:, c:c + 1], ALU.subtract, ALU.mult
                                    ).then_inc(xn_ready, 1)
                v.wait_ge(xn_ready, j * GT + GT)
                moments([XN[:, c, :] for c in range(GT)], MV[1], ln_vec,
                        j * LN_CHAIN + GT + 1, stats)

            def write_h(j):
                v.wait_ge(rstd, j * 2 + 2)
                for c in range(GT):
                    V.tensor_scalar(H[:, c, :], XN[:, c, :], MV[1][:, c, 0:1],
                                    RSTD[1][:, c:c + 1], ALU.subtract, ALU.mult
                                    ).then_inc(h_ready, 1)

            def moments_u(j):
                read(v, j, "O", GT - 2)
                read(v, j, "O", GT - 1)
                moments([U[:, c, :] for c in range(GT)], MV[2], un_vec, j * (GT + 1), u_stats)

            def norm_u(j):
                v.wait_ge(u_rstd, j + 1)
                wait(v, x_done, j * GT)
                for c in range(GT):
                    V.tensor_scalar(UN[:, c, :], U[:, c, :], MV[2][:, c, 0:1],
                                    RSTD[2][:, c:c + 1], ALU.subtract, ALU.mult
                                    ).then_inc(un_ready, 1)

            def body(i, first, last):
                VEC = 3 + GT
                link = chain_of(v, vec, i * VEC)
                bank, done = take(v, i, "B", 0)
                for q, r in enumerate(HALF):
                    ins = V.tensor_copy(BT[r, 0, q, :], bank[r, :])
                ins.then_inc(done, 1)
                for m in (0, 2):
                    bank, done = take(v, i, "C", m)
                    V.tensor_copy(CT[:, m, :], bank[:, :]).then_inc(done, 1)
                for c in range(GT):
                    bank, done = take(v, i, "X", c)
                    V.tensor_copy(XB[:, c, :], bank[:, 0:XBD]).then_inc(done, 1)
                read(v, i, "X", GT - 2)
                read(v, i, "X", GT - 1)
                V.tensor_tensor(DTR[:, :, :], XB[:, :, CDT - CX:XBD],
                                DTB[:, :].unsqueeze(1).to_broadcast([P, GT, HEADS]), ALU.add
                                ).then_inc(dt_in, 1)
                if not first:
                    norm_u(i - 1)
                v.wait_ge(dt_log, i + 1)
                link(V.scalar_tensor_tensor(out=DT[:, :, :], in0=DTR[:, :, :], scalar=0.0,
                                            in1=DTL[:, :, :], op0=ALU.max, op1=ALU.add))
                for n in range(2):
                    ins = V.tensor_tensor(
                        DA[:, n, :].rearrange("p (c h) -> p c h", c=GT), DT[:, :, :],
                        NEGA[:, :].unsqueeze(1).to_broadcast([P, GT, HEADS]), ALU.mult)
                ins.then_inc(da_ready, 1)
                bank, done = take(v, i, "CUM", 0)
                sums = bank[:, 0:2 * N32].rearrange("p (a n) -> p a n", a=2)
                rows = bank[0:64, 2 * N32:2 * N32 + P]
                link(V.tensor_copy(LT[0:64, :], rows))
                V.tensor_tensor(LT[N32:2 * N32, :], rows[N32:2 * N32, :],
                                LT[N32:2 * N32, :].bitcast(F32), ALU.subtract
                                ).then_inc(lt_ready, 1)
                V.tensor_copy(CAT[:, 0:2, :], sums).then_inc(done, 1)
                read(v, i, "CUM", 0)
                link(V.tensor_scalar(NEGL[:, :], CAT[:, 0, :], -1.0, None, ALU.mult))
                V.tensor_tensor(CAT[:, 2, :], CAT[:, 1, :], CAT[:, 0, :], ALU.subtract
                                ).then_inc(cat_ready, 1)
                V.tensor_scalar(STATE[:, :, :], STATE[:, :, :],
                                KEEP[:, i:i + 1] if isinstance(i, int)
                                else KEEP[:, bass.ds(i, 1)], None, ALU.mult
                                ).then_inc(kept, 1)
                v.wait_ge(kept, i + 1)

                def before(c):
                    bank, done = take(v, i, "F2", c)
                    if c == 0:
                        v.wait_ge(xnb_ready, i + 1)
                    V.tensor_tensor(U[:, c, :], bank[:, 0:D], XNB[:, c, :], ALU.add
                                    ).then_inc(done, 1)
                    v.wait_ge(decay_done, i * GT + c + 1)
                    v.wait_ge(g_ready, i * GT + c + 1)
                    if c >= 2:
                        v.wait_ge(y_ready, i * GT + c - 1)
                    V.tensor_tensor(
                        W[c % 2][:, :, :].rearrange("p (m q) t -> p m q t", q=2),
                        EDEC[:, :, :].rearrange("p (m q) t -> p m q t", q=2),
                        PG[:, :].rearrange("p (q m t) -> p m q t", q=2, t=P), ALU.mult
                    ).then_inc(w_done, 1)

                def carry(c):
                    cs = slice(c * HEADS, (c + 1) * HEADS)
                    v.wait_ge(exps_ready, i + 1)
                    v.wait_ge(y_ready, i * GT + c + 1)
                    v.wait_ge(xskip_done, i * GT + c + 1)
                    V.tensor_tensor(Y1[:, :], PY[:, :], XSKIP[c % 2][:, :], ALU.add
                                    ).then_inc(y_used, 1)
                    link(V.tensor_tensor(
                        STATE[:, :, :], STATE[:, :, :], EXPS[:, 1, cs].unsqueeze(2)
                        .to_broadcast([P, HEADS, HEADDIM]), ALU.mult))
                    for q, r in enumerate(HALF):
                        st = STATE[r, :, :].rearrange("p (m q) d -> p q m d", q=2)[:, q]
                        ps = PST[r, :].rearrange("p (m q d) -> p q m d", q=2, d=HEADDIM)[:, q]
                        ins = V.tensor_tensor(st, st, ps, ALU.add)
                    ins.then_inc(s_done, 1)
                    v.wait_ge(y_used, i * GT + c + 1)
                    read(v, i, "Z", c)
                    wait(v, ssq_done, i * GT + c)
                    if c:
                        v.wait_ge(pp_full, i * UNITS + seat[("GT", c - 1)] + 1)
                    V.tensor_tensor(G1[:, :], Y1[:, :], ZS[:, c, :], ALU.mult
                                    ).then_inc(g1_ready, 1)
                    v.wait_ge(s_done, i * GT + c + 1)

                def projected(c):
                    v.wait_ge(rms_done, i * GT + c + 1)
                    read(v, i, "F2", c)
                    bank, done = take(v, i, "O", c)
                    V.scalar_tensor_tensor(
                        out=U[:, c, :], in0=bank[:, 0:D], scalar=RMS[:, c:c + 1],
                        in1=U[:, c, :], op0=ALU.mult, op1=ALU.add).then_inc(done, 1)

                before(0)
                before(1)
                carry(0)
                if not last:
                    norm_x(i + 1)
                before(2)
                carry(1)
                projected(0)
                if not last:
                    norm_h(i + 1)
                before(3)
                carry(2)
                projected(1)
                if not last:
                    write_h(i + 1)
                carry(3)
                projected(2)
                projected(3)
                take(v, i, "PAD", 0)
                V.memset(PAUSE[:, :], 0.0).then_inc(pp_read[seat[("PAD", 0)] % 2], 1)
                moments_u(i)
                assert link.n[0] == VEC, link.n[0]

            V.memset(MHALF[:, :], -0.5).then_inc(prep, 1)
            V.memset(EPSC[:, :], EPS).then_inc(prep, 1)
            V.memset(STATE[:, :, :], 0.0).then_inc(prep, 1)
            norm_x(0)
            V.memset(ONES[:, :], 1.0).then_inc(prep, 1)
            V.memset(ZERO[:, :], 0.0).then_inc(prep, 1)
            norm_h(0)
            V.memset(LT[:, :].bitcast(F32), 0.0).then_inc(prep, 1)
            write_h(0)
            V.memset(BT[:, :, :, :], 0.0).then_inc(prep, 1)
            V.memset(SEL[64:, :, :].bitcast(F32), 0.0).then_inc(prep, 1)
            V.memset(SEL2[64:, :, :].bitcast(F32), 0.0).then_inc(prep, 1)
            v.wait_ge(act_prep, 1)
            V.tensor_scalar(NEGA[:, :], AH[:, :], -1.0, None, ALU.mult).then_inc(prep, 1)
            v.wait_ge(c_rest, C_REST)
            V.tensor_copy(MASKB[:, :], MASKF[:, :]).then_inc(prep, 1)
            V.tensor_copy(IDENTB[:, :], IDENT[:, :]).then_inc(prep, 1)
            V.tensor_copy(SEL[0:64, :, :].rearrange("p a b -> p (a b)"),
                          A1[0:64, :, :].rearrange("p a b -> p (a b)")).then_inc(prep, 1)
            V.tensor_copy(SEL2[0:64, :, :].rearrange("p a b -> p (a b)"),
                          ZS[0:64, :, :].rearrange("p a b -> p (a b)")).then_inc(prep, 1)
            for k in range(Z_TILES):
                V.tensor_scalar(WOUT[:, k, :], WOUT[:, k, :], NORMW[:, k:k + 1], None,
                                ALU.mult).then_inc(prep, 1)
            v.wait_ge(prep, PREPARED)
            body(0, True, False)
            with v.Fori(1, GROUPS - 1) as i:
                body(i, False, False)
            body(GROUPS - 1, False, True)
            norm_u(GROUPS - 1)
            v.wait_ge(un_ready, GROUPS * GT)

        @block.gpsimd
        def _(g):
            G = nc.gpsimd

            def inverse_std(n, chain, count, done):
                G.tensor_tensor(VE[:, :], MV[n][:, :, 1], EPSC[:, :], ALU.add).then_inc(chain, 1)
                g.wait_ge(chain, count)
                G.tensor_tensor(RSTD[n][:, :], VE[:, :], MHALF[:, :], ALU.pow).then_inc(done, 1)
                g.wait_ge(done, count)

            def input_std(j, n):
                g.wait_ge(stats, (j * 2 + n + 1) * GT)
                inverse_std(n, ln_gps, j * 2 + n + 1, rstd)

            def add_x(j):
                x = (lambda c: X[:, j, c, :])
                for c in range(GT):
                    g.wait_ge(un_ready, j * GT + c + 1)
                    G.tensor_tensor(x(c), x(c), UN[:, c, :], ALU.add).then_inc(x_done, 1)

            def body(i, first, last):
                if not first:
                    g.wait_ge(u_stats, i * GT)
                    inverse_std(2, un_gps, i, u_rstd)
                g.wait_ge(xn_ready, i * GT + GT)
                if not first:
                    read(g, i - 1, "F2", GT - 1)
                G.tensor_tensor(XNB[:, :, :], XN[:, :, :],
                                BF2[:, :].unsqueeze(1).to_broadcast([P, GT, D]), ALU.add
                                ).then_inc(xnb_ready, 1)
                if not first:
                    add_x(i - 1)
                g.wait_ge(da_ready, i + 1)
                g.wait_ge(cat_ready, i + 1)

                def by_dt(out, c, weight, done):
                    for r in range(KV):
                        ins = G.tensor_tensor(
                            out[:, r * REP:(r + 1) * REP, :],
                            XB[:, c, r * HEADDIM:(r + 1) * HEADDIM].unsqueeze(1)
                            .to_broadcast([P, REP, HEADDIM]),
                            weight[:, r * REP:(r + 1) * REP].unsqueeze(2)
                            .to_broadcast([P, REP, HEADDIM]), ALU.mult)
                    ins.then_inc(done, 1)

                def operands(c):
                    cs = slice(c * HEADS, (c + 1) * HEADS)
                    if c >= 2:
                        g.wait_ge(y_ready, i * GT + c - 1)
                    by_dt(XDT[c % 2], c, DT[:, c, :], xdt_done)
                    g.wait_ge(xdt_done, i * GT + c + 1)
                    g.wait_ge(exps_ready, i + 1)
                    G.tensor_tensor(XEND[c % 2][:, :, :], XDT[c % 2][:, :, :],
                                    EXPS[:, 2, cs].unsqueeze(2)
                                    .to_broadcast([P, HEADS, HEADDIM]), ALU.mult
                                    ).then_inc(xend_done, 1)
                    read(g, i, "E", c)
                    G.tensor_tensor(CTS[c % 2][:, :, :], CT[:, :, c * P:(c + 1) * P],
                                    ECT[:, :, :], ALU.mult).then_inc(cts_done, 1)

                def skip(c):
                    if c >= 2:
                        g.wait_ge(y_used, i * GT + c - 1)
                    by_dt(XSKIP[c % 2][:, :].rearrange("p (h d) -> p h d", d=HEADDIM), c,
                          DSK[:, :], xskip_done)

                def inverse_rms(c):
                    g.wait_ge(ssq_done, i * GT + c + 1)
                    G.tensor_tensor(RMSV[:, :], SSQ[:, c:c + 1], EPSC[:, 0:1], ALU.add
                                    ).then_inc(rms_gps, 1)
                    g.wait_ge(rms_gps, i * GT + c + 1)
                    G.tensor_tensor(RMS[:, c:c + 1], RMSV[:, :], MHALF[:, 0:1], ALU.pow
                                    ).then_inc(rms_done, 1)
                    g.wait_ge(rms_done, i * GT + c + 1)

                operands(0)
                skip(0)
                operands(1)
                skip(1)
                if not last:
                    input_std(i + 1, 0)
                operands(2)
                inverse_rms(0)
                skip(2)
                if not last:
                    input_std(i + 1, 1)
                operands(3)
                inverse_rms(1)
                skip(3)
                inverse_rms(2)
                inverse_rms(3)

            g.wait_ge(prep, 2)
            input_std(0, 0)
            input_std(0, 1)
            g.wait_ge(prep, PREPARED)
            g.wait_ge(c_rest, C_REST)
            body(0, True, False)
            with g.Fori(1, GROUPS - 1) as i:
                body(i, False, False)
            body(GROUPS - 1, False, True)
            g.wait_ge(u_stats, GROUPS * GT)
            inverse_std(2, un_gps, GROUPS, u_rstd)
            add_x(GROUPS - 1)
            g.wait_ge(x_done, GROUPS * GT)

        @block.scalar
        def _(a):
            A = nc.scalar
            a.wait_ge(c_first, C_FIRST)
            A.activation(AH[:, :], AH[:, :], ACT.Exp).then_inc(act_prep, 1)
            with a.Fori(0, GROUPS) as i:
                link = chain_of(a, scal, i * 2)
                for k in range(KD):
                    bank, done = take(a, i, "T", k)
                    A.activation(HT[:, k, :], bank[:, :], ACT.Identity, bias=LNB[:, k:k + 1],
                                 scale=LNW[:, k:k + 1]).then_inc(done, 1)
                a.wait_ge(prep, PREPARED)
                bank, done = take(a, i, "B", 1)
                for q, r in enumerate(HALF):
                    ins = A.activation(BT[r, 1, q, :], bank[r, :], ACT.Copy)
                ins.then_inc(done, 1)
                for m in (1, 3):
                    bank, done = take(a, i, "C", m)
                    A.activation(CT[:, m, :], bank[:, :], ACT.Copy).then_inc(done, 1)
                a.wait_ge(dt_in, i + 1)
                link(A.activation(DTE[:, :, :], DTR[:, :, :], ACT.Abs))
                link(A.activation(DTE[:, :, :], DTE[:, :, :], ACT.Exp, scale=-1.0))
                A.activation(DTL[:, :, :], DTE[:, :, :], ACT.Ln, bias=1.0).then_inc(dt_log, 1)
                for c in range(GT):
                    bank, done = take(a, i, "Z", c)
                    A.activation(ZS[:, c, :], bank[:, :], ACT.Silu).then_inc(done, 1)
                for m in range(FC1_TILES):
                    bank, done = take(a, i, "F1", m)
                    A.activation(A1[:, m, :], bank[:, :], ACT.Gelu_apprx_tanh,
                                 bias=BF1[:, m:m + 1]).then_inc(done, 1)
                a.wait_ge(cat_ready, i + 1)
                A.activation(EXPS[:, :, :], CAT[:, :, :], ACT.Exp).then_inc(exps_ready, 1)

                def decays(c):
                    a.wait_ge(lb_ready, i * GT + c + 1)
                    wait(a, w_done, i * GT + c)
                    for h in range(HEADS):
                        n = c * HEADS + h
                        ins = A.activation(EDEC[:, h, :], PL[:, h * P:(h + 1) * P], ACT.Exp,
                                           bias=NEGL[:, n:n + 1])
                    ins.then_inc(decay_done, 1)
                    bank, done = take(a, i, "E", c)
                    wait(a, cts_done, i * GT + c)
                    A.activation(ECT[:, :, :].rearrange("p m t -> p (m t)"), bank[:, :], ACT.Exp
                                 ).then_inc(done, 1)

                def square_and_turn(c):
                    a.wait_ge(g1_ready, i * GT + c + 1)
                    wait(a, ssq_done, i * GT + c)
                    if c:
                        a.wait_ge(rms_done, i * GT + c)
                    A.activation(SQ[:, :], G1[:, :], ACT.Square, scale=D_INNER ** -0.5,
                                 accum_out=SSQ[:, c:c + 1]).then_inc(ssq_done, 1)
                    bank, done = take(a, i, "GT", c)
                    A.activation(G1T[:, :, :].rearrange("p m t -> p (m t)"), bank[:, :], ACT.Copy
                                 ).then_inc(done, 1)

                decays(0)
                decays(1)
                decays(2)
                square_and_turn(0)
                decays(3)
                square_and_turn(1)
                square_and_turn(2)
                square_and_turn(3)
            a.wait_ge(ssq_done, GROUPS * GT)
            read(a, GROUPS - 1, "GT", GT - 1)

        @block.tensor
        def _(pe):
            T = nc.tensor
            pe.wait_ge(c_first, C_FIRST)
            with pe.Fori(0, GROUPS) as i:
                order = [0]

                def put(*name):
                    u = seat[name]
                    assert u == order[0], (name, u, order[0])
                    order[0] += 1
                    pe.wait_ge(pp_read[u % 2], i * (UNITS // 2) + u // 2)
                    return PP[u % 2]

                def wide(name, lhsT_of, rhs_of, ks, cols):
                    out = put(*name)
                    for k in range(ks):
                        ins = T.matmul(out[:, 0:cols], lhsT_of(k), rhs_of(k), start=(k == 0),
                                       stop=(k == ks - 1))
                    ins.then_inc(pp_full, 1)

                def before(c):
                    t = slice(c * P, (c + 1) * P)
                    wait(pe, decay_done, i * GT + c)
                    for half in range(2):
                        bank = PL[:, half * GROUP:(half + 1) * GROUP]
                        for n in range(GT):
                            h = half * GT + n
                            T.matmul(bank[:, n * P:(n + 1) * P], SEL[:, c * HEADS + h, :],
                                     LT[:, :], start=(n == 0), stop=False,
                                     skip_group_check=True)
                        ins = T.matmul(bank, IDENTB[:, :], MASKB[:, :], start=False, stop=True,
                                       skip_group_check=True)
                    ins.then_inc(lb_ready, 1)
                    out = put("E", c)
                    for m in range(HEADS // 2):
                        ins = T.matmul(out[:, m * P:(m + 1) * P],
                                       SEL2[:, c * HEADS // 2 + m, :], LT[:, :], start=True,
                                       stop=True)
                    ins.then_inc(pp_full, 1)
                    if c == 0:
                        read(pe, i, "F1", FC1_TILES - 2)
                        read(pe, i, "F1", FC1_TILES - 1)
                    wide(("F2", c), lambda m: A1[:, m, t], lambda m: WF2[:, m, :], FC1_TILES, D)
                    wait(pe, w_done, i * GT + c)
                    for q in range(2):
                        for k in range(KV):
                            at = q * GROUP + k * 2 * P
                            ins = T.matmul(PG[:, at:at + 2 * P], BT[:, k, q, t],
                                           CT[:, 2 * k:2 * k + 2, t], start=True, stop=True)
                    ins.then_inc(g_ready, 1)

                def outputs(c):
                    pe.wait_ge(xend_done, i * GT + c + 1)
                    wait(pe, s_done, i * GT + c)
                    for k in range(KV):
                        T.matmul(PST[:, k * 2 * P:(k + 1) * 2 * P],
                                 XB[:, c, D_XB + k * P:D_XB + (k + 1) * P],
                                 XEND[c % 2][:, k * REP:(k + 1) * REP, :]
                                 .rearrange("p h d -> p (h d)"), start=True, stop=True)
                    pe.wait_ge(w_done, i * GT + c + 1)
                    pe.wait_ge(cts_done, i * GT + c + 1)
                    wait(pe, y_used, i * GT + c)
                    if c == 0:
                        pe.wait_ge(kept, i + 1)
                    for h in range(HEADS):
                        y = PY[:, h * HEADDIM:(h + 1) * HEADDIM]
                        T.matmul(y, W[c % 2][:, h, :], XDT[c % 2][:, h, :], start=True,
                                 stop=False)
                        ins = T.matmul(y, CTS[c % 2][:, h // 2, :], STATE[:, h, :],
                                       start=False, stop=True)
                    ins.then_inc(y_ready, 1)

                def turn(c):
                    pe.wait_ge(g1_ready, i * GT + c + 1)
                    out = put("GT", c)
                    for m in range(Z_TILES):
                        ins = T.transpose(out[:, m * P:(m + 1) * P], G1[:, m * P:(m + 1) * P],
                                          IDENT[:, :])
                    ins.then_inc(pp_full, 1)

                def project(c):
                    read(pe, i, "GT", c)
                    wide(("O", c), lambda m: G1T[:, m, :], lambda m: WOUT[:, m, :], Z_TILES, D)

                for k in range(KD):
                    out = put("T", k)
                    for c in range(GT):
                        pe.wait_ge(h_ready, i * GT + c + 1)
                        ins = T.transpose(out[:, c * P:(c + 1) * P], H[:, c, k * P:(k + 1) * P],
                                          IDENT[:, :])
                    ins.then_inc(pp_full, 1)
                read(pe, i, "T", 0)
                read(pe, i, "T", 1)
                for name, col in ([(("B", k), CB + k * P) for k in range(KV)] +
                                  [(("C", m), CC + m * P) for m in range(HEADS // 2)]):
                    wide(name, lambda k: WIN[:, k, col:col + P], lambda k: HT[:, k, :], KD,
                         GROUP)
                for name, at, cols in ([(("X", c), CX, XBD) for c in range(GT)] +
                                       [(("Z", c), CZ, D_INNER) for c in range(GT)]):
                    c = name[1]
                    wide(name, lambda k: HT[:, k, c * P:(c + 1) * P],
                         lambda k: WIN[:, k, at:at + cols], KD, cols)
                pe.wait_ge(prep, PREPARED)
                pe.wait_ge(da_ready, i + 1)
                out = put("CUM", 0)
                T.matmul(out[:, 0:N32], TRI[:, :], DA[:, 0, :], start=True, stop=True)
                T.matmul(out[:, N32:2 * N32], ONES[:, :], DA[:, 0, :], start=True, stop=True)
                T.matmul(out[0:2 * N32, 2 * N32:2 * N32 + P],
                         DA[:, :, :].rearrange("p a n -> p (a n)"), TRI[:, :], start=True,
                         stop=True).then_inc(pp_full, 1)
                pe.wait_ge(c_rest, C_REST)
                for m in range(FC1_TILES):
                    wide(("F1", m), lambda k: WF1[:, k, m * P:(m + 1) * P],
                         lambda k: HT[:, k, :], KD, GROUP)
                pe.wait_ge(lt_ready, i + 1)
                before(0)
                before(1)
                outputs(0)
                before(2)
                turn(0)
                outputs(1)
                project(0)
                before(3)
                turn(1)
                outputs(2)
                project(1)
                turn(2)
                outputs(3)
                project(2)
                turn(3)
                project(3)
                T.transpose(put("PAD", 0)[:, 0:P], IDENT[:, :], IDENT[:, :]).then_inc(pp_full, 1)

EXPERTS, TOPK = 8, 2
ETILES = TOKENS * TOPK // P + EXPERTS
XS_TILES = ETILES + 8
BIG = 3.0e38


def route_stage(nc, X, XN, LOG, SHARED, w_router, ident_d, w_sgate, w_sdown, hs):
    with ExitStack() as ctx:
        s = Scope(nc, ctx, f"rt{hs}")
        sb, pb, sem = s.sb, s.pb, s.sem
        IDENT = sb("IDENT", [P, P])
        WR = sb("WR", [P, KD, EXPERTS])
        MHALF = sb("MHALF", [P, GT])
        STAT = sb("STAT", [P, GT, 6])
        MV = sb("MV", [P, GT, 2])
        VE = sb("VE", [P, GT])
        RSTD = sb("RSTD", [P, GT])
        EPSC = sb("EPSC", [P, GT])
        PAUSE = sb("PAUSE", [P, 1])
        H = sb("H", [P, GT, D])
        HT = sb("HT", [P, KD, GROUP])
        PP = [pb(f"PP{n}", [P, GROUP]) for n in range(2)]
        PR = pb("PR", [P, GT, EXPERTS])
        HSC = [min(P, hs - P * m) for m in range(-(-hs // P))]
        NS = len(HSC)
        if hs:
            WSG = sb("WSG", [P, KD, 2 * hs])
            WSD = sb("WSD", [P, NS, D])
            SG = [sb(f"SG{n}", [P, GROUP]) for n in range(2)]
            HS = sb("HS", [P, NS, GROUP])
            PY = [pb(f"PY{n}", [P, GROUP]) for n in range(2)]
            PGT = [pb(f"PGT{n}", [P, GROUP]) for n in range(2)]
        c_load = sem("c_load")
        prep = sem("prep")
        vec = sem("vec")
        gps = sem("gps")
        stats = sem("stats")
        rstd = sem("rstd")
        h_ready = sem("h_ready")
        pp_full = sem("pp_full")
        pp_read = [sem(f"pp_read{n}") for n in range(2)]
        r_full = sem("r_full")
        r_read = sem("r_read")
        xn_kept = sem("xn_kept")
        hid_full = sem("hid_full")
        sg_ready = sem("sg_ready")
        hs_ready = sem("hs_ready")
        UNITS = 6 if hs else 2
        LOADS = 16 * (2 + (1 + NS if hs else 0))
        block = ctx.enter_context(nc.Block())

        def read(eng, i, u):
            eng.wait_ge(pp_read[u % 2], i * (UNITS // 2) + u // 2 + 1)

        @block.sync
        def _(sp):
            sp.dma_start(IDENT[:, :], ident_d).then_inc(c_load, 16)
            sp.dma_start(WR[:, :, :], w_router.rearrange("(k p) n -> p k n", p=P)
                         ).then_inc(c_load, 16)
            if hs:
                sp.dma_start(WSG[:, :, :], w_sgate.rearrange("(k p) n -> p k n", p=P)
                             ).then_inc(c_load, 16)
                for m, rows in enumerate(HSC):
                    sp.dma_start(WSD[0:rows, m, :], w_sdown[m * P:m * P + rows, :]
                                 ).then_inc(c_load, 16)
            sp.wait_ge(c_load, LOADS)

        @block.vector
        def _(v):
            nc.vector.memset(MHALF[:, :], -0.5).then_inc(prep, 1)
            nc.vector.memset(EPSC[:, :], EPS).then_inc(prep, 1)
            VEC = GT + 1
            with v.Fori(0, GROUPS) as i:
                link = chain_of(v, vec, i * VEC)
                for c in range(GT):
                    link(nc.vector.bn_stats(STAT[:, c, :], X[:, i, c, :]), wait=False)
                v.wait_ge(vec, i * VEC + GT)
                link(nc.vector.memset(PAUSE[:, :], 0.0), wait=False)
                for c in range(GT):
                    nc.vector.bn_aggr(MV[:, c, :], STAT[:, c, :]).then_inc(stats, 1)
                v.wait_ge(rstd, i + 1)
                v.wait_ge(xn_kept, i)
                for c in range(GT):
                    nc.vector.tensor_scalar(H[:, c, :], X[:, i, c, :], MV[:, c, 0:1],
                                            RSTD[:, c:c + 1], ALU.subtract, ALU.mult
                                            ).then_inc(h_ready, 1)
                v.wait_ge(pp_full, i * UNITS + 1)
                nc.vector.tensor_copy(HT[:, 0, :], PP[0][:, :]).then_inc(pp_read[0], 1)
                v.wait_ge(r_full, i + 1)
                nc.vector.tensor_copy(LOG[:, i, :, :], PR[:, :, :]).then_inc(r_read, 1)
                for m in range(NS):
                    v.wait_ge(sg_ready, i * NS + m + 1)
                    nc.vector.tensor_tensor(HS[0:HSC[m], m, :], SG[m % 2][0:HSC[m], :],
                                            PY[m % 2][0:HSC[m], :], ALU.mult
                                            ).then_inc(hs_ready, 1)
                if hs:
                    for c in range(0, GT, 2):
                        v.wait_ge(pp_full, i * UNITS + 3 + c)
                        nc.vector.tensor_copy(SHARED[:, i, c, :], PP[0][:, 0:D]
                                              ).then_inc(pp_read[0], 1)
            v.wait_ge(r_read, GROUPS)
            read(v, GROUPS - 1, UNITS - 2)

        @block.gpsimd
        def _(g):
            g.wait_ge(prep, 2)
            with g.Fori(0, GROUPS) as i:
                g.wait_ge(stats, i * GT + GT)
                nc.gpsimd.tensor_tensor(VE[:, :], MV[:, :, 1], EPSC[:, :], ALU.add
                                        ).then_inc(gps, 1)
                g.wait_ge(gps, i + 1)
                nc.gpsimd.tensor_tensor(RSTD[:, :], VE[:, :], MHALF[:, :], ALU.pow
                                        ).then_inc(rstd, 1)
                g.wait_ge(h_ready, i * GT + GT)
                nc.gpsimd.tensor_copy(XN[:, i, :, :], H[:, :, :]).then_inc(xn_kept, 1)
            g.wait_ge(xn_kept, GROUPS)

        @block.scalar
        def _(a):
            with a.Fori(0, GROUPS) as i:
                a.wait_ge(pp_full, i * UNITS + 2)
                nc.scalar.activation(HT[:, 1, :], PP[1][:, :], ACT.Copy).then_inc(pp_read[1], 1)
                for m in range(NS):
                    a.wait_ge(hid_full, i * NS + m + 1)
                    if m >= 2:
                        a.wait_ge(hs_ready, i * NS + m - 1)
                    else:
                        a.wait_ge(hs_ready, i * NS)
                    nc.scalar.activation(SG[m % 2][0:HSC[m], :], PGT[m % 2][0:HSC[m], :], ACT.Silu
                                         ).then_inc(sg_ready, 1)
                if hs:
                    for c in range(1, GT, 2):
                        a.wait_ge(pp_full, i * UNITS + 3 + c)
                        nc.scalar.activation(SHARED[:, i, c, :], PP[1][:, 0:D], ACT.Copy
                                             ).then_inc(pp_read[1], 1)
            read(a, GROUPS - 1, UNITS - 1)

        @block.tensor
        def _(pe):
            pe.wait_ge(c_load, LOADS)
            with pe.Fori(0, GROUPS) as i:
                for k in range(KD):
                    pe.wait_ge(pp_read[k], i * (UNITS // 2))
                    for c in range(GT):
                        pe.wait_ge(h_ready, i * GT + c + 1)
                        ins = nc.tensor.transpose(PP[k][:, c * P:(c + 1) * P],
                                                  H[:, c, k * P:(k + 1) * P], IDENT[:, :])
                    ins.then_inc(pp_full, 1)
                read(pe, i, 0)
                read(pe, i, 1)
                pe.wait_ge(r_read, i)
                for c in range(GT):
                    for k in range(KD):
                        ins = nc.tensor.matmul(PR[:, c, :], HT[:, k, c * P:(c + 1) * P],
                                               WR[:, k, :], start=(k == 0), stop=(k == KD - 1))
                ins.then_inc(r_full, 1)
                for m in range(NS):
                    if m >= 2:
                        pe.wait_ge(hs_ready, i * NS + m - 1)
                    else:
                        pe.wait_ge(hs_ready, i * NS)
                    for bank, off in ((PY, 0), (PGT, hs)):
                        for k in range(KD):
                            at = off + m * P
                            ins = nc.tensor.matmul(bank[m % 2][0:HSC[m], :],
                                                   WSG[:, k, at:at + HSC[m]], HT[:, k, :],
                                                   start=(k == 0), stop=(k == KD - 1))
                    ins.then_inc(hid_full, 1)
                if hs:
                    pe.wait_ge(hs_ready, i * NS + NS)
                    for c in range(GT):
                        pe.wait_ge(pp_read[c % 2], i * (UNITS // 2) + 1 + c // 2)
                        for m in range(NS):
                            ins = nc.tensor.matmul(PP[c % 2][:, 0:D],
                                                   HS[0:HSC[m], m, c * P:(c + 1) * P],
                                                   WSD[0:HSC[m], m, :], start=(m == 0),
                                                   stop=(m == NS - 1))
                        ins.then_inc(pp_full, 1)


def dispatch_stage(nc, XN, LOG, POS, WT, EXP_OF, gate_bias, tri_d, rev_d, tile_d, step_d, xs, hs):
    sigmoid = hs > 0
    with ExitStack() as ctx:
        s = Scope(nc, ctx, f"dp{hs}")
        sb, pb, sem = s.sb, s.pb, s.sem
        TRI = sb("TRI", [P, P])
        ONES = sb("ONES", [P, P])
        REV = sb("REV", [P, EXPERTS])
        TIDX = sb("TIDX", [P, ETILES])
        STEP = sb("STEP", [P, TILES])
        GB = sb("GB", [P, EXPERTS])
        te = [P, TILES, EXPERTS]
        SC, SEL, EQ, T, POSF = (sb(n, te) for n in ("SC", "SEL", "EQ", "T", "POSF"))
        O = [sb(f"O{n}", te) for n in range(TOPK)]
        RUN = [sb(f"RUN{n}", te) for n in range(2)]
        M = sb("M", [P, TILES])
        R = sb("R", [P, TILES])
        PF = sb("PF", [P, TILES])
        WSUM = sb("WSUM", [P, TILES])
        CMP = sb("CMP", [P, EXPERTS, TILES])
        TE = sb("TE", [P, EXPERTS])
        CE = [sb(f"CE{n}", [P, EXPERTS]) for n in range(2)]
        BASE = sb("BASE", [P, EXPERTS])
        CMT = sb("CMT", [P, ETILES, EXPERTS - 1])
        EXF = sb("EXF", [P, ETILES])
        PC = pb("PC", [P, 2, TILES * EXPERTS])
        c_load = sem("c_load")
        vec = sem("vec")
        scores_in = sem("scores_in")
        scored = sem("scored")
        picked = sem("picked")
        counted = sem("counted")
        placed = sem("placed")
        scattered = sem("scattered")
        block = ctx.enter_context(nc.Block())
        flat = LOG[:, :, :, :].rearrange("p g c e -> p (g c) e")
        V = nc.vector

        def over_e(t):
            return t.unsqueeze(2).to_broadcast(te)

        def over_t(t):
            return t.unsqueeze(1).to_broadcast(te)

        @block.sync
        def _(sp):
            for dst, src in ((TRI, tri_d), (REV, rev_d), (TIDX, tile_d), (STEP, step_d),
                             (GB, gate_bias)):
                sp.dma_start(dst[:, :], src).then_inc(c_load, 16)
            sp.wait_ge(c_load, 80)

        @block.scalar
        def _(a):
            if sigmoid:
                nc.scalar.activation(SC[:, :, :], flat, ACT.Sigmoid).then_inc(scored, 1)
            else:
                a.wait_ge(scores_in, 1)
                nc.scalar.activation(SC[:, :, :], T[:, :, :], ACT.Exp).then_inc(scored, 1)

        @block.vector
        def _(v):
            link = chain_of(v, vec)
            link(V.memset(ONES[:, :], 1.0))
            v.wait_ge(c_load, 80)
            if sigmoid:
                v.wait_ge(scored, 1)
                link(V.tensor_tensor(SEL[:, :, :], SC[:, :, :], over_t(GB[:, :]), ALU.add))
            else:
                link(V.tensor_reduce(M[:, :], flat, AX.X, ALU.max))
                V.tensor_tensor(T[:, :, :], flat, over_e(M[:, :]), ALU.subtract
                                ).then_inc(scores_in, 1)
                v.wait_ge(scored, 1)
                link(V.tensor_reduce(M[:, :], SC[:, :, :], AX.X, ALU.add))
                link(V.reciprocal(R[:, :], M[:, :]))
                link(V.tensor_tensor(SC[:, :, :], SC[:, :, :], over_e(R[:, :]), ALU.mult))
                link(V.tensor_copy(SEL[:, :, :], SC[:, :, :]))
            for n in range(TOPK):
                link(V.tensor_reduce(M[:, :], SEL[:, :, :], AX.X, ALU.max))
                link(V.tensor_tensor(EQ[:, :, :], SEL[:, :, :], over_e(M[:, :]), ALU.is_equal))
                link(V.tensor_tensor(T[:, :, :], EQ[:, :, :], over_t(REV[:, :]), ALU.mult))
                link(V.tensor_reduce(R[:, :], T[:, :, :], AX.X, ALU.max))
                link(V.tensor_tensor(O[n][:, :, :], over_t(REV[:, :]), over_e(R[:, :]),
                                     ALU.is_equal))
                link(V.tensor_tensor(T[:, :, :], O[n][:, :, :], SC[:, :, :], ALU.mult))
                link(V.tensor_reduce(WT[:, n, :], T[:, :, :], AX.X, ALU.add))
                if n < TOPK - 1:
                    link(V.scalar_tensor_tensor(out=SEL[:, :, :], in0=O[n][:, :, :], scalar=-BIG,
                                                in1=SEL[:, :, :], op0=ALU.mult, op1=ALU.add))
            if sigmoid:
                link(V.tensor_tensor(WSUM[:, :], WT[:, 0, :], WT[:, 1, :], ALU.add))
                link(V.reciprocal(R[:, :], WSUM[:, :]))
                for n in range(TOPK):
                    link(V.tensor_tensor(WT[:, n, :], WT[:, n, :], R[:, :], ALU.mult))
            V.tensor_tensor(EQ[:, :, :], O[0][:, :, :], O[1][:, :, :], ALU.add
                            ).then_inc(picked, 1)
            v.wait_ge(counted, 1)
            total = PC[:, 1, :].rearrange("p (t e) -> p t e", e=EXPERTS)
            link(V.tensor_copy(RUN[0][:, :, :], total))
            src, d = 0, 1
            while d < TILES:
                link(V.tensor_copy(RUN[1 - src][:, 0:d, :], RUN[src][:, 0:d, :]))
                link(V.tensor_tensor(RUN[1 - src][:, d:, :], RUN[src][:, d:, :],
                                     RUN[src][:, 0:TILES - d, :], ALU.add))
                src, d = 1 - src, 2 * d
            run, other = RUN[src], RUN[1 - src]
            link(V.tensor_tensor(CMP[:, :, :],
                                 run[:, TILES - 1, :].unsqueeze(2)
                                 .to_broadcast([P, EXPERTS, TILES]),
                                 STEP[:, :].unsqueeze(1).to_broadcast([P, EXPERTS, TILES]),
                                 ALU.is_gt))
            link(V.tensor_reduce(TE[:, :], CMP[:, :, :], AX.X, ALU.add))
            link(V.tensor_copy(CE[0][:, :], TE[:, :]))
            ce, d = 0, 1
            while d < EXPERTS:
                link(V.tensor_copy(CE[1 - ce][:, 0:d], CE[ce][:, 0:d]))
                link(V.tensor_tensor(CE[1 - ce][:, d:], CE[ce][:, d:],
                                     CE[ce][:, 0:EXPERTS - d], ALU.add))
                ce, d = 1 - ce, 2 * d
            link(V.tensor_tensor(BASE[:, :], CE[ce][:, :], TE[:, :], ALU.subtract))
            link(V.tensor_scalar(BASE[:, :], BASE[:, :], float(P), -1.0, ALU.mult, ALU.add))
            link(V.tensor_tensor(other[:, :, :], run[:, :, :], total, ALU.subtract))
            link(V.tensor_tensor(POSF[:, :, :], other[:, :, :],
                                 PC[:, 0, :].rearrange("p (t e) -> p t e", e=EXPERTS), ALU.add))
            link(V.tensor_tensor(POSF[:, :, :], POSF[:, :, :], over_t(BASE[:, :]), ALU.add))
            for n in range(TOPK):
                link(V.tensor_tensor(T[:, :, :], POSF[:, :, :], O[n][:, :, :], ALU.mult))
                link(V.tensor_reduce(PF[:, :], T[:, :, :], AX.X, ALU.add))
                V.tensor_copy(POS[:, n, :], PF[:, :]).then_inc(placed, 1)
            shape = [P, ETILES, EXPERTS - 1]
            link(V.tensor_tensor(CMT[:, :, :], TIDX[:, :].unsqueeze(2).to_broadcast(shape),
                                 CE[ce][:, 0:EXPERTS - 1].unsqueeze(1).to_broadcast(shape),
                                 ALU.is_ge))
            link(V.tensor_reduce(EXF[:, :], CMT[:, :, :], AX.X, ALU.add))
            link(V.memset(EXP_OF[:, :], 0))
            link(V.tensor_copy(EXP_OF[:, 0:ETILES], EXF[:, :]))

        @block.tensor
        def _(pe):
            pe.wait_ge(picked, 1)
            picks = EQ[:, :, :].rearrange("p t e -> p (t e)")
            nc.tensor.matmul(PC[:, 0, :], TRI[:, :], picks, start=True, stop=True)
            nc.tensor.matmul(PC[:, 1, :], ONES[:, :], picks, start=True, stop=True
                             ).then_inc(counted, 1)

        @block.gpsimd
        def _(g):
            for n in range(TOPK):
                g.wait_ge(placed, n + 1)
                for t in range(TILES):
                    g.indirect_dma_start(
                        out=xs, out_offset=bass.IndirectOffsetOnAxis(ap=POS[:, n, t:t + 1], axis=0),
                        in_=XN[:, t // GT, t % GT, :], in_offset=None).then_inc(scattered, 16)
            g.wait_ge(scattered, 16 * TOPK * TILES)


def expert_stage(nc, EXP_OF, xs, ys, w_up, w_down, ident_d, hid):
    with ExitStack() as ctx:
        s = Scope(nc, ctx, f"ex{hid}")
        sb, pb, sem = s.sb, s.pb, s.sem
        HC = hid // P if hid % P == 0 else 2
        HP = hid // HC
        IDENT = sb("IDENT", [P, P])
        WU = sb("WU", [P, EXPERTS, KD, 2 * hid])
        WD = sb("WD", [P, EXPERTS, HC, D])
        XG = [sb(f"XG{n}", [P, D]) for n in range(2)]
        XT = [sb(f"XT{n}", [P, KD, P]) for n in range(2)]
        SG = [sb(f"SG{n}", [P, hid]) for n in range(2)]
        HH = [sb(f"HH{n}", [P, hid]) for n in range(2)]
        HT = [sb(f"HT{n}", [P, HC, P]) for n in range(2)]
        YO = [sb(f"YO{n}", [P, D]) for n in range(2)]
        PX = pb("PX", [P, GROUP])
        PGA = [pb(f"PGA{n}", [P, GROUP]) for n in range(2)]
        PUP = [pb(f"PUP{n}", [P, GROUP]) for n in range(2)]
        PH = pb("PH", [P, GROUP])
        PY = [pb(f"PY{n}", [P, GROUP]) for n in range(2)]
        c_load = sem("c_load")
        w_load = sem("w_load")
        x_load = [sem(f"x_load{n}") for n in range(2)]
        xt_full = sem("xt_full")
        xt_read = sem("xt_read")
        gate_full = sem("gate_full")
        up_full = sem("up_full")
        sg_ready = sem("sg_ready")
        hh_ready = sem("hh_ready")
        ht_full = sem("ht_full")
        ht_read = sem("ht_read")
        y_full = sem("y_full")
        y_read = sem("y_read")
        stored = [sem(f"stored{n}") for n in range(2)]
        block = ctx.enter_context(nc.Block())
        PAIRS = ETILES // 2

        @block.sync
        def _(sp):
            sp.dma_start(IDENT[:, :], ident_d).then_inc(c_load, 16)

            def load(t, n):
                sp.dma_start(XG[n][:, :], xs[t]).then_inc(x_load[n], 16)
            load(0, 0)
            load(1, 1)
            for e in range(EXPERTS):
                sp.dma_start(WU[:, e, :, :], w_up[e].rearrange("(k p) n -> p k n", p=P)
                             ).then_inc(w_load, 16)
                sp.dma_start(WD[0:HP, e, :, :], w_down[e].rearrange("(k p) n -> p k n", p=HP)
                             ).then_inc(w_load, 16)
            with sp.Fori(0, PAIRS) as i:
                for n in range(2):
                    sp.wait_ge(xt_full, i * 2 + n + 1)
                    load(i * 2 + n + 2, n)
            sp.wait_ge(x_load[0], 16 * (PAIRS + 1))
            sp.wait_ge(x_load[1], 16 * (PAIRS + 1))
            sp.wait_ge(w_load, 32 * EXPERTS)
            sp.wait_ge(c_load, 16)

        @block.gpsimd
        def _(g):
            with g.Fori(0, PAIRS) as i:
                for n in range(2):
                    g.wait_ge(y_read, i * 2 + n + 1)
                    g.dma_start(ys[i * 2 + n], YO[n][:, :]).then_inc(stored[n], 16)
            g.wait_ge(stored[0], 16 * PAIRS)
            g.wait_ge(stored[1], 16 * PAIRS)

        @block.scalar
        def _(a):
            with a.Fori(0, PAIRS) as i:
                for n in range(2):
                    t = i * 2 + n
                    a.wait_ge(gate_full, t + 1)
                    a.wait_ge(sg_ready, t)
                    nc.scalar.activation(SG[n][:, :], PGA[n][:, 0:hid], ACT.Silu
                                         ).then_inc(sg_ready, 1)
                    a.wait_ge(ht_full, t + 1)
                    nc.scalar.activation(HT[n][0:HP, :, :].rearrange("p c t -> p (c t)"),
                                         PH[0:HP, 0:HC * P], ACT.Copy).then_inc(ht_read, 1)

        @block.vector
        def _(v):
            def turned(t, n):
                v.wait_ge(xt_full, t + 1)
                nc.vector.tensor_copy(XT[n][:, :, :].rearrange("p k t -> p (k t)"), PX[:, 0:D]
                                      ).then_inc(xt_read, 1)
            turned(0, 0)
            turned(1, 1)
            with v.Fori(0, PAIRS) as i:
                for n in range(2):
                    t = i * 2 + n
                    v.wait_ge(sg_ready, t + 1)
                    v.wait_ge(up_full, t + 1)
                    nc.vector.tensor_tensor(HH[n][:, :], SG[n][:, :], PUP[n][:, 0:hid], ALU.mult
                                            ).then_inc(hh_ready, 1)
                    turned(t + 2, n)
                    v.wait_ge(y_full, t + 1)
                    v.wait_ge(stored[n], i * 16)
                    nc.vector.tensor_copy(YO[n][:, :], PY[n][:, 0:D]).then_inc(y_read, 1)

        @block.tensor
        def _(pe):
            def turn(t, n, loads):
                pe.wait_ge(x_load[n], loads * 16)
                pe.wait_ge(xt_read, t)
                for k in range(KD):
                    ins = nc.tensor.transpose(PX[:, k * P:(k + 1) * P],
                                              XG[n][:, k * P:(k + 1) * P], IDENT[:, :])
                ins.then_inc(xt_full, 1)

            def project(n, bank, e, at, full):
                for k in range(KD):
                    ins = nc.tensor.matmul(bank[n][:, 0:hid], XT[n][:, k, :],
                                           WU[:, e, k, at:at + hid], start=(k == 0),
                                           stop=(k == KD - 1))
                ins.then_inc(full, 1)

            def expert(t):
                return pe.value_load(EXP_OF[0:1, bass.ds(t, 1)], min_val=0, max_val=EXPERTS - 1)

            pe.wait_ge(c_load, 16)
            turn(0, 0, 1)
            pe.wait_ge(w_load, 32 * EXPERTS)
            first = pe.value_load(EXP_OF[0:1, 0:1], min_val=0, max_val=EXPERTS - 1)
            pe.wait_ge(xt_read, 1)
            project(0, PGA, first, 0, gate_full)
            project(0, PUP, first, hid, up_full)
            turn(1, 1, 1)
            with pe.Fori(0, PAIRS) as i:
                for n in range(2):
                    t = i * 2 + n
                    m = 1 - n
                    here = expert(t)
                    ahead = expert(t + 1)
                    pe.wait_ge(xt_read, t + 2)
                    pe.wait_ge(sg_ready, t)
                    project(m, PGA, ahead, 0, gate_full)
                    pe.wait_ge(hh_ready, t + 1)
                    pe.wait_ge(ht_read, t)
                    for c in range(HC):
                        ins = nc.tensor.transpose(PH[0:HP, c * P:(c + 1) * P],
                                                  HH[n][:, c * HP:(c + 1) * HP], IDENT[:, :])
                    ins.then_inc(ht_full, 1)
                    project(m, PUP, ahead, hid, up_full)
                    turn(t + 2, n, i + 2)
                    pe.wait_ge(ht_read, t + 1)
                    if n:
                        pe.wait_ge(y_read, i * 2)
                    else:
                        pe.wait_ge(y_read, i * 2)
                    for c in range(HC):
                        ins = nc.tensor.matmul(PY[n][:, 0:D], HT[n][0:HP, c, :],
                                               WD[0:HP, here, c, :], start=(c == 0),
                                               stop=(c == HC - 1))
                    ins.then_inc(y_full, 1)


def combine_stage(nc, X, POS, WT, SHARED, ys, out, hs):
    with ExitStack() as ctx:
        s = Scope(nc, ctx, f"cb{hs}")
        sb, sem = s.sb, s.sem
        GY = [[sb(f"GY{c}_{n}", [P, D]) for n in range(TOPK)] for c in range(GT)]
        MHALF = sb("MHALF", [P, GT])
        STAT = sb("STAT", [P, GT, 6])
        MV = sb("MV", [P, GT, 2])
        VE = sb("VE", [P, GT])
        RSTD = sb("RSTD", [P, GT])
        EPSC = sb("EPSC", [P, GT])
        PAUSE = sb("PAUSE", [P, 1])
        U = sb("U", [P, GT, D])
        UN = sb("UN", [P, GT, D])
        gathered = [sem(f"gathered{c}") for c in range(GT)]
        used = sem("used")
        prep = sem("prep")
        vec = sem("vec")
        act = sem("act")
        sqrt_done = sem("sqrt_done")
        stats = sem("stats")
        x_done = sem("x_done")
        stored = sem("stored")
        block = ctx.enter_context(nc.Block())

        @block.gpsimd
        def _(g):
            for t in range(TILES):
                c = t % GT
                if t >= GT:
                    g.wait_ge(used, t - GT + 1)
                for n in range(TOPK):
                    g.indirect_dma_start(
                        out=GY[c][n][:, :], out_offset=None, in_=ys,
                        in_offset=bass.IndirectOffsetOnAxis(ap=POS[:, n, t:t + 1], axis=0)
                    ).then_inc(gathered[c], 16)

        @block.vector
        def _(v):
            V = nc.vector
            PER = GT * (3 if hs else 2) + 3 + GT
            with v.Fori(0, GROUPS) as i:
                link = chain_of(v, vec, i * PER)
                for c in range(GT):
                    v.wait_ge(gathered[c], (i + 1) * 16 * TOPK)
                    link(V.tensor_scalar(U[:, c, :], GY[c][0][:, :], WT[:, 0, bass.ds(i * GT + c, 1)],
                                         None, ALU.mult))
                    ins = V.scalar_tensor_tensor(
                        out=U[:, c, :], in0=GY[c][1][:, :], scalar=WT[:, 1, bass.ds(i * GT + c, 1)],
                        in1=U[:, c, :], op0=ALU.mult, op1=ALU.add)
                    ins.then_inc(used, 1)
                    v.wait_ge(used, i * GT + c + 1)
                    if hs:
                        link(V.tensor_tensor(U[:, c, :], U[:, c, :], SHARED[:, i, c, :], ALU.add))
                    link(V.bn_stats(STAT[:, c, :], U[:, c, :]))
                link(V.memset(PAUSE[:, :], 0.0), wait=False)
                for c in range(GT):
                    ins = V.bn_aggr(MV[:, c, :], STAT[:, c, :])
                link(ins)
                V.tensor_scalar(VE[:, :], MV[:, :, 1], EPS, None, ALU.add).then_inc(stats, 1)
                v.wait_ge(sqrt_done, i + 1)
                link(V.reciprocal(RSTD[:, :], RSTD[:, :]))
                for c in range(GT):
                    link(V.tensor_scalar(UN[:, c, :], U[:, c, :], MV[:, c, 0:1], RSTD[:, c:c + 1],
                                         ALU.subtract, ALU.mult))
                V.tensor_tensor(X[:, i, :, :], X[:, i, :, :], UN[:, :, :], ALU.add
                                ).then_inc(x_done, 1)
                assert link.n[0] == PER
            v.wait_ge(x_done, GROUPS)

        @block.scalar
        def _(a):
            with a.Fori(0, GROUPS) as i:
                a.wait_ge(stats, i + 1)
                nc.scalar.activation(RSTD[:, :], VE[:, :], ACT.Sqrt).then_inc(sqrt_done, 1)

        if out is not None:
            @block.sync
            def _(sp):
                with sp.Fori(0, GROUPS) as i:
                    sp.wait_ge(x_done, i + 1)
                    sp.dma_start(out[i], X[:, i, :, :]).then_inc(stored, 16)
                sp.wait_ge(stored, 16 * GROUPS)


def moe_layer(nc, X, xs, ys, w_router, gate_bias, w_up, w_down, w_sgate, w_sdown, hs, hid,
              consts, out):
    xs_tiles = xs.rearrange("(t p) d -> t p d", p=P)
    ys_tiles = ys.rearrange("(t p) d -> t p d", p=P)
    tag = f"moe{hs}_"
    with ExitStack() as ctx:
        def keep(name, shape, dt=F32):
            return ctx.enter_context(nc.sbuf_tensor(tag + name, shape, dt))
        POS = keep("POS", [P, TOPK, TILES], U32)
        WT = keep("WT", [P, TOPK, TILES])
        EXP_OF = keep("EXP_OF", [P, XS_TILES], I32)
        SHARED = keep("SHARED", [P, GROUPS, GT, D]) if hs else None
        with nc.sbuf_tensor(tag + "XN", [P, GROUPS, GT, D], F32) as XN, \
                nc.sbuf_tensor(tag + "LOG", [P, GROUPS, GT, EXPERTS], F32) as LOG:
            route_stage(nc, X, XN, LOG, SHARED, w_router, consts["ident"], w_sgate, w_sdown, hs)
            dispatch_stage(nc, XN, LOG, POS, WT, EXP_OF, gate_bias, consts["tri"], consts["rev"],
                           consts["tidx"], consts["step"], xs, hs)
        expert_stage(nc, EXP_OF, xs_tiles, ys_tiles, w_up, w_down, consts["ident"], hid)
        combine_stage(nc, X, POS, WT, SHARED, ys, out, hs)

AH_HEADS, AH_DIM = 16, 16
SCALE = float(D) ** -0.5
AT = SEQ // P
HALVES = SEQ // GROUP
PAIRED = AH_HEADS // 2
QUADS = AH_HEADS // 4
VW = AH_DIM + 1
SHIFT_ROW = 32
MW = 64 + SHIFT_ROW + 1


def attention_stage(nc, X, wq, bq, wk, bk, wv, bv, wo, bo, ident_d, stack_d, one_row_d):
    with ExitStack() as ctx:
        s = Scope(nc, ctx, "at")
        sb, pb, sem = s.sb, s.pb, s.sem
        IDENT = sb("IDENT", [P, P])
        IDENTR = sb("IDENTR", [P, P], F32R)
        WQ = sb("WQ", [P, KD, D])
        WK = sb("WK", [P, KD, D])
        WV = sb("WV", [P, KD, AH_HEADS * VW])
        WO = sb("WO", [P, KD, D])
        BQ = sb("BQ", [P, KD])
        BK = sb("BK", [P, KD])
        BV = sb("BV", [P, AH_HEADS * VW])
        BO = sb("BO", [P, D])
        STACK = sb("STACK", [P, 4, 4, P], F32R)
        ONE_ROW = sb("ONE_ROW", [P, 1])
        MHALF = sb("MHALF", [P, GT])
        STAT = sb("STAT", [P, GT, 6])
        MV = sb("MV", [P, GT, 2])
        VE = sb("VE", [P, GT])
        RSTD = sb("RSTD", [P, GT])
        EPSC = sb("EPSC", [P, GT])
        PAUSE = sb("PAUSE", [P, 1])
        H = sb("H", [P, GT, D])
        HT = sb("HT", [P, KD, GROUP])
        FQK = sb("FQK", [P, 2, KD, GROUP])
        F = [FQK[:, n, :, :] for n in range(2)]
        HI = [sb(f"HI{n}", [P, KD, GROUP], F32R) for n in range(2)]
        LO = [sb(f"LO{n}", [P, KD, GROUP], F32R) for n in range(2)]
        QS = sb("QS", [P, PAIRED, SEQ], F32R)
        KS = sb("KS", [P, AH_HEADS, SEQ], F32R)
        VS = sb("VS", [P, AT, AH_HEADS * VW])
        M2 = sb("M2", [P, 4, AT, HALVES])
        MP = sb("MP", [P, AT, 2, MW], F32R)
        PBUF = 8
        PB = [sb(f"PB{n}", [P, GROUP])[:, :] for n in range(PBUF - 4)]
        PB += [H[:, 2 * n:2 * n + 2, :].rearrange("p c d -> p (c d)") for n in range(2)]
        PB += [HT[:, n, :] for n in range(2)]
        OS = sb("OS", [P, GROUP])
        RS = sb("RS", [P, GT, 4])
        ATT = FQK[:, :, :, :].rearrange("p n k (a d) -> p (n k a) d", d=D)
        ATTT = [sb(f"ATTT{n}", [P, D]) for n in range(2)]
        U = H
        STAGE = VS[:, :, :].rearrange("p a b -> p (a b)")[:, 0:4 * GROUP]
        UN = HT[:, :, :].rearrange("p k (a d) -> p (k a) d", d=D)
        NR, NM = 4, 3
        RING = [pb(f"RING{n}", [P, GROUP]) for n in range(NR)]
        MRING = [pb(f"MRING{n}", [P, GROUP]) for n in range(NM)]
        PO = pb("PO", [P, GROUP])

        c_load = sem("c_load")
        prep = sem("prep")
        vec = sem("vec")
        gps = sem("gps")
        stats = sem("stats")
        rstd = sem("rstd")
        h_ready = sem("h_ready")
        r_full = sem("r_full")
        r_vec = sem("r_vec")
        r_act = sem("r_act")
        m_full = sem("m_full")
        m_read = sem("m_read")
        hi_ready = sem("hi_ready")
        lo_ready = sem("lo_ready")
        max_ready = sem("max_ready")
        pv_done = sem("pv_done")
        o_read = sem("o_read")
        x_done = sem("x_done")

        plan = []
        for g in range(HALVES):
            plan += [(("T", g, 0), "v"), (("T", g, 1), "a")]
            plan += [(("F", g, n, k), "v") for n in range(2) for k in range(KD)]
            plan += [(("V", g, c), "v") for c in range(GT)]
            plan += [(("ST", g, n, c), "va"[c % 2]) for n in range(2) for c in range(PAIRED)]
        for quad in range(QUADS):
            for g in range(HALVES):
                for kt in range(AT):
                    plan += [(("S", quad, g, kt, j), "a") for j in range(4)]
                    if kt == 1 and (quad or g):
                        before = (quad, g - 1) if g else (quad - 1, HALVES - 1)
                        plan += [(("OT",) + before, "v")]
        plan += [(("OT", QUADS - 1, HALVES - 1), "v")]
        for t in range(AT):
            plan += [(("AT", t), "a"), (("Y", t), "v")]
        while len(plan) % NR:
            plan += [(("pad", len(plan)), "v")]
        NUNITS = len(plan)
        seat, readers = {}, {"v": 0, "a": 0}
        for u, (name, who) in enumerate(plan):
            readers[who] += 1
            seat[name] = (u, who, readers[who])
        ring_read = {"v": r_vec, "a": r_act}
        NMU = QUADS * (4 * AT * HALVES + 2 * HALVES)
        NGROUPS = QUADS * HALVES * AT

        def wait_read(eng, i, u):
            _, who, n = seat[plan[u][0]]
            eng.wait_ge(ring_read[who], i * readers[who] + n)

        block = ctx.enter_context(nc.Block())

        @block.sync
        def _(sp):
            loads = ((IDENT[:, :], ident_d), (WQ[:, :, :], wq.rearrange("(k p) n -> p k n", p=P)),
                     (WK[:, :, :], wk.rearrange("(k p) n -> p k n", p=P)),
                     (WV[:, :, :], wv.rearrange("(k p) n -> p k n", p=P)),
                     (WO[:, :, :], wo.rearrange("(k p) n -> p k n", p=P)),
                     (BQ[:, :], bq), (BK[:, :], bk), (BV[:, :], bv), (BO[:, :], bo),
                     (ONE_ROW[:, :], one_row_d),
                     (STAGE, stack_d.rearrange("p a b -> p (a b)")))
            for dst, src in loads:
                sp.dma_start(dst, src).then_inc(c_load, 16)
            sp.wait_ge(c_load, 16 * len(loads))
        CLOAD = 16 * 11

        @block.gpsimd
        def _(g):
            g.wait_ge(prep, 2)
            with g.Fori(0, BATCH) as i:
                for n in range(2 * HALVES):
                    at = i * 2 * HALVES + n
                    g.wait_ge(stats, at * GT + GT)
                    nc.gpsimd.tensor_tensor(VE[:, :], MV[:, :, 1], EPSC[:, :], ALU.add
                                            ).then_inc(gps, 1)
                    g.wait_ge(gps, at + 1)
                    nc.gpsimd.tensor_tensor(RSTD[:, :], VE[:, :], MHALF[:, :], ALU.pow
                                            ).then_inc(rstd, 1)
            g.wait_ge(rstd, BATCH * 2 * HALVES)

        @block.vector
        def _(v):
            V = nc.vector
            V.memset(MHALF[:, :], -0.5).then_inc(prep, 1)
            V.memset(EPSC[:, :], EPS).then_inc(prep, 1)
            V.memset(MP[:, :, :, :].bitcast(F32), 0.0).then_inc(prep, 1)
            V.memset(PO[:, :], 0.0).then_inc(prep, 1)
            for h in range(2):
                V.memset(KS[HALF[1 - h], h::2, :].bitcast(F32), 0.0).then_inc(prep, 1)
            v.wait_ge(c_load, CLOAD)
            V.tensor_copy(STACK[:, :, :, :].rearrange("p a b c -> p (a b c)"),
                          STAGE).then_inc(prep, 1)
            V.tensor_copy(IDENTR[:, :], IDENT[:, :]).then_inc(prep, 1)
            V.tensor_scalar(BQ[:, :], BQ[:, :], SCALE, None, ALU.mult).then_inc(prep, 1)
            v.wait_ge(prep, 9)
            PER = 2 * HALVES * (GT + 1) + QUADS * HALVES + HALVES
            with v.Fori(0, BATCH) as i:
                link = chain_of(v, vec, i * PER)
                m_at = [0]

                def take(name):
                    u, who, _ = seat[name]
                    v.wait_ge(r_full, i * NUNITS + u + 1)
                    return RING[u % NR]

                def mtake():
                    v.wait_ge(m_full, i * NMU + m_at[0] + 1)
                    m_at[0] += 1
                    return MRING[(m_at[0] - 1) % NM]

                def normed(src, dst, n, done):
                    for c in range(GT):
                        link(V.bn_stats(STAT[:, c, :], src[c]), wait=False)
                    v.wait_ge(vec, i * PER + link.n[0])
                    link(V.memset(PAUSE[:, :], 0.0), wait=False)
                    for c in range(GT):
                        V.bn_aggr(MV[:, c, :], STAT[:, c, :]).then_inc(stats, 1)
                    v.wait_ge(rstd, i * 2 * HALVES + n + 1)
                    for c in range(GT):
                        ins = V.tensor_scalar(dst[:, c, :], src[c], MV[:, c, 0:1],
                                              RSTD[:, c:c + 1], ALU.subtract, ALU.mult)
                        if done is not None:
                            ins.then_inc(done, 1)
                    return ins

                for g in range(HALVES):
                    normed([X[:, i * HALVES + g, c, :] for c in range(GT)], H, g, h_ready)
                    V.tensor_copy(HT[:, 0, :], take(("T", g, 0))[:, :]).then_inc(r_vec, 1)
                    for n, bias in ((0, BQ), (1, BK)):
                        for k in range(KD):
                            bank = take(("F", g, n, k))
                            V.tensor_scalar(F[n][:, k, :], bank[:, :], 1.0 if n else SCALE,
                                            bias[:, k:k + 1], ALU.mult, ALU.add
                                            ).then_inc(r_vec, 1)
                    for c in range(GT):
                        bank = take(("V", g, c))
                        V.tensor_tensor(VS[:, g * GT + c, :], bank[:, 0:AH_HEADS * VW], BV[:, :],
                                        ALU.add
                                        ).then_inc(r_vec, 1)
                    for n in range(2):
                        v.wait_ge(hi_ready, (i * HALVES + g) * 2 + n + 1)
                        V.tensor_tensor(LO[n][:, :, :], F[n][:, :, :],
                                        HI[n][:, :, :].bitcast(F32), ALU.subtract
                                        ).then_inc(lo_ready, 1)
                    for n in range(2):
                        for c in range(0, PAIRED, 2):
                            bank = take(("ST", g, n, c))
                            cols = slice(g * GROUP, (g + 1) * GROUP)
                            if n:
                                for h, r in enumerate(HALF):
                                    ins = V.tensor_scalar(KS[r, 2 * c + h, cols], bank[r, :],
                                                          ONE_ROW[r, 0:1], None, ALU.add)
                            else:
                                ins = V.tensor_copy(QS[:, c, cols], bank[:, :])
                            ins.then_inc(r_vec, 1)

                def maxima(n):
                    j, qt, half = n // (AT * HALVES), n // HALVES % AT, n % HALVES
                    bank = mtake()
                    V.tensor_reduce(M2[:, j, qt, half:half + 1], bank[:, :], AX.X, ALU.max
                                    ).then_inc(m_read, 1)

                def shifts(quad):
                    v.wait_ge(m_read, i * NMU + m_at[0])
                    for j in range(4):
                        at = SHIFT_ROW + 64 * (j % 2)
                        V.tensor_reduce(MP[:, :, j // 2, at:at + 1], M2[:, j, :, :], AX.X, ALU.max,
                                        negate=True).then_inc(max_ready, 1)
                    for cc in range(2):
                        for half in range(HALVES):
                            bank = mtake()
                            q = QS[0:MW, quad * 2 + cc, half * GROUP:(half + 1) * GROUP]
                            V.tensor_tensor(q, q.bitcast(F32), bank[0:MW, :], ALU.add
                                            ).then_inc(m_read, 1)

                def normalise(quad, g):
                    bank = take(("OT", quad, g))
                    o = bank[:, :].rearrange("p (t j d) -> p t j d", t=GT, j=4)
                    link(V.reciprocal(RS[:, :, :].unsqueeze(3), o[:, :, :, AH_DIM:AH_DIM + 1]))
                    out = ATT[:, g * GT:(g + 1) * GT, quad * 64:(quad + 1) * 64]
                    V.tensor_tensor(out.rearrange("p t (j d) -> p t j d", j=4),
                                    o[:, :, :, 0:AH_DIM],
                                    RS[:, :, :].unsqueeze(3).to_broadcast([P, GT, 4, AH_DIM]),
                                    ALU.mult).then_inc(r_vec, 1)

                UNITS1 = 4 * AT * HALVES
                for n in range(UNITS1):
                    maxima(n)
                shifts(0)
                for quad in range(QUADS):
                    for step in range(HALVES * AT):
                        if quad < QUADS - 1:
                            for n in range(4 * step, 4 * step + 4):
                                maxima(n)
                        g, kt = step // AT, step % AT
                        if kt == 1 and (quad or g):
                            normalise(*((quad, g - 1) if g else (quad - 1, HALVES - 1)))
                    if quad < QUADS - 1:
                        shifts(quad + 1)
                normalise(QUADS - 1, HALVES - 1)
                for g in range(HALVES):
                    for c in range(GT):
                        bank = take(("Y", g * GT + c))
                        V.tensor_tensor(U[:, c, :], bank[:, 0:D], BO[:, :], ALU.add
                                        ).then_inc(r_vec, 1)
                    wait_read(v, i, seat[("Y", g * GT + GT - 1)][0])
                    link(normed([U[:, c, :] for c in range(GT)], UN, HALVES + g, None))
                    x = X[:, i * HALVES + g, :, :]
                    V.tensor_tensor(x, x, UN[:, :, :], ALU.add).then_inc(x_done, 1)
                for name, _ in plan:
                    if name[0] == "pad":
                        take(name)
                        V.tensor_copy(RS[:, 0, 0:1], MHALF[:, 0:1]).then_inc(r_vec, 1)
                        v.wait_ge(r_vec, i * readers["v"] + seat[name][2])
                v.wait_ge(x_done, i * HALVES + HALVES)
                assert m_at[0] == NMU
                assert link.n[0] == PER, link.n[0]

        @block.scalar
        def _(a):
            a.wait_ge(prep, 9)
            with a.Fori(0, BATCH) as i:
                def take(name):
                    u, who, _ = seat[name]
                    a.wait_ge(r_full, i * NUNITS + u + 1)
                    return RING[u % NR]
                for g in range(HALVES):
                    nc.scalar.activation(HT[:, 1, :], take(("T", g, 1))[:, :], ACT.Copy
                                         ).then_inc(r_act, 1)
                    for n in range(2):
                        wait_read(a, i, seat[("F", g, n, KD - 1)][0])
                        nc.scalar.activation(HI[n][:, :, :], F[n][:, :, :], ACT.Copy
                                             ).then_inc(hi_ready, 1)
                    for n in range(2):
                        for c in range(1, PAIRED, 2):
                            bank = take(("ST", g, n, c))
                            cols = slice(g * GROUP, (g + 1) * GROUP)
                            if n:
                                for h, r in enumerate(HALF):
                                    ins = nc.scalar.activation(KS[r, 2 * c + h, cols], bank[r, :],
                                                               ACT.Identity,
                                                               bias=ONE_ROW[r, 0:1])
                            else:
                                ins = nc.scalar.activation(QS[:, c, cols], bank[:, :], ACT.Copy)
                            ins.then_inc(r_act, 1)
                for quad in range(QUADS):
                    for g in range(HALVES):
                        for kt in range(AT):
                            step = (quad * HALVES + g) * AT + kt
                            if step >= PBUF // 4:
                                a.wait_ge(pv_done, i * NGROUPS + step - PBUF // 4 + 1)
                            for j in range(4):
                                bank = take(("S", quad, g, kt, j))
                                nc.scalar.activation(PB[(step * 4 + j) % PBUF], bank[:, :],
                                                     ACT.Exp).then_inc(r_act, 1)
                            if kt == 0 and (quad or g):
                                n = quad * HALVES + g
                                a.wait_ge(pv_done, i * NGROUPS + n * AT)
                                nc.scalar.activation(OS[:, :], PO[:, :], ACT.Copy
                                                     ).then_inc(o_read, 1)
                a.wait_ge(pv_done, i * NGROUPS + NGROUPS)
                a.wait_ge(o_read, i * QUADS * HALVES + QUADS * HALVES - 1)
                nc.scalar.activation(OS[:, :], PO[:, :], ACT.Copy).then_inc(o_read, 1)
                for t in range(AT):
                    nc.scalar.activation(ATTT[t % 2][:, :], take(("AT", t))[:, 0:D], ACT.Copy
                                         ).then_inc(r_act, 1)

        @block.tensor
        def _(pe):
            T = nc.tensor
            pe.wait_ge(prep, 9)
            with pe.Fori(0, BATCH) as i:
                m_at = [0]
                order = [0]

                def put(name):
                    u, _, _ = seat[name]
                    assert u == order[0], (name, u, order[0])
                    order[0] += 1
                    if u >= NR:
                        wait_read(pe, i, u - NR)
                    return RING[u % NR]

                def mput():
                    n = m_at[0]
                    m_at[0] += 1
                    pe.wait_ge(m_read, i * NMU + max(0, n - NM + 1))
                    return MRING[n % NM]

                pe.wait_ge(r_vec, i * readers["v"])
                pe.wait_ge(r_act, i * readers["a"])
                for g in range(HALVES):
                    for k in range(KD):
                        bank = put(("T", g, k))
                        for c in range(GT):
                            pe.wait_ge(h_ready, (i * HALVES + g) * GT + c + 1)
                            ins = T.transpose(bank[:, c * P:(c + 1) * P],
                                              H[:, c, k * P:(k + 1) * P], IDENT[:, :])
                        ins.then_inc(r_full, 1)
                    wait_read(pe, i, seat[("T", g, 0)][0])
                    wait_read(pe, i, seat[("T", g, 1)][0])
                    for n, w in ((0, WQ), (1, WK)):
                        for m in range(KD):
                            bank = put(("F", g, n, m))
                            for k in range(KD):
                                ins = T.matmul(bank[:, :], w[:, k, m * P:(m + 1) * P], HT[:, k, :],
                                               start=(k == 0), stop=(k == KD - 1))
                            ins.then_inc(r_full, 1)
                    for c in range(GT):
                        bank = put(("V", g, c))
                        for k in range(KD):
                            ins = T.matmul(bank[:, 0:AH_HEADS * VW],
                                           HT[:, k, c * P:(c + 1) * P], WV[:, k, :],
                                           start=(k == 0), stop=(k == KD - 1))
                        ins.then_inc(r_full, 1)
                    for n in range(2):
                        pe.wait_ge(lo_ready, (i * HALVES + g) * 2 + n + 1)
                        for c in range(PAIRED):
                            bank = put(("ST", g, n, c))
                            k, cc = c // 4, c % 4
                            T.matmul(bank[:, :], STACK[:, 2 * n, cc, :], HI[n][:, k, :],
                                     start=True, stop=False)
                            T.matmul(bank[:, :], STACK[:, 2 * n + 1, cc, :], LO[n][:, k, :],
                                     start=False, stop=True).then_inc(r_full, 1)
                wait_read(pe, i, seat[("ST", HALVES - 1, 1, PAIRED - 1)][0])
                wait_read(pe, i, seat[("ST", HALVES - 1, 1, PAIRED - 2)][0])

                def maxima(quad, n):
                    j, qt, half = n // (AT * HALVES), n // HALVES % AT, n % HALVES
                    c = quad * 2 + j // 2
                    T.matmul(mput()[:, :], QS[:, c, qt * P:(qt + 1) * P],
                             KS[:, quad * 4 + j, half * GROUP:(half + 1) * GROUP], start=True,
                             stop=True).then_inc(m_full, 1)

                def shifts(quad):
                    pe.wait_ge(max_ready, i * QUADS * 4 + quad * 4 + 4)
                    for cc in range(2):
                        for half in range(HALVES):
                            bank = mput()
                            for t in range(GT):
                                ins = T.matmul(bank[0:MW, t * P:(t + 1) * P],
                                               MP[:, half * GT + t, cc, :], IDENTR[:, :],
                                               start=True, stop=True)
                            ins.then_inc(m_full, 1)

                def with_values(step):
                    quad, g, kt = step // (HALVES * AT), step // AT % HALVES, step % AT
                    n = quad * HALVES + g
                    wait_read(pe, i, seat[("S", quad, g, kt, 3)][0])
                    if kt == 0:
                        pe.wait_ge(o_read, i * QUADS * HALVES + n)
                    for j in range(4):
                        head = quad * 4 + j
                        ins = T.matmul(PO[32 * j:32 * j + VW, :],
                                       VS[:, kt, head * VW:(head + 1) * VW],
                                       PB[(step * 4 + j) % PBUF], start=(kt == 0),
                                       stop=(kt == AT - 1))
                    ins.then_inc(pv_done, 1)

                def turn_output(quad, g):
                    pe.wait_ge(o_read, i * QUADS * HALVES + quad * HALVES + g + 1)
                    bank = put(("OT", quad, g))
                    for t in range(GT):
                        ins = T.transpose(bank[:, t * P:(t + 1) * P], OS[:, t * P:(t + 1) * P],
                                          IDENT[:, :])
                    ins.then_inc(r_full, 1)

                for n in range(4 * AT * HALVES):
                    maxima(0, n)
                shifts(0)
                for quad in range(QUADS):
                    pe.wait_ge(m_read, i * NMU + m_at[0])
                    for step in range(HALVES * AT):
                        g, kt = step // AT, step % AT
                        whole = quad * HALVES * AT + step
                        for j in range(4):
                            c = quad * 2 + j // 2
                            T.matmul(put(("S", quad, g, kt, j))[:, :],
                                     KS[:, quad * 4 + j, kt * P:(kt + 1) * P],
                                     QS[:, c, g * GROUP:(g + 1) * GROUP], start=True,
                                     stop=True).then_inc(r_full, 1)
                            if quad < QUADS - 1:
                                maxima(quad + 1, 4 * step + j)
                        if whole:
                            with_values(whole - 1)
                        if kt == 1 and (quad or g):
                            turn_output(*((quad, g - 1) if g else (quad - 1, HALVES - 1)))
                    if quad < QUADS - 1:
                        shifts(quad + 1)
                with_values(QUADS * HALVES * AT - 1)
                turn_output(QUADS - 1, HALVES - 1)
                wait_read(pe, i, seat[("OT", QUADS - 1, HALVES - 1)][0])
                for t in range(AT):
                    bank = put(("AT", t))
                    for k in range(KD):
                        ins = T.transpose(bank[:, k * P:(k + 1) * P],
                                          ATT[:, t, k * P:(k + 1) * P], IDENT[:, :])
                    ins.then_inc(r_full, 1)
                    wait_read(pe, i, seat[("AT", t)][0])
                    bank = put(("Y", t))
                    for k in range(KD):
                        ins = T.matmul(bank[:, 0:D], ATTT[t % 2][:, k * P:(k + 1) * P], WO[:, k, :],
                                       start=(k == 0), stop=(k == KD - 1))
                    ins.then_inc(r_full, 1)
                for name, _ in plan:
                    if name[0] == "pad":
                        T.transpose(put(name)[:, 0:P], IDENT[:, :], IDENT[:, :]
                                    ).then_inc(r_full, 1)


def whole_program(nc, a, out):
    xs = nc.dram_tensor("routed_rows", (XS_TILES * P, D), F32, kind="Internal").ap()
    ys = nc.dram_tensor("expert_rows", (ETILES * P, D), F32, kind="Internal").ap()
    with nc.sbuf_tensor("X", [P, GROUPS, GT, D], F32) as X:
        mamba_stage(nc, X, a["x"], a["w_in"], a["ln_w"], a["ln_b"], a["dt_bias"], a["a_log"],
                    a["d_skip"], a["norm_w"], a["w_out"], a["w_fc1"], a["b_fc1"], a["w_fc2"],
                    a["b_fc2"], a["ident"], a["tri"], a["mask"], a["sel"],
                    a["sel2"], a["keep"], xs.rearrange("(t p r) d -> t p (r d)", p=P, r=4))
        moe_layer(nc, X, xs, ys, a["router0"], a["gate_bias"], a["up0"], a["down0"],
                  a["shared_up"], a["shared_down"], 352, 176, a, None)
        attention_stage(nc, X, a["wq"], a["bq"], a["wk"], a["bk"], a["wv"], a["bv"], a["wo"],
                        a["bo"], a["ident"], a["stack"], a["one_row"])
        moe_layer(nc, X, xs, ys, a["router1"], a["gate_bias"], a["up1"], a["down1"], None, None,
                  0, 512, a, out)


def _constants(np):
    t = np.arange(P)
    full = lambda v: np.ascontiguousarray(np.broadcast_to(np.asarray(v, np.float32), (P, len(v))))
    c = {
        "ident": np.eye(P, dtype=np.float32),
        "tri": (t[:, None] <= t[None, :]).astype(np.float32),
        "mask": np.tile(np.where(t[:, None] <= t[None, :], 0, -1e30).astype(np.float32), (1, GT)),
        "keep": full(np.arange(GROUPS) % (SEQ // GROUP) != 0),
        "rev": full(EXPERTS - np.arange(EXPERTS)),
        "tidx": full(np.arange(ETILES)),
        "step": full(P * np.arange(TILES)),
    }
    heads = np.eye(GT * HEADS, dtype=np.float32)[:, :, None]
    c["sel"] = np.tile(np.repeat(heads, P, axis=2).reshape(GT * HEADS, -1), (2, 1))
    c["sel2"] = np.tile(np.repeat(heads, P // 2, axis=2).reshape(GT * HEADS, -1), (2, 1))
    stack = np.zeros((P, 4, 4, P), np.float32)
    d = np.arange(AH_DIM)
    for cc in range(4):
        for pair in range(2):
            src, at = (2 * cc + pair) * AH_DIM + d, 64 * pair
            stack[src, 0, cc, at + d] = 1
            stack[src, 0, cc, at + SHIFT_ROW + 1 + d] = 1
            stack[src, 1, cc, at + AH_DIM + d] = 1
            stack[src, 2, cc, at + d] = 1
            stack[src, 2, cc, at + AH_DIM + d] = 1
            stack[src, 3, cc, at + SHIFT_ROW + 1 + d] = 1
    c["stack"] = stack.reshape(P, 4, GROUP)
    c["one_row"] = np.isin(t, (SHIFT_ROW, 64 + SHIFT_ROW)).astype(np.float32)[:, None]
    return c


def _layout(np, v):
    def turned(name):
        return np.swapaxes(v[name], -1, -2)

    def chunked(name):
        return v[name].reshape(-1, P).T

    def rows(name):
        return np.broadcast_to(v[name], (P, v[name].shape[-1]))
    w = turned("L0_attn_in_proj_w")
    cut = np.cumsum([D_INNER, D_XB, HEADDIM, HEADDIM, D_INNER])
    z, x, b0, b1, c, dt = np.split(w, cut, axis=1)
    wv = np.zeros((D, AH_HEADS, VW), np.float32)
    wv[:, :, 0:AH_DIM] = v["L1_attn_wv"].reshape(D, AH_HEADS, AH_DIM)
    bv = np.zeros((AH_HEADS, VW), np.float32)
    bv[:, 0:AH_DIM] = v["L1_attn_bv"].reshape(AH_HEADS, AH_DIM)
    bv[:, AH_DIM] = 1
    a = {
        "x": v["L0_attn_hidden_states"].reshape(GROUPS, GT, P, D).transpose(0, 2, 1, 3),
        "w_in": np.concatenate([z, x, b0, b0, b1, b1, dt, c], axis=1),
        "ln_w": chunked("L0_attn_ln_w"), "ln_b": chunked("L0_attn_ln_b"),
        "dt_bias": rows("L0_attn_dt_bias"), "a_log": rows("L0_attn_A_log"),
        "d_skip": rows("L0_attn_Dp"), "norm_w": chunked("L0_attn_norm_w"),
        "w_out": turned("L0_attn_out_proj_w"), "w_fc1": turned("L0_attn_fc1_w"),
        "b_fc1": chunked("L0_attn_fc1_b"), "w_fc2": turned("L0_attn_fc2_w"),
        "b_fc2": rows("L0_attn_fc2_b"),
        "router0": turned("L0_ffn_gate_w"), "gate_bias": rows("L0_ffn_gate_bias"),
        "shared_up": turned("L0_ffn_shared_gw"), "shared_down": turned("L0_ffn_shared_dw"),
        "up0": turned("L0_ffn_up_w"), "down0": turned("L0_ffn_down_w"),
        "wq": v["L1_attn_wq"], "wk": v["L1_attn_wk"], "wo": v["L1_attn_wo"],
        "wv": wv.reshape(D, AH_HEADS * VW), "bq": chunked("L1_attn_bq"),
        "bk": chunked("L1_attn_bk"),
        "bv": np.broadcast_to(bv.reshape(-1), (P, AH_HEADS * VW)), "bo": rows("L1_attn_bo"),
        "router1": turned("L1_ffn_router_weight"), "up1": turned("L1_ffn_ws"),
        "down1": turned("L1_ffn_w2s"),
    }
    return {k: np.ascontiguousarray(x) for k, x in a.items()}


def kernel(**inputs):
    import numpy as np
    import concourse.bacc as bacc
    from concourse.bass_utils import run_bass_kernel_spmd

    arrays = _layout(np, {k: np.asarray(x) for k, x in inputs.items()})
    arrays.update(_constants(np))
    nc = bacc.Bacc("TRN2", target_bir_lowering=False, num_devices=1)
    aps = {k: nc.dram_tensor(f"in_{k}", x.shape, mybir.dt.from_np(x.dtype),
                             kind="ExternalInput").ap() for k, x in arrays.items()}
    out = nc.dram_tensor("out", (GROUPS, P, GT, D), F32, kind="ExternalOutput").ap()
    whole_program(nc, aps, out)
    r = run_bass_kernel_spmd(nc, [{f"in_{k}": x for k, x in arrays.items()}], core_ids=[0])
    y = r.results[0]["out"]
    return y.transpose(0, 2, 1, 3).reshape(BATCH, SEQ, D)
```

```python
import concourse.bass as bass
from concourse import mybir
from contextlib import ExitStack

F32 = mybir.dt.float32
F32R = mybir.dt.float32r
BF16 = mybir.dt.bfloat16
I32 = mybir.dt.int32
U32 = mybir.dt.uint32
ALU = mybir.AluOpType
ACT = mybir.ActivationFunctionType
AX = mybir.AxisListType

P = 128
BATCH, SEQ, D = 4, 1024, 256
TOKENS = BATCH * SEQ
TILES = TOKENS // P
GT = 4
GROUP = GT * P
GROUPS = TILES // GT
KD = D // P
EPS = 1e-5


class Scope:

    def __init__(self, nc, ctx, stage):
        self.nc, self.ctx, self.stage = nc, ctx, stage
        self.sems = []
        ctx.callback(self.release)

    def sb(self, name, shape, dt=F32):
        return self.ctx.enter_context(self.nc.sbuf_tensor(f"{self.stage}_{name}", shape, dt))

    def pb(self, name, shape, dt=F32):
        return self.ctx.enter_context(self.nc.psum_tensor(f"{self.stage}_{name}", shape, dt))

    def sem(self, name):
        self.sems.append(self.nc.alloc_semaphore(name=f"{self.stage}_{name}"))
        return self.sems[-1]

    def release(self):
        self.nc.clear_and_free_semaphores(self.sems)
        self.nc.all_engine_barrier()


def chain_of(eng, sem, at=0):
    n = [0]

    def link(ins, wait=True):
        n[0] += 1
        ins.then_inc(sem, 1)
        if wait:
            eng.wait_ge(sem, at + n[0])
    link.n = n
    return link


def wait(eng, sem, value):
    if not isinstance(value, int) or value > 0:
        eng.wait_ge(sem, value)


D_INNER, D_XB, HEADDIM, D_STATE = 512, 128, 64, 64
HEADS = D_INNER // HEADDIM
KV = D_XB // HEADDIM
REP = HEADS // KV
INTER = 1024
CZ, CX = 0, D_INNER
CB = CX + D_XB
CDT = CB + 2 * D_XB
CC = CDT + HEADS
CEND = CC + D_INNER
XBD = CC - CX
FC1_TILES = INTER // P
Z_TILES = D_INNER // P


HALF = (slice(0, 64), slice(64, 128))


EXPERTS, TOPK = 8, 2
SLOTS = TOPK * TOKENS
ETILES = SLOTS // P + EXPERTS
AHEAD = 8
XS_TILES = ETILES + AHEAD
ROW = D + 1
BIG = 3.0e38
assert ETILES % AHEAD == 0


def mamba_stage(nc, X, x_dram, w_in, ln_w, ln_b, dt_bias, a_log, d_skip, norm_w, w_out,
                w_fc1, b_fc1, w_fc2, b_fc2, ident_d, tri_d, mask_d, sel_d, sel2_d, keep_d,
                fill_d, routed):
    with ExitStack() as ctx:
        s = Scope(nc, ctx, "mb")
        sb, pb, sem = s.sb, s.pb, s.sem
        N32 = GT * HEADS
        WIN = sb("WIN", [P, KD, CEND])
        WF1 = sb("WF1", [P, KD, INTER])
        WF2 = sb("WF2", [P, FC1_TILES, D])
        WOUT = sb("WOUT", [P, Z_TILES, D])
        IDENT = sb("IDENT", [P, P])
        TRI = sb("TRI", [P, P])
        ONES = sb("ONES", [P, P])
        MASKB = sb("MASKB", [P, GROUP], BF16)
        IDENTB = sb("IDENTB", [P, P], BF16)
        SEL = sb("SEL", [P, N32, P], F32R)
        SEL2 = sb("SEL2", [P, N32 // 2, P], F32R)
        LNW = sb("LNW", [P, KD])
        LNB = sb("LNB", [P, KD])
        NORMW = sb("NORMW", [P, Z_TILES])
        BF1 = sb("BF1", [P, FC1_TILES])
        BF2 = sb("BF2", [P, D])
        DTB = sb("DTB", [P, HEADS])
        AH = sb("AH", [P, HEADS])
        NEGA = sb("NEGA", [P, HEADS])
        DSK = sb("DSK", [P, HEADS])
        KEEP = sb("KEEP", [P, GROUPS])
        MHALF = sb("MHALF", [P, GT])
        EPSC = sb("EPSC", [P, GT])
        PAUSE = sb("PAUSE", [P, 1])
        EMPTY = sb("EMPTY", [P, 2, D])
        STAT = sb("STAT", [P, GT, 6])
        MV = [sb(f"MV{n}", [P, GT, 2]) for n in range(3)]
        VE = sb("VE", [P, GT])
        RSTD = [sb(f"RSTD{n}", [P, GT]) for n in range(3)]
        XN = sb("XN", [P, GT, D])
        XNB = sb("XNB", [P, GT, D])
        H = sb("H", [P, GT, D])
        HT = sb("HT", [P, KD, GROUP])
        BT = sb("BT", [P, KV, 2, GROUP])
        CT = sb("CT", [P, HEADS // 2, GROUP])
        XB = sb("XB", [P, GT, XBD])
        ZS = sb("ZS", [P, GT, D_INNER])
        A1 = sb("A1", [P, FC1_TILES, GROUP])
        DTR = sb("DTR", [P, GT, HEADS])
        DTE = sb("DTE", [P, GT, HEADS])
        DTL = sb("DTL", [P, GT, HEADS])
        DT = sb("DT", [P, GT, HEADS])
        DA = sb("DA", [P, 2, N32])
        LT = sb("LT", [P, P], F32R)
        CAT = sb("CAT", [P, 3, N32])
        EXPS = sb("EXPS", [P, 3, N32])
        NEGL = sb("NEGL", [P, N32])
        EDEC = sb("EDEC", [P, HEADS, P])
        ECT = sb("ECT", [P, HEADS // 2, P])
        W = [sb(f"W{n}", [P, HEADS, P]) for n in range(2)]
        CTS = [sb(f"CTS{n}", [P, HEADS // 2, P]) for n in range(2)]
        XDT = [sb(f"XDT{n}", [P, HEADS, HEADDIM]) for n in range(2)]
        XEND = [sb(f"XEND{n}", [P, HEADS, HEADDIM]) for n in range(2)]
        XSKIP = [sb(f"XSKIP{n}", [P, D_INNER]) for n in range(2)]
        STATE = sb("STATE", [P, HEADS, HEADDIM])
        Y1 = sb("Y1", [P, D_INNER])
        G1 = sb("G1", [P, D_INNER])
        SQ = sb("SQ", [P, D_INNER])
        MASKF = SQ
        SSQ = sb("SSQ", [P, GT])
        RMSV = sb("RMSV", [P, 1])
        RMS = sb("RMS", [P, GT])
        G1T = sb("G1T", [P, Z_TILES, P])
        U = sb("U", [P, GT, D])
        UN = sb("UN", [P, GT, D])

        PP = [pb(f"PP{n}", [P, GROUP]) for n in range(2)]
        PL = pb("PL", [P, 2 * GROUP])
        PG = pb("PG", [P, 2 * GROUP])
        PST = pb("PST", [P, GROUP])
        PY = pb("PY", [P, GROUP])

        c_first = sem("c_first")
        c_rest = sem("c_rest")
        prep = sem("prep")
        act_prep = sem("act_prep")
        x_in = sem("x_in")
        ln_vec = sem("ln_vec")
        vec = sem("vec")
        un_vec = sem("un_vec")
        scal = sem("scal")
        ln_gps = sem("ln_gps")
        rms_gps = sem("rms_gps")
        un_gps = sem("un_gps")
        stats = sem("stats")
        rstd = sem("rstd")
        u_stats = sem("u_stats")
        u_rstd = sem("u_rstd")
        xn_ready = sem("xn_ready")
        h_ready = sem("h_ready")
        pp_full = sem("pp_full")
        pp_read = [sem(f"pp_read{n}") for n in range(2)]
        dt_in = sem("dt_in")
        dt_log = sem("dt_log")
        da_ready = sem("da_ready")
        lt_ready = sem("lt_ready")
        cat_ready = sem("cat_ready")
        exps_ready = sem("exps_ready")
        xnb_ready = sem("xnb_ready")
        lb_ready = sem("lb_ready")
        g_ready = sem("g_ready")
        decay_done = sem("decay_done")
        w_done = sem("w_done")
        xdt_done = sem("xdt_done")
        xend_done = sem("xend_done")
        cts_done = sem("cts_done")
        xskip_done = sem("xskip_done")
        y_ready = sem("y_ready")
        kept = sem("kept")
        s_done = sem("s_done")
        y_used = sem("y_used")
        g1_ready = sem("g1_ready")
        ssq_done = sem("ssq_done")
        rms_done = sem("rms_done")
        un_ready = sem("un_ready")
        x_done = sem("x_done")
        z_fill = sem("z_fill")

        plan = [("T", k) for k in range(KD)]
        plan += [("X", c) for c in range(GT)]
        plan += [("B", k) for k in range(KV)]
        plan += [("C", m) for m in range(HEADS // 2)]
        plan += [("CUM", 0)]
        plan += [("Z", c) for c in range(GT)]
        plan += [("F1", m) for m in range(FC1_TILES)]
        plan += [(n, c) for n, c in
                 (("E", 0), ("F2", 0), ("E", 1), ("F2", 1), ("E", 2), ("F2", 2), ("GT", 0),
                  ("O", 0), ("E", 3), ("GT", 1), ("O", 1), ("F2", 3), ("GT", 2), ("O", 2),
                  ("GT", 3), ("O", 3))]
        plan += [("PAD", 0)]
        UNITS = len(plan)
        assert UNITS % 2 == 0
        seat = {name: u for u, name in enumerate(plan)}

        def read(eng, i, *name):
            u = seat[name]
            wait(eng, pp_read[u % 2], i * (UNITS // 2) + u // 2 + 1)

        def take(eng, i, *name):
            u = seat[name]
            eng.wait_ge(pp_full, i * UNITS + u + 1)
            return PP[u % 2], pp_read[u % 2]
        PREPARED = 18

        block = ctx.enter_context(nc.Block())

        @block.sync
        def _(sp):
            sp.dma_start(X[:, 0, :, :], x_dram[0]).then_inc(x_in, 16)
            for dst, src in ((IDENT[:, :], ident_d), (LNW[:, :], ln_w), (LNB[:, :], ln_b),
                             (WIN[:, :, :], w_in.rearrange("(k p) n -> p k n", p=P)),
                             (DTB[:, :], dt_bias), (AH[:, :], a_log)):
                sp.dma_start(dst, src).then_inc(c_first, 16)
            for dst, src in ((DSK[:, :], d_skip), (TRI[:, :], tri_d), (MASKF[:, :], mask_d),
                             (ZS[0:64, :, :].rearrange("p a b -> p (a b)"), sel2_d),
                             (A1[0:64, :, :].rearrange("p a b -> p (a b)"), sel_d),
                             (KEEP[:, :], keep_d),
                             (NORMW[:, :], norm_w), (BF1[:, :], b_fc1), (BF2[:, :], b_fc2),
                             (WOUT[:, :, :], w_out.rearrange("(k p) n -> p k n", p=P)),
                             (WF1[:, :, :], w_fc1.rearrange("(k p) n -> p k n", p=P)),
                             (WF2[:, :, :], w_fc2.rearrange("(k p) n -> p k n", p=P))):
                sp.dma_start(dst, src).then_inc(c_rest, 16)
            with sp.Fori(1, GROUPS) as i:
                sp.wait_ge(x_in, i * 16)
                sp.dma_start(X[:, i, :, :], x_dram[i]).then_inc(x_in, 16)
            sp.wait_ge(prep, PREPARED)
            blocks = XS_TILES // 2
            for xs in routed:
                rows = xs.rearrange("(i p r) d -> i p r d", p=P, r=2)
                with sp.Fori(0, blocks) as i:
                    sp.dma_start(rows[i, :, :, 0:D], EMPTY[:, :, :]).then_inc(z_fill, 16)
                with nc.allow_non_contiguous_dma(reason="one word of each row"):
                    sp.dma_start(xs[:, D:ROW].bitcast(I32), fill_d).then_inc(z_fill, 16)
            sp.wait_ge(z_fill, 16 * (blocks + 1) * len(routed))
        C_FIRST, C_REST = 16 * 6, 16 * 12

        @block.vector
        def _(v):
            V = nc.vector

            def moments(src, mv, chain, at, done):
                for c in range(GT):
                    V.bn_stats(STAT[:, c, :], src[c]).then_inc(chain, 1)
                v.wait_ge(chain, at + GT)
                V.memset(PAUSE[:, :], 0.0).then_inc(chain, 1)
                for c in range(GT):
                    V.bn_aggr(mv[:, c, :], STAT[:, c, :]).then_inc(done, 1)

            LN_CHAIN = 2 * (GT + 1)

            def norm_x(j):
                v.wait_ge(x_in, j * 16 + 16)
                moments([X[:, j, c, :] for c in range(GT)], MV[0], ln_vec, j * LN_CHAIN, stats)

            def norm_h(j):
                v.wait_ge(rstd, j * 2 + 1)
                wait(v, xnb_ready, j * 1)
                for c in range(GT):
                    V.tensor_scalar(XN[:, c, :], X[:, j, c, :], MV[0][:, c, 0:1],
                                    RSTD[0][:, c:c + 1], ALU.subtract, ALU.mult
                                    ).then_inc(xn_ready, 1)
                v.wait_ge(xn_ready, j * GT + GT)
                moments([XN[:, c, :] for c in range(GT)], MV[1], ln_vec,
                        j * LN_CHAIN + GT + 1, stats)

            def write_h(j):
                v.wait_ge(rstd, j * 2 + 2)
                for c in range(GT):
                    V.tensor_scalar(H[:, c, :], XN[:, c, :], MV[1][:, c, 0:1],
                                    RSTD[1][:, c:c + 1], ALU.subtract, ALU.mult
                                    ).then_inc(h_ready, 1)

            def moments_u(j):
                read(v, j, "O", GT - 2)
                read(v, j, "O", GT - 1)
                moments([U[:, c, :] for c in range(GT)], MV[2], un_vec, j * (GT + 1), u_stats)

            def norm_u(j):
                v.wait_ge(u_rstd, j + 1)
                wait(v, x_done, j * GT)
                for c in range(GT):
                    V.tensor_scalar(UN[:, c, :], U[:, c, :], MV[2][:, c, 0:1],
                                    RSTD[2][:, c:c + 1], ALU.subtract, ALU.mult
                                    ).then_inc(un_ready, 1)

            def body(i, first, last):
                VEC = 3 + GT
                link = chain_of(v, vec, i * VEC)
                for c in range(GT):
                    bank, done = take(v, i, "X", c)
                    V.tensor_copy(XB[:, c, :], bank[:, 0:XBD]).then_inc(done, 1)
                read(v, i, "X", GT - 2)
                read(v, i, "X", GT - 1)
                V.tensor_tensor(DTR[:, :, :], XB[:, :, CDT - CX:XBD],
                                DTB[:, :].unsqueeze(1).to_broadcast([P, GT, HEADS]), ALU.add
                                ).then_inc(dt_in, 1)
                bank, done = take(v, i, "B", 0)
                for q, r in enumerate(HALF):
                    ins = V.tensor_copy(BT[r, 0, q, :], bank[r, :])
                ins.then_inc(done, 1)
                v.wait_ge(dt_log, i + 1)
                link(V.scalar_tensor_tensor(out=DT[:, :, :], in0=DTR[:, :, :], scalar=0.0,
                                            in1=DTL[:, :, :], op0=ALU.max, op1=ALU.add))
                for n in range(2):
                    ins = V.tensor_tensor(
                        DA[:, n, :].rearrange("p (c h) -> p c h", c=GT), DT[:, :, :],
                        NEGA[:, :].unsqueeze(1).to_broadcast([P, GT, HEADS]), ALU.mult)
                ins.then_inc(da_ready, 1)
                for m in (0, 2):
                    bank, done = take(v, i, "C", m)
                    V.tensor_copy(CT[:, m, :], bank[:, :]).then_inc(done, 1)
                bank, done = take(v, i, "CUM", 0)
                sums = bank[:, 0:2 * N32].rearrange("p (a n) -> p a n", a=2)
                rows = bank[0:64, 2 * N32:2 * N32 + P]
                link(V.tensor_copy(LT[0:64, :], rows))
                V.tensor_tensor(LT[N32:2 * N32, :], rows[N32:2 * N32, :],
                                LT[N32:2 * N32, :].bitcast(F32), ALU.subtract
                                ).then_inc(lt_ready, 1)
                V.tensor_copy(CAT[:, 0:2, :], sums).then_inc(done, 1)
                read(v, i, "CUM", 0)
                link(V.tensor_scalar(NEGL[:, :], CAT[:, 0, :], -1.0, None, ALU.mult))
                V.tensor_tensor(CAT[:, 2, :], CAT[:, 1, :], CAT[:, 0, :], ALU.subtract
                                ).then_inc(cat_ready, 1)
                V.tensor_scalar(STATE[:, :, :], STATE[:, :, :],
                                KEEP[:, i:i + 1] if isinstance(i, int)
                                else KEEP[:, bass.ds(i, 1)], None, ALU.mult
                                ).then_inc(kept, 1)
                v.wait_ge(kept, i + 1)
                if not first:
                    norm_u(i - 1)

                def mlp(c):
                    bank, done = take(v, i, "F2", c)
                    if c == 0:
                        v.wait_ge(xnb_ready, i + 1)
                        wait(v, un_ready, i * GT)
                    V.tensor_tensor(U[:, c, :], bank[:, 0:D], XNB[:, c, :], ALU.add
                                    ).then_inc(done, 1)

                def before(c):
                    if c < GT - 1:
                        mlp(c)
                    v.wait_ge(decay_done, i * GT + c + 1)
                    v.wait_ge(g_ready, i * GT + c + 1)
                    if c >= 2:
                        v.wait_ge(y_ready, i * GT + c - 1)
                    V.tensor_tensor(
                        W[c % 2][:, :, :].rearrange("p (m q) t -> p m q t", q=2),
                        EDEC[:, :, :].rearrange("p (m q) t -> p m q t", q=2),
                        PG[:, :].rearrange("p (q m t) -> p m q t", q=2, t=P), ALU.mult
                    ).then_inc(w_done, 1)

                def carry(c):
                    cs = slice(c * HEADS, (c + 1) * HEADS)
                    v.wait_ge(exps_ready, i + 1)
                    v.wait_ge(y_ready, i * GT + c + 1)
                    v.wait_ge(xskip_done, i * GT + c + 1)
                    V.tensor_tensor(Y1[:, :], PY[:, :], XSKIP[c % 2][:, :], ALU.add
                                    ).then_inc(y_used, 1)
                    link(V.tensor_tensor(
                        STATE[:, :, :], STATE[:, :, :], EXPS[:, 1, cs].unsqueeze(2)
                        .to_broadcast([P, HEADS, HEADDIM]), ALU.mult))
                    for q, r in enumerate(HALF):
                        st = STATE[r, :, :].rearrange("p (m q) d -> p q m d", q=2)[:, q]
                        ps = PST[r, :].rearrange("p (m q d) -> p q m d", q=2, d=HEADDIM)[:, q]
                        ins = V.tensor_tensor(st, st, ps, ALU.add)
                    ins.then_inc(s_done, 1)
                    v.wait_ge(y_used, i * GT + c + 1)
                    read(v, i, "Z", c)
                    wait(v, ssq_done, i * GT + c)
                    if c:
                        v.wait_ge(pp_full, i * UNITS + seat[("GT", c - 1)] + 1)
                    V.tensor_tensor(G1[:, :], Y1[:, :], ZS[:, c, :], ALU.mult
                                    ).then_inc(g1_ready, 1)
                    v.wait_ge(s_done, i * GT + c + 1)

                def projected(c):
                    v.wait_ge(rms_done, i * GT + c + 1)
                    read(v, i, "F2", c)
                    bank, done = take(v, i, "O", c)
                    V.scalar_tensor_tensor(
                        out=U[:, c, :], in0=bank[:, 0:D], scalar=RMS[:, c:c + 1],
                        in1=U[:, c, :], op0=ALU.mult, op1=ALU.add).then_inc(done, 1)

                before(0)
                before(1)
                carry(0)
                if not last:
                    norm_x(i + 1)
                before(2)
                carry(1)
                projected(0)
                if not last:
                    norm_h(i + 1)
                before(3)
                carry(2)
                projected(1)
                mlp(3)
                carry(3)
                if not last:
                    write_h(i + 1)
                projected(2)
                projected(3)
                take(v, i, "PAD", 0)
                V.memset(PAUSE[:, :], 0.0).then_inc(pp_read[seat[("PAD", 0)] % 2], 1)
                moments_u(i)
                assert link.n[0] == VEC, link.n[0]

            V.memset(MHALF[:, :], -0.5).then_inc(prep, 1)
            V.memset(EPSC[:, :], EPS).then_inc(prep, 1)
            V.memset(STATE[:, :, :], 0.0).then_inc(prep, 1)
            norm_x(0)
            V.memset(ONES[:, :], 1.0).then_inc(prep, 1)
            V.memset(EMPTY[:, :, :], 0.0).then_inc(prep, 1)
            norm_h(0)
            V.memset(LT[:, :].bitcast(F32), 0.0).then_inc(prep, 1)
            write_h(0)
            V.memset(BT[:, :, :, :], 0.0).then_inc(prep, 1)
            V.memset(SEL[64:, :, :].bitcast(F32), 0.0).then_inc(prep, 1)
            V.memset(SEL2[64:, :, :].bitcast(F32), 0.0).then_inc(prep, 1)
            v.wait_ge(act_prep, 1)
            V.tensor_scalar(NEGA[:, :], AH[:, :], -1.0, None, ALU.mult).then_inc(prep, 1)
            v.wait_ge(c_rest, C_REST)
            V.tensor_copy(MASKB[:, :], MASKF[:, :]).then_inc(prep, 1)
            V.tensor_copy(IDENTB[:, :], IDENT[:, :]).then_inc(prep, 1)
            V.tensor_copy(SEL[0:64, :, :].rearrange("p a b -> p (a b)"),
                          A1[0:64, :, :].rearrange("p a b -> p (a b)")).then_inc(prep, 1)
            V.tensor_copy(SEL2[0:64, :, :].rearrange("p a b -> p (a b)"),
                          ZS[0:64, :, :].rearrange("p a b -> p (a b)")).then_inc(prep, 1)
            for k in range(Z_TILES):
                V.tensor_scalar(WOUT[:, k, :], WOUT[:, k, :], NORMW[:, k:k + 1], None,
                                ALU.mult).then_inc(prep, 1)
            v.wait_ge(prep, PREPARED)
            body(0, True, False)
            with v.Fori(1, GROUPS - 1) as i:
                body(i, False, False)
            body(GROUPS - 1, False, True)
            norm_u(GROUPS - 1)
            v.wait_ge(un_ready, GROUPS * GT)

        @block.gpsimd
        def _(g):
            G = nc.gpsimd

            def inverse_std(n, chain, count, done):
                G.tensor_tensor(VE[:, :], MV[n][:, :, 1], EPSC[:, :], ALU.add).then_inc(chain, 1)
                g.wait_ge(chain, count)
                G.tensor_tensor(RSTD[n][:, :], VE[:, :], MHALF[:, :], ALU.pow).then_inc(done, 1)
                g.wait_ge(done, count)

            def input_std(j, n):
                g.wait_ge(stats, (j * 2 + n + 1) * GT)
                inverse_std(n, ln_gps, j * 2 + n + 1, rstd)

            def add_x(j):
                x = (lambda c: X[:, j, c, :])
                for c in range(GT):
                    g.wait_ge(un_ready, j * GT + c + 1)
                    G.tensor_tensor(x(c), x(c), UN[:, c, :], ALU.add).then_inc(x_done, 1)

            def body(i, first, last):
                if not first:
                    g.wait_ge(u_stats, i * GT)
                    inverse_std(2, un_gps, i, u_rstd)
                g.wait_ge(xn_ready, i * GT + GT)
                if not first:
                    read(g, i - 1, "F2", GT - 1)
                G.tensor_tensor(XNB[:, :, :], XN[:, :, :],
                                BF2[:, :].unsqueeze(1).to_broadcast([P, GT, D]), ALU.add
                                ).then_inc(xnb_ready, 1)
                if not first:
                    add_x(i - 1)
                g.wait_ge(da_ready, i + 1)
                g.wait_ge(cat_ready, i + 1)

                def by_dt(out, c, weight, done):
                    for r in range(KV):
                        ins = G.tensor_tensor(
                            out[:, r * REP:(r + 1) * REP, :],
                            XB[:, c, r * HEADDIM:(r + 1) * HEADDIM].unsqueeze(1)
                            .to_broadcast([P, REP, HEADDIM]),
                            weight[:, r * REP:(r + 1) * REP].unsqueeze(2)
                            .to_broadcast([P, REP, HEADDIM]), ALU.mult)
                    ins.then_inc(done, 1)

                def operands(c):
                    cs = slice(c * HEADS, (c + 1) * HEADS)
                    if c >= 2:
                        g.wait_ge(y_ready, i * GT + c - 1)
                    by_dt(XDT[c % 2], c, DT[:, c, :], xdt_done)
                    g.wait_ge(xdt_done, i * GT + c + 1)
                    g.wait_ge(exps_ready, i + 1)
                    G.tensor_tensor(XEND[c % 2][:, :, :], XDT[c % 2][:, :, :],
                                    EXPS[:, 2, cs].unsqueeze(2)
                                    .to_broadcast([P, HEADS, HEADDIM]), ALU.mult
                                    ).then_inc(xend_done, 1)
                    read(g, i, "E", c)
                    G.tensor_tensor(CTS[c % 2][:, :, :], CT[:, :, c * P:(c + 1) * P],
                                    ECT[:, :, :], ALU.mult).then_inc(cts_done, 1)

                def skip(c):
                    if c >= 2:
                        g.wait_ge(y_used, i * GT + c - 1)
                    by_dt(XSKIP[c % 2][:, :].rearrange("p (h d) -> p h d", d=HEADDIM), c,
                          DSK[:, :], xskip_done)

                def inverse_rms(c):
                    g.wait_ge(ssq_done, i * GT + c + 1)
                    G.tensor_tensor(RMSV[:, :], SSQ[:, c:c + 1], EPSC[:, 0:1], ALU.add
                                    ).then_inc(rms_gps, 1)
                    g.wait_ge(rms_gps, i * GT + c + 1)
                    G.tensor_tensor(RMS[:, c:c + 1], RMSV[:, :], MHALF[:, 0:1], ALU.pow
                                    ).then_inc(rms_done, 1)
                    g.wait_ge(rms_done, i * GT + c + 1)

                operands(0)
                skip(0)
                operands(1)
                skip(1)
                if not last:
                    input_std(i + 1, 0)
                operands(2)
                inverse_rms(0)
                skip(2)
                if not last:
                    input_std(i + 1, 1)
                operands(3)
                inverse_rms(1)
                skip(3)
                inverse_rms(2)
                inverse_rms(3)

            g.wait_ge(prep, 2)
            input_std(0, 0)
            input_std(0, 1)
            g.wait_ge(prep, PREPARED)
            g.wait_ge(c_rest, C_REST)
            body(0, True, False)
            with g.Fori(1, GROUPS - 1) as i:
                body(i, False, False)
            body(GROUPS - 1, False, True)
            g.wait_ge(u_stats, GROUPS * GT)
            inverse_std(2, un_gps, GROUPS, u_rstd)
            add_x(GROUPS - 1)
            g.wait_ge(x_done, GROUPS * GT)

        @block.scalar
        def _(a):
            A = nc.scalar
            a.wait_ge(c_first, C_FIRST)
            A.activation(AH[:, :], AH[:, :], ACT.Exp).then_inc(act_prep, 1)
            with a.Fori(0, GROUPS) as i:
                link = chain_of(a, scal, i * 2)
                for k in range(KD):
                    bank, done = take(a, i, "T", k)
                    A.activation(HT[:, k, :], bank[:, :], ACT.Identity, bias=LNB[:, k:k + 1],
                                 scale=LNW[:, k:k + 1]).then_inc(done, 1)
                a.wait_ge(prep, PREPARED)
                a.wait_ge(dt_in, i + 1)
                link(A.activation(DTE[:, :, :], DTR[:, :, :], ACT.Abs))
                link(A.activation(DTE[:, :, :], DTE[:, :, :], ACT.Exp, scale=-1.0))
                A.activation(DTL[:, :, :], DTE[:, :, :], ACT.Ln, bias=1.0).then_inc(dt_log, 1)
                bank, done = take(a, i, "B", 1)
                for q, r in enumerate(HALF):
                    ins = A.activation(BT[r, 1, q, :], bank[r, :], ACT.Copy)
                ins.then_inc(done, 1)
                for m in (1, 3):
                    bank, done = take(a, i, "C", m)
                    A.activation(CT[:, m, :], bank[:, :], ACT.Copy).then_inc(done, 1)
                for c in range(GT):
                    bank, done = take(a, i, "Z", c)
                    A.activation(ZS[:, c, :], bank[:, :], ACT.Silu).then_inc(done, 1)
                for m in range(FC1_TILES):
                    bank, done = take(a, i, "F1", m)
                    A.activation(A1[:, m, :], bank[:, :], ACT.Gelu_apprx_tanh,
                                 bias=BF1[:, m:m + 1]).then_inc(done, 1)
                a.wait_ge(cat_ready, i + 1)
                A.activation(EXPS[:, :, :], CAT[:, :, :], ACT.Exp).then_inc(exps_ready, 1)

                def decays(c):
                    a.wait_ge(lb_ready, i * GT + c + 1)
                    wait(a, w_done, i * GT + c)
                    for h in range(HEADS):
                        n = c * HEADS + h
                        ins = A.activation(EDEC[:, h, :], PL[:, h * P:(h + 1) * P], ACT.Exp,
                                           bias=NEGL[:, n:n + 1])
                    ins.then_inc(decay_done, 1)
                    bank, done = take(a, i, "E", c)
                    wait(a, cts_done, i * GT + c)
                    A.activation(ECT[:, :, :].rearrange("p m t -> p (m t)"), bank[:, :], ACT.Exp
                                 ).then_inc(done, 1)

                def square_and_turn(c):
                    a.wait_ge(g1_ready, i * GT + c + 1)
                    wait(a, ssq_done, i * GT + c)
                    if c:
                        a.wait_ge(rms_done, i * GT + c)
                    A.activation(SQ[:, :], G1[:, :], ACT.Square, scale=D_INNER ** -0.5,
                                 accum_out=SSQ[:, c:c + 1]).then_inc(ssq_done, 1)
                    bank, done = take(a, i, "GT", c)
                    A.activation(G1T[:, :, :].rearrange("p m t -> p (m t)"), bank[:, :], ACT.Copy
                                 ).then_inc(done, 1)

                decays(0)
                decays(1)
                decays(2)
                square_and_turn(0)
                decays(3)
                square_and_turn(1)
                square_and_turn(2)
                square_and_turn(3)
            a.wait_ge(ssq_done, GROUPS * GT)
            read(a, GROUPS - 1, "GT", GT - 1)

        @block.tensor
        def _(pe):
            T = nc.tensor
            pe.wait_ge(c_first, C_FIRST)
            with pe.Fori(0, GROUPS) as i:
                order = [0]

                def put(*name):
                    u = seat[name]
                    assert u == order[0], (name, u, order[0])
                    order[0] += 1
                    pe.wait_ge(pp_read[u % 2], i * (UNITS // 2) + u // 2)
                    return PP[u % 2]

                def wide(name, lhsT_of, rhs_of, ks, cols):
                    out = put(*name)
                    for k in range(ks):
                        ins = T.matmul(out[:, 0:cols], lhsT_of(k), rhs_of(k), start=(k == 0),
                                       stop=(k == ks - 1))
                    ins.then_inc(pp_full, 1)

                def mlp(c):
                    wide(("F2", c), lambda m: A1[:, m, c * P:(c + 1) * P],
                         lambda m: WF2[:, m, :], FC1_TILES, D)

                def before(c):
                    t = slice(c * P, (c + 1) * P)
                    wait(pe, decay_done, i * GT + c)
                    for half in range(2):
                        bank = PL[:, half * GROUP:(half + 1) * GROUP]
                        for n in range(GT):
                            h = half * GT + n
                            T.matmul(bank[:, n * P:(n + 1) * P], SEL[:, c * HEADS + h, :],
                                     LT[:, :], start=(n == 0), stop=False,
                                     skip_group_check=True)
                        ins = T.matmul(bank, IDENTB[:, :], MASKB[:, :], start=False, stop=True,
                                       skip_group_check=True)
                    ins.then_inc(lb_ready, 1)
                    out = put("E", c)
                    for m in range(HEADS // 2):
                        ins = T.matmul(out[:, m * P:(m + 1) * P],
                                       SEL2[:, c * HEADS // 2 + m, :], LT[:, :], start=True,
                                       stop=True)
                    ins.then_inc(pp_full, 1)
                    if c == 0:
                        read(pe, i, "F1", FC1_TILES - 2)
                        read(pe, i, "F1", FC1_TILES - 1)
                    if c < GT - 1:
                        mlp(c)
                    wait(pe, w_done, i * GT + c)
                    for q in range(2):
                        for k in range(KV):
                            at = q * GROUP + k * 2 * P
                            ins = T.matmul(PG[:, at:at + 2 * P], BT[:, k, q, t],
                                           CT[:, 2 * k:2 * k + 2, t], start=True, stop=True)
                    ins.then_inc(g_ready, 1)

                def outputs(c):
                    pe.wait_ge(xend_done, i * GT + c + 1)
                    wait(pe, s_done, i * GT + c)
                    for k in range(KV):
                        T.matmul(PST[:, k * 2 * P:(k + 1) * 2 * P],
                                 XB[:, c, D_XB + k * P:D_XB + (k + 1) * P],
                                 XEND[c % 2][:, k * REP:(k + 1) * REP, :]
                                 .rearrange("p h d -> p (h d)"), start=True, stop=True)
                    pe.wait_ge(w_done, i * GT + c + 1)
                    pe.wait_ge(cts_done, i * GT + c + 1)
                    wait(pe, y_used, i * GT + c)
                    if c == 0:
                        pe.wait_ge(kept, i + 1)
                    for h in range(HEADS):
                        y = PY[:, h * HEADDIM:(h + 1) * HEADDIM]
                        T.matmul(y, W[c % 2][:, h, :], XDT[c % 2][:, h, :], start=True,
                                 stop=False)
                        ins = T.matmul(y, CTS[c % 2][:, h // 2, :], STATE[:, h, :],
                                       start=False, stop=True)
                    ins.then_inc(y_ready, 1)

                def turn(c):
                    pe.wait_ge(g1_ready, i * GT + c + 1)
                    out = put("GT", c)
                    for m in range(Z_TILES):
                        ins = T.transpose(out[:, m * P:(m + 1) * P], G1[:, m * P:(m + 1) * P],
                                          IDENT[:, :])
                    ins.then_inc(pp_full, 1)

                def project(c):
                    read(pe, i, "GT", c)
                    wide(("O", c), lambda m: G1T[:, m, :], lambda m: WOUT[:, m, :], Z_TILES, D)

                for k in range(KD):
                    out = put("T", k)
                    for c in range(GT):
                        pe.wait_ge(h_ready, i * GT + c + 1)
                        ins = T.transpose(out[:, c * P:(c + 1) * P], H[:, c, k * P:(k + 1) * P],
                                          IDENT[:, :])
                    ins.then_inc(pp_full, 1)
                read(pe, i, "T", 0)
                read(pe, i, "T", 1)
                def by_token(kind, at, cols):
                    for c in range(GT):
                        wide((kind, c), lambda k: HT[:, k, c * P:(c + 1) * P],
                             lambda k: WIN[:, k, at:at + cols], KD, cols)

                by_token("X", CX, XBD)
                for name, col in ([(("B", k), CB + k * P) for k in range(KV)] +
                                  [(("C", m), CC + m * P) for m in range(HEADS // 2)]):
                    wide(name, lambda k: WIN[:, k, col:col + P], lambda k: HT[:, k, :], KD,
                         GROUP)
                pe.wait_ge(prep, PREPARED)
                pe.wait_ge(da_ready, i + 1)
                out = put("CUM", 0)
                T.matmul(out[:, 0:N32], TRI[:, :], DA[:, 0, :], start=True, stop=True)
                T.matmul(out[:, N32:2 * N32], ONES[:, :], DA[:, 0, :], start=True, stop=True)
                T.matmul(out[0:2 * N32, 2 * N32:2 * N32 + P],
                         DA[:, :, :].rearrange("p a n -> p (a n)"), TRI[:, :], start=True,
                         stop=True).then_inc(pp_full, 1)
                by_token("Z", CZ, D_INNER)
                pe.wait_ge(c_rest, C_REST)
                for m in range(FC1_TILES):
                    wide(("F1", m), lambda k: WF1[:, k, m * P:(m + 1) * P],
                         lambda k: HT[:, k, :], KD, GROUP)
                pe.wait_ge(lt_ready, i + 1)
                before(0)
                before(1)
                outputs(0)
                before(2)
                turn(0)
                outputs(1)
                project(0)
                before(3)
                turn(1)
                outputs(2)
                project(1)
                mlp(3)
                turn(2)
                outputs(3)
                project(2)
                turn(3)
                project(3)
                T.transpose(put("PAD", 0)[:, 0:P], IDENT[:, :], IDENT[:, :]).then_inc(pp_full, 1)

def route_stage(nc, X, XN, HTA, LOG, w_router, ident_d, weight_loads, w_load, hs):
    with ExitStack() as ctx:
        s = Scope(nc, ctx, f"rt{hs}")
        sb, pb, sem = s.sb, s.pb, s.sem
        IDENT = sb("IDENT", [P, P])
        WR = sb("WR", [P, KD, EXPERTS])
        MHALF = sb("MHALF", [P, GT])
        STAT = sb("STAT", [P, GT, 6])
        MV = sb("MV", [P, GT, 2])
        VE = sb("VE", [P, GT])
        RSTD = sb("RSTD", [P, GT])
        EPSC = sb("EPSC", [P, GT])
        PAUSE = sb("PAUSE", [P, 1])
        H = sb("H", [P, GT, D])
        HT = sb("HT", [P, KD, GROUP])
        PP = [pb(f"PP{n}", [P, GROUP]) for n in range(2)]
        PR = pb("PR", [P, GT, EXPERTS])
        c_load = sem("c_load")
        prep = sem("prep")
        vec = sem("vec")
        gps = sem("gps")
        stats = sem("stats")
        rstd = sem("rstd")
        h_ready = sem("h_ready")
        pp_full = sem("pp_full")
        ht_vec = sem("ht_vec")
        ht_act = sem("ht_act")
        ht_kept = sem("ht_kept")
        r_full = sem("r_full")
        r_read = sem("r_read")
        xn_kept = sem("xn_kept")
        block = ctx.enter_context(nc.Block())

        @block.sync
        def _(sp):
            sp.dma_start(IDENT[:, :], ident_d).then_inc(c_load, 16)
            sp.dma_start(WR[:, :, :], w_router.rearrange("(k p) n -> p k n", p=P)
                         ).then_inc(c_load, 16)
            for dst, src in weight_loads:
                sp.dma_start(dst, src).then_inc(w_load, 16)

        @block.vector
        def _(v):
            V = nc.vector

            def moments(j):
                for c in range(GT):
                    V.bn_stats(STAT[:, c, :], X[:, j, c, :]).then_inc(vec, 1)
                v.wait_ge(vec, j * (GT + 1) + GT)
                V.memset(PAUSE[:, :], 0.0).then_inc(vec, 1)
                for c in range(GT):
                    V.bn_aggr(MV[:, c, :], STAT[:, c, :]).then_inc(stats, 1)

            def normed(j):
                v.wait_ge(rstd, j + 1)
                wait(v, xn_kept, j * 1)
                for c in range(GT):
                    V.tensor_scalar(H[:, c, :], X[:, j, c, :], MV[:, c, 0:1],
                                    RSTD[:, c:c + 1], ALU.subtract, ALU.mult
                                    ).then_inc(h_ready, 1)

            def body(i, last):
                if not last:
                    moments(i + 1)
                v.wait_ge(pp_full, i * 2 + 2)
                if HTA is not None:
                    wait(v, ht_kept, i * 1)
                V.tensor_copy(HT[:, 0, :], PP[0][:, :]).then_inc(ht_vec, 1)
                if not last:
                    normed(i + 1)

            V.memset(MHALF[:, :], -0.5).then_inc(prep, 1)
            V.memset(EPSC[:, :], EPS).then_inc(prep, 1)
            moments(0)
            normed(0)
            with v.Fori(0, GROUPS - 1) as i:
                body(i, False)
            body(GROUPS - 1, True)
            v.wait_ge(ht_vec, GROUPS)

        @block.gpsimd
        def _(g):
            g.wait_ge(prep, 2)

            def inverse_std(j):
                g.wait_ge(stats, j * GT + GT)
                nc.gpsimd.tensor_tensor(VE[:, :], MV[:, :, 1], EPSC[:, :], ALU.add
                                        ).then_inc(gps, 1)
                g.wait_ge(gps, j + 1)
                nc.gpsimd.tensor_tensor(RSTD[:, :], VE[:, :], MHALF[:, :], ALU.pow
                                        ).then_inc(rstd, 1)

            def keep_ht(j):
                if HTA is not None:
                    g.wait_ge(ht_vec, j + 1)
                    g.wait_ge(ht_act, j + 1)
                    nc.gpsimd.tensor_copy(HTA[:, j, :, :], HT[:, :, :]).then_inc(ht_kept, 1)

            inverse_std(0)
            with g.Fori(0, GROUPS - 1) as i:
                inverse_std(i + 1)
                keep_ht(i)
            keep_ht(GROUPS - 1)
            g.wait_ge(rstd, GROUPS)
            if HTA is not None:
                g.wait_ge(ht_kept, GROUPS)

        @block.scalar
        def _(a):
            with a.Fori(0, GROUPS) as i:
                a.wait_ge(h_ready, i * GT + GT)
                nc.scalar.activation(XN[:, i, :, 0:D], H[:, :, :], ACT.Copy
                                     ).then_inc(xn_kept, 1)
                a.wait_ge(pp_full, i * 2 + 2)
                if HTA is not None:
                    a.wait_ge(ht_kept, i)
                nc.scalar.activation(HT[:, 1, :], PP[1][:, :], ACT.Copy).then_inc(ht_act, 1)
                a.wait_ge(r_full, i + 1)
                nc.scalar.activation(LOG[:, i, :, :], PR[:, :, :], ACT.Copy).then_inc(r_read, 1)
            a.wait_ge(ht_act, GROUPS)
            a.wait_ge(r_read, GROUPS)
            a.wait_ge(xn_kept, GROUPS)

        @block.tensor
        def _(pe):
            pe.wait_ge(c_load, 32)
            with pe.Fori(0, GROUPS) as i:
                for k, done in enumerate((ht_vec, ht_act)):
                    pe.wait_ge(done, i)
                    for c in range(GT):
                        pe.wait_ge(h_ready, i * GT + c + 1)
                        ins = nc.tensor.transpose(PP[k][:, c * P:(c + 1) * P],
                                                  H[:, c, k * P:(k + 1) * P], IDENT[:, :])
                    ins.then_inc(pp_full, 1)
                pe.wait_ge(ht_vec, i + 1)
                pe.wait_ge(ht_act, i + 1)
                pe.wait_ge(r_read, i)
                for c in range(GT):
                    for k in range(KD):
                        ins = nc.tensor.matmul(PR[:, c, :], HT[:, k, c * P:(c + 1) * P],
                                               WR[:, k, :], start=(k == 0), stop=(k == KD - 1))
                ins.then_inc(r_full, 1)


def dispatch_stage(nc, XN, HTA, LOG, WT, EXP_OF, SHARED, gate_bias, w_sgate, w_sdown, tri_d,
                   rev_d, tile_d, step_d, slot_d, xs, hs):
    sigmoid = hs > 0
    with ExitStack() as ctx:
        s = Scope(nc, ctx, f"dp{hs}")
        sb, pb, sem = s.sb, s.pb, s.sem
        TRI = sb("TRI", [P, P])
        ONES = sb("ONES", [P, P])
        REV = sb("REV", [P, EXPERTS])
        TIDX = sb("TIDX", [P, ETILES])
        STEP = sb("STEP", [P, TILES])
        GB = sb("GB", [P, EXPERTS])
        te = [P, TILES, EXPERTS]
        SC, SEL, EQ, T, POSF = (sb(n, te) for n in ("SC", "SEL", "EQ", "T", "POSF"))
        O = [sb(f"O{n}", te) for n in range(TOPK)]
        RUN = [sb(f"RUN{n}", te) for n in range(2)]
        M = sb("M", [P, TILES])
        R = sb("R", [P, TILES])
        PF = sb("PF", [P, TILES])
        WSUM = sb("WSUM", [P, TILES])
        CMP = sb("CMP", [P, EXPERTS, TILES])
        TE = sb("TE", [P, EXPERTS])
        CE = [sb(f"CE{n}", [P, EXPERTS]) for n in range(2)]
        BASE = sb("BASE", [P, EXPERTS])
        CMT = sb("CMT", [P, ETILES, EXPERTS - 1])
        EXF = sb("EXF", [P, ETILES])
        POS = sb("POS", [P, TOPK, TILES], U32)
        SLOT = sb("SLOT", [P, TOPK, TILES], I32)
        PC = pb("PC", [P, 2, TILES * EXPERTS])
        HSC = [min(P, hs - P * m) for m in range(-(-hs // P))]
        NS = len(HSC)
        if hs:
            WSG = sb("WSG", [P, KD, 2 * hs])
            WSD = sb("WSD", [P, NS, D])
            SG = [sb(f"SG{n}", [P, GROUP]) for n in range(2)]
            HS = sb("HS", [P, NS, GROUP])
            PY = [pb(f"PY{n}", [P, GROUP]) for n in range(2)]
            PGT = [pb(f"PGT{n}", [P, GROUP]) for n in range(2)]
            PP = [pb(f"PP{n}", [P, GROUP]) for n in range(2)]
        c_load = sem("c_load")
        vec = sem("vec")
        scores_in = sem("scores_in")
        scored = sem("scored")
        picked = sem("picked")
        counted = sem("counted")
        placed = sem("placed")
        scattered = sem("scattered")
        slots_in = sem("slots_in")
        s_load = sem("s_load")
        hid_full = sem("hid_full")
        sg_ready = sem("sg_ready")
        hs_ready = sem("hs_ready")
        out_full = sem("out_full")
        out_read = [sem(f"out_read{n}") for n in range(2)]
        block = ctx.enter_context(nc.Block())
        flat = LOG[:, :, :, :].rearrange("p g c e -> p (g c) e")
        V = nc.vector

        def over_e(t):
            return t.unsqueeze(2).to_broadcast(te)

        def over_t(t):
            return t.unsqueeze(1).to_broadcast(te)

        @block.sync
        def _(sp):
            for dst, src in ((TRI, tri_d), (REV, rev_d), (TIDX, tile_d), (STEP, step_d),
                             (GB, gate_bias)):
                sp.dma_start(dst[:, :], src).then_inc(c_load, 16)
            sp.dma_start(SLOT[:, :, :], slot_d).then_inc(c_load, 16)
            if hs:
                sp.dma_start(WSG[:, :, :], w_sgate.rearrange("(k p) n -> p k n", p=P)
                             ).then_inc(s_load, 16)
                for m, rows in enumerate(HSC):
                    sp.dma_start(WSD[0:rows, m, :], w_sdown[m * P:m * P + rows, :]
                                 ).then_inc(s_load, 16)

        @block.scalar
        def _(a):
            if sigmoid:
                nc.scalar.activation(SC[:, :, :], flat, ACT.Sigmoid).then_inc(scored, 1)
            else:
                a.wait_ge(scores_in, 1)
                nc.scalar.activation(SC[:, :, :], T[:, :, :], ACT.Exp).then_inc(scored, 1)
            if hs:
                with a.Fori(0, GROUPS) as i:
                    for m in range(NS):
                        a.wait_ge(hid_full, i * NS + m + 1)
                        a.wait_ge(hs_ready, i * NS + max(0, m - 1))
                        nc.scalar.activation(SG[m % 2][0:HSC[m], :], PGT[m % 2][0:HSC[m], :],
                                             ACT.Silu).then_inc(sg_ready, 1)
                    for c in range(1, GT, 2):
                        a.wait_ge(out_full, i * GT + c + 1)
                        nc.scalar.activation(SHARED[:, i, c, :], PP[1][:, 0:D], ACT.Copy
                                             ).then_inc(out_read[1], 1)
                a.wait_ge(out_read[1], GROUPS * GT // 2)

        @block.vector
        def _(v):
            link = chain_of(v, vec)
            link(V.memset(ONES[:, :], 1.0))
            v.wait_ge(c_load, 96)
            if sigmoid:
                v.wait_ge(scored, 1)
                link(V.tensor_tensor(SEL[:, :, :], SC[:, :, :], over_t(GB[:, :]), ALU.add))
            else:
                link(V.tensor_reduce(M[:, :], flat, AX.X, ALU.max))
                V.tensor_tensor(T[:, :, :], flat, over_e(M[:, :]), ALU.subtract
                                ).then_inc(scores_in, 1)
                v.wait_ge(scored, 1)
                link(V.tensor_reduce(M[:, :], SC[:, :, :], AX.X, ALU.add))
                link(V.reciprocal(R[:, :], M[:, :]))
                link(V.tensor_tensor(SC[:, :, :], SC[:, :, :], over_e(R[:, :]), ALU.mult))
                link(V.tensor_copy(SEL[:, :, :], SC[:, :, :]))
            for n in range(TOPK):
                link(V.tensor_reduce(M[:, :], SEL[:, :, :], AX.X, ALU.max))
                link(V.tensor_tensor(EQ[:, :, :], SEL[:, :, :], over_e(M[:, :]), ALU.is_equal))
                link(V.tensor_tensor(T[:, :, :], EQ[:, :, :], over_t(REV[:, :]), ALU.mult))
                link(V.tensor_reduce(R[:, :], T[:, :, :], AX.X, ALU.max))
                link(V.tensor_tensor(O[n][:, :, :], over_t(REV[:, :]), over_e(R[:, :]),
                                     ALU.is_equal))
                link(V.tensor_tensor(T[:, :, :], O[n][:, :, :], SC[:, :, :], ALU.mult))
                link(V.tensor_reduce(WT[:, n, :], T[:, :, :], AX.X, ALU.add))
                if n < TOPK - 1:
                    link(V.scalar_tensor_tensor(out=SEL[:, :, :], in0=O[n][:, :, :], scalar=-BIG,
                                                in1=SEL[:, :, :], op0=ALU.mult, op1=ALU.add))
            if sigmoid:
                link(V.tensor_tensor(WSUM[:, :], WT[:, 0, :], WT[:, 1, :], ALU.add))
                link(V.reciprocal(R[:, :], WSUM[:, :]))
                for n in range(TOPK):
                    link(V.tensor_tensor(WT[:, n, :], WT[:, n, :], R[:, :], ALU.mult))
            V.tensor_tensor(EQ[:, :, :], O[0][:, :, :], O[1][:, :, :], ALU.add
                            ).then_inc(picked, 1)
            v.wait_ge(counted, 1)
            total = PC[:, 1, :].rearrange("p (t e) -> p t e", e=EXPERTS)
            link(V.tensor_copy(RUN[0][:, :, :], total))
            src, d = 0, 1
            while d < TILES:
                link(V.tensor_copy(RUN[1 - src][:, 0:d, :], RUN[src][:, 0:d, :]))
                link(V.tensor_tensor(RUN[1 - src][:, d:, :], RUN[src][:, d:, :],
                                     RUN[src][:, 0:TILES - d, :], ALU.add))
                src, d = 1 - src, 2 * d
            run, other = RUN[src], RUN[1 - src]
            link(V.tensor_tensor(CMP[:, :, :],
                                 run[:, TILES - 1, :].unsqueeze(2)
                                 .to_broadcast([P, EXPERTS, TILES]),
                                 STEP[:, :].unsqueeze(1).to_broadcast([P, EXPERTS, TILES]),
                                 ALU.is_gt))
            link(V.tensor_reduce(TE[:, :], CMP[:, :, :], AX.X, ALU.add))
            link(V.tensor_copy(CE[0][:, :], TE[:, :]))
            ce, d = 0, 1
            while d < EXPERTS:
                link(V.tensor_copy(CE[1 - ce][:, 0:d], CE[ce][:, 0:d]))
                link(V.tensor_tensor(CE[1 - ce][:, d:], CE[ce][:, d:],
                                     CE[ce][:, 0:EXPERTS - d], ALU.add))
                ce, d = 1 - ce, 2 * d
            link(V.tensor_tensor(BASE[:, :], CE[ce][:, :], TE[:, :], ALU.subtract))
            link(V.tensor_scalar(BASE[:, :], BASE[:, :], float(P), -1.0, ALU.mult, ALU.add))
            link(V.tensor_tensor(other[:, :, :], run[:, :, :], total, ALU.subtract))
            link(V.tensor_tensor(POSF[:, :, :], other[:, :, :],
                                 PC[:, 0, :].rearrange("p (t e) -> p t e", e=EXPERTS), ALU.add))
            link(V.tensor_tensor(POSF[:, :, :], POSF[:, :, :], over_t(BASE[:, :]), ALU.add))
            for n in range(TOPK):
                link(V.tensor_tensor(T[:, :, :], POSF[:, :, :], O[n][:, :, :], ALU.mult))
                link(V.tensor_reduce(PF[:, :], T[:, :, :], AX.X, ALU.add))
                V.tensor_copy(POS[:, n, :], PF[:, :]).then_inc(placed, 1)
            shape = [P, ETILES, EXPERTS - 1]
            link(V.tensor_tensor(CMT[:, :, :], TIDX[:, :].unsqueeze(2).to_broadcast(shape),
                                 CE[ce][:, 0:EXPERTS - 1].unsqueeze(1).to_broadcast(shape),
                                 ALU.is_ge))
            link(V.tensor_reduce(EXF[:, :], CMT[:, :, :], AX.X, ALU.add))
            link(V.memset(EXP_OF[:, :], 0))
            link(V.tensor_copy(EXP_OF[:, 0:ETILES], EXF[:, :]))
            if hs:
                with v.Fori(0, GROUPS) as i:
                    for m in range(NS):
                        v.wait_ge(sg_ready, i * NS + m + 1)
                        V.tensor_tensor(HS[0:HSC[m], m, :], SG[m % 2][0:HSC[m], :],
                                        PY[m % 2][0:HSC[m], :], ALU.mult).then_inc(hs_ready, 1)
                    for c in range(0, GT, 2):
                        v.wait_ge(out_full, i * GT + c + 1)
                        V.tensor_copy(SHARED[:, i, c, :], PP[0][:, 0:D]
                                      ).then_inc(out_read[0], 1)
                v.wait_ge(out_read[0], GROUPS * GT // 2)

        @block.tensor
        def _(pe):
            pe.wait_ge(picked, 1)
            picks = EQ[:, :, :].rearrange("p t e -> p (t e)")
            nc.tensor.matmul(PC[:, 0, :], TRI[:, :], picks, start=True, stop=True)
            nc.tensor.matmul(PC[:, 1, :], ONES[:, :], picks, start=True, stop=True
                             ).then_inc(counted, 1)
            if hs:
                pe.wait_ge(s_load, 16 * (1 + NS))
                with pe.Fori(0, GROUPS) as i:
                    for m in range(NS):
                        pe.wait_ge(hs_ready, i * NS + max(0, m - 1))
                        for bank, off in ((PY, 0), (PGT, hs)):
                            for k in range(KD):
                                at = off + m * P
                                ins = nc.tensor.matmul(bank[m % 2][0:HSC[m], :],
                                                       WSG[:, k, at:at + HSC[m]],
                                                       HTA[:, i, k, :], start=(k == 0),
                                                       stop=(k == KD - 1))
                        ins.then_inc(hid_full, 1)
                    pe.wait_ge(hs_ready, i * NS + NS)
                    for c in range(GT):
                        pe.wait_ge(out_read[c % 2], i * (GT // 2) + c // 2)
                        for m in range(NS):
                            ins = nc.tensor.matmul(PP[c % 2][:, 0:D],
                                                   HS[0:HSC[m], m, c * P:(c + 1) * P],
                                                   WSD[0:HSC[m], m, :], start=(m == 0),
                                                   stop=(m == NS - 1))
                        ins.then_inc(out_full, 1)

        @block.gpsimd
        def _(g):
            slots = XN[:, :, :, D].rearrange("p g c -> p (g c)").bitcast(I32)
            g.wait_ge(c_load, 96)
            for n in range(TOPK):
                wait(g, scattered, 16 * TILES * n)
                nc.gpsimd.tensor_copy(slots, SLOT[:, n, :]).then_inc(slots_in, 1)
                g.wait_ge(slots_in, n + 1)
                g.wait_ge(placed, n + 1)
                for t in range(TILES):
                    g.indirect_dma_start(
                        out=xs, out_offset=bass.IndirectOffsetOnAxis(ap=POS[:, n, t:t + 1], axis=0),
                        in_=XN[:, t // GT, t % GT, :], in_offset=None).then_inc(scattered, 16)
            g.wait_ge(scattered, 16 * TOPK * TILES)


def expert_stage(nc, EXP_OF, WU, WD, w_load, xs, ys, ident_d, hid):
    with ExitStack() as ctx:
        s = Scope(nc, ctx, f"ex{hid}")
        sb, pb, sem = s.sb, s.pb, s.sem
        HC, HP = hidden_cut(hid)
        IDENT = sb("IDENT", [P, P])
        XG = [sb(f"XG{n}", [P, ROW]) for n in range(AHEAD)]
        XT = [sb(f"XT{n}", [P, KD, P]) for n in range(2)]
        SG = [sb(f"SG{n}", [P, hid]) for n in range(2)]
        HH = [sb(f"HH{n}", [P, hid]) for n in range(2)]
        HT = [sb(f"HT{n}", [P, HC, P]) for n in range(2)]
        YO = [sb(f"YO{n}", [P, D]) for n in range(AHEAD)]
        PAUSE = sb("PAUSE", [P, 1])
        PX = pb("PX", [P, GROUP])
        PGA = [pb(f"PGA{n}", [P, GROUP]) for n in range(2)]
        PUP = [pb(f"PUP{n}", [P, GROUP]) for n in range(2)]
        PH = pb("PH", [P, GROUP])
        PY = [pb(f"PY{n}", [P, GROUP]) for n in range(2)]
        c_load = sem("c_load")
        x_load = [sem(f"x_load{n}") for n in range(AHEAD)]
        xt_full = sem("xt_full")
        xt_read = sem("xt_read")
        gate_full = sem("gate_full")
        up_full = sem("up_full")
        sg_ready = sem("sg_ready")
        hh_ready = sem("hh_ready")
        ht_full = sem("ht_full")
        ht_read = sem("ht_read")
        y_full = sem("y_full")
        y_read = sem("y_read")
        stored = [sem(f"stored{n}") for n in range(AHEAD)]
        pause = sem("pause")
        block = ctx.enter_context(nc.Block())
        ROUNDS = ETILES // AHEAD
        xs_rounds = xs.rearrange("(i n p) d -> i n p d", n=AHEAD, p=P)

        @block.sync
        def _(sp):
            sp.dma_start(IDENT[:, :], ident_d).then_inc(c_load, 16)
            for n in range(AHEAD):
                sp.dma_start(XG[n][:, :], xs_rounds[0, n]).then_inc(x_load[n], 16)
            with sp.Fori(0, ROUNDS) as i:
                for n in range(AHEAD):
                    sp.wait_ge(stored[n], i * 16 + 16)
                    sp.dma_start(XG[n][:, :], xs_rounds[i + 1, n]).then_inc(x_load[n], 16)
            for n in range(AHEAD):
                sp.wait_ge(x_load[n], 16 * (ROUNDS + 1))

        @block.gpsimd
        def _(g):
            nc.gpsimd.memset(PAUSE[:, :], 1.0).then_inc(pause, 1)
            with g.Fori(0, ROUNDS) as i:
                for n in range(AHEAD):
                    t = i * AHEAD + n
                    g.wait_ge(pause, t + 1)
                    g.wait_ge(y_read, t + 1)
                    nc.gpsimd.tensor_tensor(PAUSE[:, :], PAUSE[:, :], PAUSE[:, :], ALU.mult
                                            ).then_inc(pause, 1)
                    g.indirect_dma_start(
                        out=ys, out_offset=bass.IndirectOffsetOnAxis(
                            ap=XG[n][:, D:ROW].bitcast(U32), axis=0),
                        in_=YO[n][:, :], in_offset=None).then_inc(stored[n], 16)
            g.wait_ge(pause, ETILES + 1)
            for n in range(AHEAD):
                g.wait_ge(stored[n], 16 * ROUNDS)

        @block.scalar
        def _(a):
            def silu(t, m):
                a.wait_ge(gate_full, t + 1)
                nc.scalar.activation(SG[m][:, :], PGA[m][:, 0:hid], ACT.Silu
                                     ).then_inc(sg_ready, 1)
            silu(0, 0)
            with a.Fori(0, ROUNDS) as i:
                for n in range(AHEAD):
                    t = i * AHEAD + n
                    a.wait_ge(hh_ready, t)
                    silu(t + 1, 1 - n % 2)
                    a.wait_ge(ht_full, t + 1)
                    nc.scalar.activation(HT[n % 2][0:HP, :, :].rearrange("p c t -> p (c t)"),
                                         PH[0:HP, 0:HC * P], ACT.Copy).then_inc(ht_read, 1)

        @block.vector
        def _(v):
            def turned(t, m):
                v.wait_ge(xt_full, t + 1)
                nc.vector.tensor_copy(XT[m][:, :, :].rearrange("p k t -> p (k t)"), PX[:, 0:D]
                                      ).then_inc(xt_read, 1)

            def hidden(t, m):
                v.wait_ge(sg_ready, t + 1)
                v.wait_ge(up_full, t + 1)
                nc.vector.tensor_tensor(HH[m][:, :], SG[m][:, :], PUP[m][:, 0:hid], ALU.mult
                                        ).then_inc(hh_ready, 1)
            turned(0, 0)
            turned(1, 1)
            hidden(0, 0)
            with v.Fori(0, ROUNDS) as i:
                for n in range(AHEAD):
                    t = i * AHEAD + n
                    hidden(t + 1, 1 - n % 2)
                    turned(t + 2, n % 2)
                    v.wait_ge(y_full, t + 1)
                    v.wait_ge(stored[n], i * 16)
                    nc.vector.tensor_copy(YO[n][:, :], PY[n % 2][:, 0:D]).then_inc(y_read, 1)

        @block.tensor
        def _(pe):
            def turn(t, n, loads):
                pe.wait_ge(x_load[n], loads * 16)
                wait(pe, xt_read, t)
                for k in range(KD):
                    ins = nc.tensor.transpose(PX[:, k * P:(k + 1) * P],
                                              XG[n][:, k * P:(k + 1) * P], IDENT[:, :])
                ins.then_inc(xt_full, 1)

            def project(m, bank, e, at, full):
                for k in range(KD):
                    ins = nc.tensor.matmul(bank[m][:, 0:hid], XT[m][:, k, :],
                                           WU[:, e, k, at:at + hid], start=(k == 0),
                                           stop=(k == KD - 1))
                ins.then_inc(full, 1)

            def expert(t):
                at = slice(t, t + 1) if isinstance(t, int) else bass.ds(t, 1)
                return pe.value_load(EXP_OF[0:1, at], min_val=0, max_val=EXPERTS - 1)

            pe.wait_ge(c_load, 16)
            turn(0, 0, 1)
            pe.wait_ge(w_load, 32 * EXPERTS)
            first = expert(0)
            pe.wait_ge(xt_read, 1)
            project(0, PGA, first, 0, gate_full)
            project(0, PUP, first, hid, up_full)
            turn(1, 1, 1)
            with pe.Fori(0, ROUNDS) as i:
                here = expert(i * AHEAD)
                for n in range(AHEAD):
                    t = i * AHEAD + n
                    m = 1 - n % 2
                    ahead = expert(t + 1)
                    pe.wait_ge(xt_read, t + 2)
                    pe.wait_ge(sg_ready, t)
                    project(m, PGA, ahead, 0, gate_full)
                    pe.wait_ge(hh_ready, t + 1)
                    pe.wait_ge(ht_read, t)
                    for c in range(HC):
                        ins = nc.tensor.transpose(PH[0:HP, c * P:(c + 1) * P],
                                                  HH[n % 2][:, c * HP:(c + 1) * HP], IDENT[:, :])
                    ins.then_inc(ht_full, 1)
                    project(m, PUP, ahead, hid, up_full)
                    turn(t + 2, (n + 2) % AHEAD, i + 1 + (n + 2) // AHEAD)
                    pe.wait_ge(ht_read, t + 1)
                    pe.wait_ge(y_read, i * AHEAD + max(0, n - 1))
                    for c in range(HC):
                        ins = nc.tensor.matmul(PY[n % 2][:, 0:D], HT[n % 2][0:HP, c, :],
                                               WD[0:HP, here, c, :], start=(c == 0),
                                               stop=(c == HC - 1))
                    ins.then_inc(y_full, 1)
                    here = ahead


def hidden_cut(hid):
    chunks = max(2, hid // P)
    return chunks, hid // chunks


def combine_stage(nc, X, WT, SHARED, ys, out, hs):
    with ExitStack() as ctx:
        s = Scope(nc, ctx, f"cb{hs}")
        sb, sem = s.sb, s.sem
        GY = sb("GY", [P, GROUPS, TOPK, GT, D])
        STAT = sb("STAT", [P, GT, 6])
        MV = [sb(f"MV{n}", [P, GT, 2]) for n in range(2)]
        VE = [sb(f"VE{n}", [P, GT]) for n in range(2)]
        RSTD = [sb(f"RSTD{n}", [P, GT]) for n in range(2)]
        STD = [sb(f"STD{n}", [P, GT]) for n in range(2)]
        PAUSE = sb("PAUSE", [P, 1])
        A = [sb(f"A{n}", [P, GT, D]) for n in range(2)]
        U = [sb(f"U{n}", [P, GT, D]) for n in range(2)]
        UN = sb("UN", [P, GT, D])
        loaded = [sem(f"loaded{n}") for n in range(2)]
        weighted = sem("weighted")
        summed = sem("summed")
        added = sem("added")
        vec = sem("vec")
        var_ready = sem("var_ready")
        sqrt_done = sem("sqrt_done")
        un_ready = sem("un_ready")
        x_done = sem("x_done")
        inverted = sem("inverted")
        stored = sem("stored")
        block = ctx.enter_context(nc.Block())
        PAIRS = GROUPS // 2

        def at(t):
            return slice(t, t + 1) if isinstance(t, int) else bass.ds(t, 1)
        slots = ys[0:SLOTS, :].rearrange("(n g c p) d -> g p n c d", n=TOPK, g=GROUPS, c=GT)

        @block.sync
        def _(sp):
            with sp.Fori(0, PAIRS) as i:
                for m in range(2):
                    sp.wait_ge(loaded[m], i * 16 * TOPK)
                    for n in range(TOPK):
                        sp.dma_start(GY[:, i * 2 + m, n, :, :], slots[i * 2 + m, :, n, :, :]
                                     ).then_inc(loaded[m], 16)
            for m in range(2):
                sp.wait_ge(loaded[m], PAIRS * 16 * TOPK)
            if out is not None:
                with sp.Fori(0, GROUPS) as i:
                    sp.wait_ge(x_done, i + 1)
                    sp.dma_start(out[i], X[:, i, :, :]).then_inc(stored, 16)
                sp.wait_ge(stored, 16 * GROUPS)

        @block.scalar
        def _(a):
            def weigh(i, m):
                g = i * 2 + m
                a.wait_ge(loaded[m], (i + 1) * 16 * TOPK)
                wait(a, summed, (i - 1) * 2 * GT + (m + 1) * GT)
                for c in range(GT):
                    nc.scalar.activation(A[m][:, c, :], GY[:, g, 0, c, :], ACT.Copy,
                                         scale=WT[:, 0, at(g * GT + c)]).then_inc(weighted, 1)

            def root(i, m):
                a.wait_ge(var_ready, i * 2 + m + 1)
                nc.scalar.activation(STD[m][:, :], VE[m][:, :], ACT.Sqrt).then_inc(sqrt_done, 1)

            def pair(i, last):
                weigh(i, 1)
                root(i, 0)
                if not last:
                    weigh(i + 1, 0)
                root(i, 1)
            weigh(0, 0)
            pair(0, False)
            with a.Fori(1, PAIRS - 1) as i:
                pair(i, False)
            pair(PAIRS - 1, True)

        @block.gpsimd
        def _(g_):
            G = nc.gpsimd

            def add_x(g):
                g_.wait_ge(un_ready, g * GT + GT)
                G.tensor_tensor(X[:, g, :, :], X[:, g, :, :], UN[:, :, :], ALU.add
                                ).then_inc(x_done, 1)
            with g_.Fori(0, GROUPS) as i:
                add_x(i)
            g_.wait_ge(x_done, GROUPS)

        @block.vector
        def _(v):
            V = nc.vector
            PER = GT + 2

            def gather(i, m):
                g = i * 2 + m
                v.wait_ge(loaded[m], (i + 1) * 16 * TOPK)
                wait(v, un_ready, ((i - 1) * 2 + m + 1) * GT)
                for c in range(GT):
                    v.wait_ge(weighted, g * GT + c + 1)
                    V.scalar_tensor_tensor(
                        out=U[m][:, c, :], in0=GY[:, g, 1, c, :],
                        scalar=WT[:, 1, at(g * GT + c)],
                        in1=A[m][:, c, :], op0=ALU.mult, op1=ALU.add).then_inc(summed, 1)
                if hs:
                    v.wait_ge(summed, g * GT + GT)
                    V.tensor_tensor(U[m][:, :, :], U[m][:, :, :], SHARED[:, g, :, :], ALU.add
                                    ).then_inc(added, 1)

            def moments(i, m):
                g = i * 2 + m
                link = chain_of(v, vec, g * PER)
                if hs:
                    v.wait_ge(added, g + 1)
                else:
                    v.wait_ge(summed, g * GT + GT)
                for c in range(GT):
                    link(V.bn_stats(STAT[:, c, :], U[m][:, c, :]), wait=False)
                v.wait_ge(vec, g * PER + GT)
                link(V.memset(PAUSE[:, :], 0.0), wait=False)
                for c in range(GT):
                    ins = V.bn_aggr(MV[m][:, c, :], STAT[:, c, :])
                link(ins)
                V.tensor_scalar(VE[m][:, :], MV[m][:, :, 1], EPS, None, ALU.add
                                ).then_inc(var_ready, 1)

            def normed(i, m):
                g = i * 2 + m
                v.wait_ge(sqrt_done, g + 1)
                V.reciprocal(RSTD[m][:, :], STD[m][:, :]).then_inc(inverted, 1)
                v.wait_ge(inverted, g + 1)
                wait(v, x_done, g)
                for c in range(GT):
                    V.tensor_scalar(UN[:, c, :], U[m][:, c, :], MV[m][:, c, 0:1],
                                    RSTD[m][:, c:c + 1], ALU.subtract, ALU.mult
                                    ).then_inc(un_ready, 1)

            def pair(i, first):
                gather(i, 0)
                moments(i, 0)
                if not first:
                    normed(i - 1, 1)
                gather(i, 1)
                moments(i, 1)
                normed(i, 0)
            pair(0, True)
            with v.Fori(1, PAIRS) as i:
                pair(i, False)
            normed(PAIRS - 1, 1)
            v.wait_ge(un_ready, GROUPS * GT)


def moe_layer(nc, X, xs, ys, w_router, gate_bias, w_up, w_down, w_sgate, w_sdown, hs, hid,
              consts, out):
    tag = f"moe{hs}_"
    HC, HP = hidden_cut(hid)
    with ExitStack() as ctx:
        w_load = Scope(nc, ctx, f"moe{hs}").sem("w_load")

        def keep(name, shape, dt=F32):
            return ctx.enter_context(nc.sbuf_tensor(tag + name, shape, dt))
        WT = keep("WT", [P, TOPK, TILES])
        SHARED = keep("SHARED", [P, GROUPS, GT, D]) if hs else None
        with nc.sbuf_tensor(tag + "EXP_OF", [P, XS_TILES], I32) as EXP_OF, \
                nc.sbuf_tensor(tag + "WU", [P, EXPERTS, KD, 2 * hid], F32) as WU, \
                nc.sbuf_tensor(tag + "WD", [P, EXPERTS, HC, D], F32) as WD:
            loads = []
            for e in range(EXPERTS):
                loads += [(WU[:, e, :, :], w_up[e].rearrange("(k p) n -> p k n", p=P)),
                          (WD[0:HP, e, :, :], w_down[e].rearrange("(k p) n -> p k n", p=HP))]
            with ExitStack() as inner:
                def hold(name, shape):
                    return inner.enter_context(nc.sbuf_tensor(tag + name, shape, F32))
                XN = hold("XN", [P, GROUPS, GT, ROW])
                HTA = hold("HTA", [P, GROUPS, KD, GROUP]) if hs else None
                LOG = hold("LOG", [P, GROUPS, GT, EXPERTS])
                route_stage(nc, X, XN, HTA, LOG, w_router, consts["ident"], loads, w_load, hs)
                dispatch_stage(nc, XN, HTA, LOG, WT, EXP_OF, SHARED, gate_bias, w_sgate,
                               w_sdown, consts["tri"], consts["rev"], consts["tidx"],
                               consts["step"], consts["slot"], xs, hs)
            expert_stage(nc, EXP_OF, WU, WD, w_load, xs, ys, consts["ident"], hid)
        combine_stage(nc, X, WT, SHARED, ys, out, hs)

AH_HEADS, AH_DIM = 16, 16
SCALE = float(D) ** -0.5
AT = SEQ // P
HALVES = SEQ // GROUP
PAIRED = AH_HEADS // 2
QUADS = AH_HEADS // 4
VW = AH_DIM + 1
SHIFT_ROW = 32
MW = 64 + SHIFT_ROW + 1


def attention_stage(nc, X, wq, bq, wk, bk, wv, bv, wo, bo, ident_d, stack_d, one_row_d):
    with ExitStack() as ctx:
        s = Scope(nc, ctx, "at")
        sb, pb, sem = s.sb, s.pb, s.sem
        IDENT = sb("IDENT", [P, P])
        IDENTR = sb("IDENTR", [P, P], F32R)
        WQ = sb("WQ", [P, KD, D])
        WK = sb("WK", [P, KD, D])
        WV = sb("WV", [P, KD, AH_HEADS * VW])
        WO = sb("WO", [P, KD, D])
        BQ = sb("BQ", [P, KD])
        BK = sb("BK", [P, KD])
        BV = sb("BV", [P, AH_HEADS * VW])
        BO = sb("BO", [P, D])
        STACK = sb("STACK", [P, 4, 4, P], F32R)
        ONE_ROW = sb("ONE_ROW", [P, 1])
        MHALF = sb("MHALF", [P, GT])
        STATX, STATU = (sb(n, [P, HALVES, GT, 6]) for n in ("STATX", "STATU"))
        MVX, MVU = (sb(n, [P, HALVES, GT, 2]) for n in ("MVX", "MVU"))
        RSTDX, RSTDU = (sb(n, [P, HALVES, GT]) for n in ("RSTDX", "RSTDU"))
        VE = sb("VE", [P, GT])
        EPSC = sb("EPSC", [P, GT])
        PAUSE = sb("PAUSE", [P, 1])
        H = sb("H", [P, GT, D])
        HT = sb("HT", [P, KD, GROUP])
        FQK = sb("FQK", [P, 2, KD, GROUP])
        F = [FQK[:, n, :, :] for n in range(2)]
        HI = [sb(f"HI{n}", [P, KD, GROUP], F32R) for n in range(2)]
        LO = [sb(f"LO{n}", [P, KD, GROUP], F32R) for n in range(2)]
        QS = sb("QS", [P, PAIRED, SEQ], F32R)
        KS = sb("KS", [P, AH_HEADS, SEQ], F32R)
        VS = sb("VS", [P, AT, AH_HEADS * VW])
        M2 = sb("M2", [P, 4, AT, HALVES])
        MP = sb("MP", [P, AT, 2, MW], F32R)
        PBUF = 8
        PB = [sb(f"PB{n}", [P, GROUP])[:, :] for n in range(PBUF - 4)]
        PB += [H[:, 2 * n:2 * n + 2, :].rearrange("p c d -> p (c d)") for n in range(2)]
        PB += [HT[:, n, :] for n in range(2)]
        OS = sb("OS", [P, GROUP])
        RS = sb("RS", [P, GT, 4])
        ATT = FQK[:, :, :, :].rearrange("p n k (a d) -> p (n k a) d", d=D)
        ATTT = [sb(f"ATTT{n}", [P, D]) for n in range(2)]
        U = ATT
        STAGE = VS[:, :, :].rearrange("p a b -> p (a b)")[:, 0:4 * GROUP]
        NR, NM = 4, 3
        RING = [pb(f"RING{n}", [P, GROUP]) for n in range(NR)]
        MRING = [pb(f"MRING{n}", [P, GROUP]) for n in range(NM)]
        PO = pb("PO", [P, GROUP])

        c_load = sem("c_load")
        prep = sem("prep")
        k_zero = sem("k_zero")
        vec = sem("vec")
        x_vec = sem("x_vec")
        u_vec = sem("u_vec")
        x_gps = sem("x_gps")
        u_gps = sem("u_gps")
        x_stats = sem("x_stats")
        x_rstd = sem("x_rstd")
        u_stats = sem("u_stats")
        u_rstd = sem("u_rstd")
        u_sum = sem("u_sum")
        un_ready = sem("un_ready")
        h_ready = sem("h_ready")
        r_full = sem("r_full")
        r_vec = sem("r_vec")
        r_act = sem("r_act")
        m_full = sem("m_full")
        m_read = sem("m_read")
        hi_ready = sem("hi_ready")
        lo_ready = sem("lo_ready")
        max_ready = sem("max_ready")
        pv_done = sem("pv_done")
        o_read = sem("o_read")
        x_done = sem("x_done")

        plan = []

        def stacked(g):
            return [(("ST", g, n, c), ("va"[c % 2], "vaaa"[c % 4])[n]) for n in range(2)
                    for c in range(PAIRED)]
        now = [(("ST", HALVES - 1, n, c), "va"[c]) for n in range(2) for c in range(2)]
        later = [(("ST", HALVES - 1, n, c), "a") for n in range(2) for c in range(2, PAIRED)]
        for g in range(HALVES):
            plan += [(("T", g, 0), "v"), (("T", g, 1), "a")]
            if g:
                plan += stacked(g - 1)
            plan += [(("F", g, n, k), "v") for n in range(2) for k in range(KD)]
            plan += [(("V", g, c), "v") for c in range(GT)]
        plan += now + later

        def also(quad, g, kt):
            found = []
            if kt == 1 and (quad or g):
                found += [("OT", quad, g - 1) if g else ("OT", quad - 1, HALVES - 1)]
            if quad == QUADS - 1 and g:
                if kt >= AT - GT:
                    found += [("Y", kt - (AT - GT))]
                if AT - GT - 1 <= kt < AT - 1:
                    found += [("AT", kt - (AT - GT - 1))]
            return found
        for quad in range(QUADS):
            for g in range(HALVES):
                for kt in range(AT):
                    plan += [(("S", quad, g, kt, j), "a") for j in range(4)]
                    plan += [(name, "v") for name in also(quad, g, kt)]
        AHEAD_STEPS = HALVES * AT - 2

        def ahead(step):
            units = 4 * AT * HALVES
            return range(units * step // AHEAD_STEPS,
                         min(units, units * (step + 1) // AHEAD_STEPS))
        LAST = [("AT", GT), ("AT", GT + 1), ("Y", GT), ("AT", GT + 2), ("Y", GT + 1),
                ("AT", GT + 3), ("Y", GT + 2), ("Y", GT + 3)]
        plan += [(("OT", QUADS - 1, HALVES - 1), "v")]
        plan += [(name, "a" if name[0] == "AT" else "v") for name in LAST]
        while len(plan) % NR:
            plan += [(("pad", len(plan)), "v")]
        NUNITS = len(plan)
        seat, readers = {}, {"v": 0, "a": 0}
        for u, (name, who) in enumerate(plan):
            readers[who] += 1
            seat[name] = (u, who, readers[who])
        ring_read = {"v": r_vec, "a": r_act}
        NMU = QUADS * (4 * AT * HALVES + 2 * HALVES)
        NGROUPS = QUADS * HALVES * AT

        def wait_read(eng, i, u):
            _, who, n = seat[plan[u][0]]
            eng.wait_ge(ring_read[who], i * readers[who] + n)

        block = ctx.enter_context(nc.Block())

        @block.sync
        def _(sp):
            loads = ((IDENT[:, :], ident_d), (WQ[:, :, :], wq.rearrange("(k p) n -> p k n", p=P)),
                     (WK[:, :, :], wk.rearrange("(k p) n -> p k n", p=P)),
                     (WV[:, :, :], wv.rearrange("(k p) n -> p k n", p=P)),
                     (WO[:, :, :], wo.rearrange("(k p) n -> p k n", p=P)),
                     (BQ[:, :], bq), (BK[:, :], bk), (BV[:, :], bv), (BO[:, :], bo),
                     (ONE_ROW[:, :], one_row_d),
                     (STAGE, stack_d.rearrange("p a b -> p (a b)")))
            for dst, src in loads:
                sp.dma_start(dst, src).then_inc(c_load, 16)
            sp.wait_ge(c_load, 16 * len(loads))
        CLOAD = 16 * 11

        @block.gpsimd
        def _(g):
            nc.gpsimd.memset(KS[HALF[1], 0::2, :].bitcast(F32), 0.0).then_inc(k_zero, 1)
            g.wait_ge(k_zero, 1)
            g.wait_ge(prep, 2)

            def inverse_std(mv, out, count, stats, chain, done):
                g.wait_ge(stats, count * GT)
                nc.gpsimd.tensor_tensor(VE[:, :], mv[:, :, 1], EPSC[:, :], ALU.add
                                        ).then_inc(chain, 1)
                g.wait_ge(chain, count)
                nc.gpsimd.tensor_tensor(out, VE[:, :], MHALF[:, :], ALU.pow).then_inc(done, 1)
                g.wait_ge(done, count)

            def inputs(i):
                for h in range(HALVES):
                    inverse_std(MVX[:, h, :, :], RSTDX[:, h, :], i * HALVES + h + 1, x_stats,
                                x_gps, x_rstd)

            def outputs(i):
                for h in range(HALVES):
                    inverse_std(MVU[:, h, :, :], RSTDU[:, h, :], i * HALVES + h + 1, u_stats,
                                u_gps, u_rstd)
                    x = X[:, i * HALVES + h, :, :]
                    g.wait_ge(un_ready, (i * HALVES + h + 1) * GT)
                    nc.gpsimd.tensor_tensor(x, x, U[:, h * GT:(h + 1) * GT, :], ALU.add
                                            ).then_inc(x_done, 1)
                    g.wait_ge(x_done, i * HALVES + h + 1)
            inputs(0)
            with g.Fori(0, BATCH - 1) as i:
                inputs(i + 1)
                outputs(i)
            outputs(BATCH - 1)

        @block.vector
        def _(v):
            V = nc.vector
            V.memset(MHALF[:, :], -0.5).then_inc(prep, 1)
            V.memset(EPSC[:, :], EPS).then_inc(prep, 1)
            V.memset(MP[:, :, :, :].bitcast(F32), 0.0).then_inc(prep, 1)
            V.memset(PO[:, :], 0.0).then_inc(prep, 1)
            V.memset(KS[HALF[0], 1::2, :].bitcast(F32), 0.0).then_inc(prep, 1)
            v.wait_ge(c_load, CLOAD)
            V.tensor_copy(STACK[:, :, :, :].rearrange("p a b c -> p (a b c)"),
                          STAGE).then_inc(prep, 1)
            V.tensor_copy(IDENTR[:, :], IDENT[:, :]).then_inc(prep, 1)
            V.tensor_scalar(BQ[:, :], BQ[:, :], SCALE, None, ALU.mult).then_inc(prep, 1)
            v.wait_ge(prep, 8)
            PER = QUADS * HALVES

            def moments(src, stat, mv, chain, at, done):
                for c in range(GT):
                    V.bn_stats(stat[:, c, :], src[c]).then_inc(chain, 1)
                v.wait_ge(chain, at + GT)
                V.memset(PAUSE[:, :], 0.0).then_inc(chain, 1)
                for c in range(GT):
                    V.bn_aggr(mv[:, c, :], stat[:, c, :]).then_inc(done, 1)

            def moments_x(i, g):
                at = i * HALVES + g
                moments([X[:, at, c, :] for c in range(GT)], STATX[:, g, :, :],
                        MVX[:, g, :, :], x_vec, at * (GT + 1), x_stats)

            def body(i, last):
                link = chain_of(v, vec, i * PER)
                m_at = [0]

                def take(name):
                    u, who, _ = seat[name]
                    v.wait_ge(r_full, i * NUNITS + u + 1)
                    return RING[u % NR]

                def mtake():
                    v.wait_ge(m_full, i * NMU + m_at[0] + 1)
                    m_at[0] += 1
                    return MRING[(m_at[0] - 1) % NM]

                def normed_x(g):
                    at = i * HALVES + g
                    v.wait_ge(x_rstd, at + 1)
                    for c in range(GT):
                        V.tensor_scalar(H[:, c, :], X[:, at, c, :], MVX[:, g, c, 0:1],
                                        RSTDX[:, g, c:c + 1], ALU.subtract, ALU.mult
                                        ).then_inc(h_ready, 1)

                def moments_u(g):
                    at = i * HALVES + g
                    v.wait_ge(u_sum, at * GT + GT)
                    moments([U[:, g * GT + c, :] for c in range(GT)], STATU[:, g, :, :],
                            MVU[:, g, :, :], u_vec, at * (GT + 1), u_stats)

                def normed_u(g):
                    at = i * HALVES + g
                    v.wait_ge(u_rstd, at + 1)
                    for c in range(GT):
                        u = U[:, g * GT + c, :]
                        V.tensor_scalar(u, u, MVU[:, g, c, 0:1], RSTDU[:, g, c:c + 1],
                                        ALU.subtract, ALU.mult).then_inc(un_ready, 1)

                def turned(t):
                    V.tensor_copy(ATTT[t % 2][:, :], take(("AT", t))[:, 0:D]).then_inc(r_vec, 1)

                def output(t):
                    V.tensor_tensor(U[:, t, :], take(("Y", t))[:, 0:D], BO[:, :], ALU.add
                                    ).then_inc(u_sum, 1)
                    v.wait_ge(u_sum, i * AT + t + 1)
                    V.memset(PAUSE[:, :], 0.0).then_inc(r_vec, 1)

                def stacks(units):
                    for name, who in units:
                        if who != "v":
                            continue
                        _, g, n, c = name
                        bank = take(name)
                        cols = slice(g * GROUP, (g + 1) * GROUP)
                        if n:
                            for h, rows in enumerate(HALF):
                                ins = V.tensor_scalar(KS[rows, 2 * c + h, cols], bank[rows, :],
                                                      ONE_ROW[rows, 0:1], None, ALU.add)
                        else:
                            ins = V.tensor_copy(QS[:, c, cols], bank[:, :])
                        ins.then_inc(r_vec, 1)

                wait(v, pv_done, i * NGROUPS)
                normed_x(0)
                wait(v, x_done, i * HALVES)
                for g in range(HALVES):
                    V.tensor_copy(HT[:, 0, :], take(("T", g, 0))[:, :]).then_inc(r_vec, 1)
                    if g:
                        stacks(stacked(g - 1))
                    for n, bias in ((0, BQ), (1, BK)):
                        for k in range(KD):
                            bank = take(("F", g, n, k))
                            V.tensor_scalar(F[n][:, k, :], bank[:, :], 1.0 if n else SCALE,
                                            bias[:, k:k + 1], ALU.mult, ALU.add
                                            ).then_inc(r_vec, 1)
                    if g < HALVES - 1:
                        normed_x(g + 1)
                    for c in range(GT):
                        bank = take(("V", g, c))
                        V.tensor_tensor(VS[:, g * GT + c, :], bank[:, 0:AH_HEADS * VW], BV[:, :],
                                        ALU.add
                                        ).then_inc(r_vec, 1)
                    for n in range(2):
                        v.wait_ge(hi_ready, (i * HALVES + g) * 2 + n + 1)
                        V.tensor_tensor(LO[n][:, :, :], F[n][:, :, :],
                                        HI[n][:, :, :].bitcast(F32), ALU.subtract
                                        ).then_inc(lo_ready, 1)
                stacks(now)

                def maxima(n):
                    j, qt, half = n // (AT * HALVES), n // HALVES % AT, n % HALVES
                    bank = mtake()
                    V.tensor_reduce(M2[:, j, qt, half:half + 1], bank[:, :], AX.X, ALU.max
                                    ).then_inc(m_read, 1)

                def shifts(quad):
                    v.wait_ge(m_read, i * NMU + m_at[0])
                    for j in range(4):
                        at = SHIFT_ROW + 64 * (j % 2)
                        V.tensor_reduce(MP[:, :, j // 2, at:at + 1], M2[:, j, :, :], AX.X, ALU.max,
                                        negate=True).then_inc(max_ready, 1)
                    for cc in range(2):
                        for half in range(HALVES):
                            bank = mtake()
                            q = QS[0:MW, quad * 2 + cc, half * GROUP:(half + 1) * GROUP]
                            V.tensor_tensor(q, q.bitcast(F32), bank[0:MW, :], ALU.add
                                            ).then_inc(m_read, 1)

                def normalise(quad, g):
                    bank = take(("OT", quad, g))
                    o = bank[:, :].rearrange("p (t j d) -> p t j d", t=GT, j=4)
                    link(V.reciprocal(RS[:, :, :].unsqueeze(3), o[:, :, :, AH_DIM:AH_DIM + 1]))
                    out = ATT[:, g * GT:(g + 1) * GT, quad * 64:(quad + 1) * 64]
                    V.tensor_tensor(out.rearrange("p t (j d) -> p t j d", j=4),
                                    o[:, :, :, 0:AH_DIM],
                                    RS[:, :, :].unsqueeze(3).to_broadcast([P, GT, 4, AH_DIM]),
                                    ALU.mult).then_inc(r_vec, 1)

                UNITS1 = 4 * AT * HALVES
                for n in range(UNITS1):
                    maxima(n)
                shifts(0)
                for quad in range(QUADS):
                    for step in range(HALVES * AT):
                        if quad < QUADS - 1:
                            for n in ahead(step):
                                maxima(n)
                            if step == AHEAD_STEPS:
                                shifts(quad + 1)
                        g, kt = step // AT, step % AT
                        for name in also(quad, g, kt):
                            if name[0] == "OT":
                                normalise(name[1], name[2])
                            elif name[0] == "AT":
                                turned(name[1])
                            else:
                                output(name[1])
                        if quad == QUADS - 1 and not last and g == 0 and kt in (3, 5):
                            moments_x(i + 1, kt // 5)
                normalise(QUADS - 1, HALVES - 1)
                moments_u(0)
                for name in LAST:
                    if name[0] == "Y":
                        output(name[1])
                    if name == ("Y", GT):
                        normed_u(0)
                moments_u(1)
                normed_u(1)
                for name, _ in plan:
                    if name[0] == "pad":
                        take(name)
                        V.tensor_copy(RS[:, 0, 0:1], MHALF[:, 0:1]).then_inc(r_vec, 1)
                        v.wait_ge(r_vec, i * readers["v"] + seat[name][2])
                assert m_at[0] == NMU
                assert link.n[0] == PER, link.n[0]

            moments_x(0, 0)
            moments_x(0, 1)
            with v.Fori(0, BATCH - 1) as i:
                body(i, False)
            body(BATCH - 1, True)
            v.wait_ge(x_done, BATCH * HALVES)

        @block.scalar
        def _(a):
            a.wait_ge(prep, 8)
            with a.Fori(0, BATCH) as i:
                def take(name):
                    u, who, _ = seat[name]
                    a.wait_ge(r_full, i * NUNITS + u + 1)
                    return RING[u % NR]
                def stacks(units):
                    for name, who in units:
                        if who != "a":
                            continue
                        _, g, n, c = name
                        bank = take(name)
                        cols = slice(g * GROUP, (g + 1) * GROUP)
                        if n:
                            for h, rows in enumerate(HALF):
                                ins = nc.scalar.activation(
                                    KS[rows, 2 * c + h, cols], bank[rows, :], ACT.Identity,
                                    bias=ONE_ROW[rows, 0:1])
                        else:
                            ins = nc.scalar.activation(QS[:, c, cols], bank[:, :], ACT.Copy)
                        ins.then_inc(r_act, 1)

                for g in range(HALVES):
                    nc.scalar.activation(HT[:, 1, :], take(("T", g, 1))[:, :], ACT.Copy
                                         ).then_inc(r_act, 1)
                    if g:
                        stacks(stacked(g - 1))
                    for n in range(2):
                        wait_read(a, i, seat[("F", g, n, KD - 1)][0])
                        nc.scalar.activation(HI[n][:, :, :], F[n][:, :, :], ACT.Copy
                                             ).then_inc(hi_ready, 1)
                stacks(now + later)
                for quad in range(QUADS):
                    for g in range(HALVES):
                        for kt in range(AT):
                            step = (quad * HALVES + g) * AT + kt
                            if step >= PBUF // 4:
                                a.wait_ge(pv_done, i * NGROUPS + step - PBUF // 4 + 1)
                            for j in range(4):
                                bank = take(("S", quad, g, kt, j))
                                nc.scalar.activation(PB[(step * 4 + j) % PBUF], bank[:, :],
                                                     ACT.Exp).then_inc(r_act, 1)
                            if kt == 0 and (quad or g):
                                n = quad * HALVES + g
                                a.wait_ge(pv_done, i * NGROUPS + n * AT)
                                nc.scalar.activation(OS[:, :], PO[:, :], ACT.Copy
                                                     ).then_inc(o_read, 1)
                a.wait_ge(pv_done, i * NGROUPS + NGROUPS)
                a.wait_ge(o_read, i * QUADS * HALVES + QUADS * HALVES - 1)
                nc.scalar.activation(OS[:, :], PO[:, :], ACT.Copy).then_inc(o_read, 1)
                for t in range(GT, AT):
                    nc.scalar.activation(ATTT[t % 2][:, :], take(("AT", t))[:, 0:D], ACT.Copy
                                         ).then_inc(r_act, 1)

        @block.tensor
        def _(pe):
            T = nc.tensor
            pe.wait_ge(prep, 8)
            pe.wait_ge(k_zero, 1)
            with pe.Fori(0, BATCH) as i:
                m_at = [0]
                order = [0]

                def put(name):
                    u, _, _ = seat[name]
                    assert u == order[0], (name, u, order[0])
                    order[0] += 1
                    if u >= NR:
                        wait_read(pe, i, u - NR)
                    return RING[u % NR]

                def mput():
                    n = m_at[0]
                    m_at[0] += 1
                    pe.wait_ge(m_read, i * NMU + max(0, n - NM + 1))
                    return MRING[n % NM]

                pe.wait_ge(r_vec, i * readers["v"])
                pe.wait_ge(r_act, i * readers["a"])
                def stack(name):
                    _, g, n, c = name
                    pe.wait_ge(lo_ready, (i * HALVES + g) * 2 + n + 1)
                    bank = put(name)
                    k, cc = c // 4, c % 4
                    T.matmul(bank[:, :], STACK[:, 2 * n, cc, :], HI[n][:, k, :], start=True,
                             stop=False)
                    T.matmul(bank[:, :], STACK[:, 2 * n + 1, cc, :], LO[n][:, k, :],
                             start=False, stop=True).then_inc(r_full, 1)

                def stacks(units):
                    for name, _ in units:
                        stack(name)

                for g in range(HALVES):
                    for k in range(KD):
                        bank = put(("T", g, k))
                        for c in range(GT):
                            pe.wait_ge(h_ready, (i * HALVES + g) * GT + c + 1)
                            ins = T.transpose(bank[:, c * P:(c + 1) * P],
                                              H[:, c, k * P:(k + 1) * P], IDENT[:, :])
                        ins.then_inc(r_full, 1)
                    if g:
                        stacks(stacked(g - 1))
                    wait_read(pe, i, seat[("T", g, 0)][0])
                    wait_read(pe, i, seat[("T", g, 1)][0])
                    for n, w in ((0, WQ), (1, WK)):
                        for m in range(KD):
                            bank = put(("F", g, n, m))
                            for k in range(KD):
                                ins = T.matmul(bank[:, :], w[:, k, m * P:(m + 1) * P], HT[:, k, :],
                                               start=(k == 0), stop=(k == KD - 1))
                            ins.then_inc(r_full, 1)
                    for c in range(GT):
                        bank = put(("V", g, c))
                        for k in range(KD):
                            ins = T.matmul(bank[:, 0:AH_HEADS * VW],
                                           HT[:, k, c * P:(c + 1) * P], WV[:, k, :],
                                           start=(k == 0), stop=(k == KD - 1))
                        ins.then_inc(r_full, 1)
                stacks(now)
                for c in range(2):
                    wait_read(pe, i, seat[("ST", HALVES - 1, 1, c)][0])

                def maxima(quad, n):
                    j, qt, half = n // (AT * HALVES), n // HALVES % AT, n % HALVES
                    c = quad * 2 + j // 2
                    T.matmul(mput()[:, :], QS[:, c, qt * P:(qt + 1) * P],
                             KS[:, quad * 4 + j, half * GROUP:(half + 1) * GROUP], start=True,
                             stop=True).then_inc(m_full, 1)

                def shifts(quad):
                    pe.wait_ge(max_ready, i * QUADS * 4 + quad * 4 + 4)
                    for cc in range(2):
                        for half in range(HALVES):
                            bank = mput()
                            for t in range(GT):
                                ins = T.matmul(bank[0:MW, t * P:(t + 1) * P],
                                               MP[:, half * GT + t, cc, :], IDENTR[:, :],
                                               start=True, stop=True)
                            ins.then_inc(m_full, 1)

                def with_values(step):
                    quad, g, kt = step // (HALVES * AT), step // AT % HALVES, step % AT
                    n = quad * HALVES + g
                    wait_read(pe, i, seat[("S", quad, g, kt, 3)][0])
                    if kt == 0:
                        pe.wait_ge(o_read, i * QUADS * HALVES + n)
                    for j in range(4):
                        head = quad * 4 + j
                        ins = T.matmul(PO[32 * j:32 * j + VW, :],
                                       VS[:, kt, head * VW:(head + 1) * VW],
                                       PB[(step * 4 + j) % PBUF], start=(kt == 0),
                                       stop=(kt == AT - 1))
                    ins.then_inc(pv_done, 1)

                def turn_output(quad, g):
                    pe.wait_ge(o_read, i * QUADS * HALVES + quad * HALVES + g + 1)
                    bank = put(("OT", quad, g))
                    for t in range(GT):
                        ins = T.transpose(bank[:, t * P:(t + 1) * P], OS[:, t * P:(t + 1) * P],
                                          IDENT[:, :])
                    ins.then_inc(r_full, 1)

                def turn_tile(t):
                    wait_read(pe, i, seat[("OT", QUADS - 1, t // GT)][0])
                    bank = put(("AT", t))
                    for k in range(KD):
                        ins = T.transpose(bank[:, k * P:(k + 1) * P],
                                          ATT[:, t, k * P:(k + 1) * P], IDENT[:, :])
                    ins.then_inc(r_full, 1)

                def project(t):
                    wait_read(pe, i, seat[("AT", t)][0])
                    bank = put(("Y", t))
                    for k in range(KD):
                        ins = T.matmul(bank[:, 0:D], ATTT[t % 2][:, k * P:(k + 1) * P],
                                       WO[:, k, :], start=(k == 0), stop=(k == KD - 1))
                    ins.then_inc(r_full, 1)

                for n in range(4 * AT * HALVES):
                    maxima(0, n)
                    if n % 4 == 3 and n // 4 < len(later):
                        stack(later[n // 4][0])
                wait_read(pe, i, seat[later[-1][0]][0])
                shifts(0)
                for quad in range(QUADS):
                    pe.wait_ge(m_read, i * NMU + m_at[0])
                    for step in range(HALVES * AT):
                        g, kt = step // AT, step % AT
                        whole = quad * HALVES * AT + step
                        for j in range(4):
                            c = quad * 2 + j // 2
                            T.matmul(put(("S", quad, g, kt, j))[:, :],
                                     KS[:, quad * 4 + j, kt * P:(kt + 1) * P],
                                     QS[:, c, g * GROUP:(g + 1) * GROUP], start=True,
                                     stop=True).then_inc(r_full, 1)
                            if quad < QUADS - 1:
                                units = ahead(step)
                                for n in units[len(units) * j // 4:len(units) * (j + 1) // 4]:
                                    maxima(quad + 1, n)
                        if step == AHEAD_STEPS and quad < QUADS - 1:
                            shifts(quad + 1)
                        if whole:
                            with_values(whole - 1)
                        for name in also(quad, g, kt):
                            if name[0] == "OT":
                                turn_output(name[1], name[2])
                            elif name[0] == "AT":
                                turn_tile(name[1])
                            else:
                                project(name[1])
                with_values(QUADS * HALVES * AT - 1)
                turn_output(QUADS - 1, HALVES - 1)
                for name in LAST:
                    if name[0] == "AT":
                        turn_tile(name[1])
                    else:
                        project(name[1])
                for name, _ in plan:
                    if name[0] == "pad":
                        T.transpose(put(name)[:, 0:P], IDENT[:, :], IDENT[:, :]
                                    ).then_inc(r_full, 1)


def whole_program(nc, a, out):
    xs = [nc.dram_tensor(f"routed_rows{n}", (XS_TILES * P, ROW), F32, kind="Internal").ap()
          for n in range(2)]
    ys = [nc.dram_tensor(f"expert_rows{n}", (SLOTS + XS_TILES * P, D), F32, kind="Internal").ap()
          for n in range(2)]
    with nc.sbuf_tensor("X", [P, GROUPS, GT, D], F32) as X:
        mamba_stage(nc, X, a["x"], a["w_in"], a["ln_w"], a["ln_b"], a["dt_bias"], a["a_log"],
                    a["d_skip"], a["norm_w"], a["w_out"], a["w_fc1"], a["b_fc1"], a["w_fc2"],
                    a["b_fc2"], a["ident"], a["tri"], a["mask"], a["sel"],
                    a["sel2"], a["keep"], a["fill"], xs)
        moe_layer(nc, X, xs[0], ys[0], a["router0"], a["gate_bias"], a["up0"], a["down0"],
                  a["shared_up"], a["shared_down"], 352, 176, a, None)
        attention_stage(nc, X, a["wq"], a["bq"], a["wk"], a["bk"], a["wv"], a["bv"], a["wo"],
                        a["bo"], a["ident"], a["stack"], a["one_row"])
        moe_layer(nc, X, xs[1], ys[1], a["router1"], a["gate_bias"], a["up1"], a["down1"], None, None,
                  0, 512, a, out)


def _constants(np):
    t = np.arange(P)
    full = lambda v: np.ascontiguousarray(np.broadcast_to(np.asarray(v, np.float32), (P, len(v))))
    c = {
        "ident": np.eye(P, dtype=np.float32),
        "tri": (t[:, None] <= t[None, :]).astype(np.float32),
        "mask": np.tile(np.where(t[:, None] <= t[None, :], 0, -1e30).astype(np.float32), (1, GT)),
        "keep": full(np.arange(GROUPS) % (SEQ // GROUP) != 0),
        "rev": full(EXPERTS - np.arange(EXPERTS)),
        "tidx": full(np.arange(ETILES)),
        "step": full(P * np.arange(TILES)),
        "slot": (np.arange(TOPK)[None, :, None] * TOKENS + np.arange(TILES)[None, None, :] * P
                 + t[:, None, None]).astype(np.int32),
        "fill": (SLOTS + np.arange(XS_TILES * P)).astype(np.int32)[:, None],
    }
    heads = np.eye(GT * HEADS, dtype=np.float32)[:, :, None]
    c["sel"] = np.tile(np.repeat(heads, P, axis=2).reshape(GT * HEADS, -1), (2, 1))
    c["sel2"] = np.tile(np.repeat(heads, P // 2, axis=2).reshape(GT * HEADS, -1), (2, 1))
    stack = np.zeros((P, 4, 4, P), np.float32)
    d = np.arange(AH_DIM)
    for cc in range(4):
        for pair in range(2):
            src, at = (2 * cc + pair) * AH_DIM + d, 64 * pair
            stack[src, 0, cc, at + d] = 1
            stack[src, 0, cc, at + SHIFT_ROW + 1 + d] = 1
            stack[src, 1, cc, at + AH_DIM + d] = 1
            stack[src, 2, cc, at + d] = 1
            stack[src, 2, cc, at + AH_DIM + d] = 1
            stack[src, 3, cc, at + SHIFT_ROW + 1 + d] = 1
    c["stack"] = stack.reshape(P, 4, GROUP)
    c["one_row"] = np.isin(t, (SHIFT_ROW, 64 + SHIFT_ROW)).astype(np.float32)[:, None]
    return c


def _layout(np, v):
    def turned(name):
        return np.swapaxes(v[name], -1, -2)

    def chunked(name):
        return v[name].reshape(-1, P).T

    def rows(name):
        return np.broadcast_to(v[name], (P, v[name].shape[-1]))
    w = turned("L0_attn_in_proj_w")
    cut = np.cumsum([D_INNER, D_XB, HEADDIM, HEADDIM, D_INNER])
    z, x, b0, b1, c, dt = np.split(w, cut, axis=1)
    wv = np.zeros((D, AH_HEADS, VW), np.float32)
    wv[:, :, 0:AH_DIM] = v["L1_attn_wv"].reshape(D, AH_HEADS, AH_DIM)
    bv = np.zeros((AH_HEADS, VW), np.float32)
    bv[:, 0:AH_DIM] = v["L1_attn_bv"].reshape(AH_HEADS, AH_DIM)
    bv[:, AH_DIM] = 1
    a = {
        "x": v["L0_attn_hidden_states"].reshape(GROUPS, GT, P, D).transpose(0, 2, 1, 3),
        "w_in": np.concatenate([z, x, b0, b0, b1, b1, dt, c], axis=1),
        "ln_w": chunked("L0_attn_ln_w"), "ln_b": chunked("L0_attn_ln_b"),
        "dt_bias": rows("L0_attn_dt_bias"), "a_log": rows("L0_attn_A_log"),
        "d_skip": rows("L0_attn_Dp"), "norm_w": chunked("L0_attn_norm_w"),
        "w_out": turned("L0_attn_out_proj_w"), "w_fc1": turned("L0_attn_fc1_w"),
        "b_fc1": chunked("L0_attn_fc1_b"), "w_fc2": turned("L0_attn_fc2_w"),
        "b_fc2": rows("L0_attn_fc2_b"),
        "router0": turned("L0_ffn_gate_w"), "gate_bias": rows("L0_ffn_gate_bias"),
        "shared_up": turned("L0_ffn_shared_gw"), "shared_down": turned("L0_ffn_shared_dw"),
        "up0": turned("L0_ffn_up_w"), "down0": turned("L0_ffn_down_w"),
        "wq": v["L1_attn_wq"], "wk": v["L1_attn_wk"], "wo": v["L1_attn_wo"],
        "wv": wv.reshape(D, AH_HEADS * VW), "bq": chunked("L1_attn_bq"),
        "bk": chunked("L1_attn_bk"),
        "bv": np.broadcast_to(bv.reshape(-1), (P, AH_HEADS * VW)), "bo": rows("L1_attn_bo"),
        "router1": turned("L1_ffn_router_weight"), "up1": turned("L1_ffn_ws"),
        "down1": turned("L1_ffn_w2s"),
    }
    return {k: np.ascontiguousarray(x) for k, x in a.items()}


def kernel(**inputs):
    import numpy as np
    import concourse.bacc as bacc
    from concourse.bass_utils import run_bass_kernel_spmd

    arrays = _layout(np, {k: np.asarray(x) for k, x in inputs.items()})
    arrays.update(_constants(np))
    nc = bacc.Bacc("TRN2", target_bir_lowering=False, num_devices=1)
    aps = {k: nc.dram_tensor(f"in_{k}", x.shape, mybir.dt.from_np(x.dtype),
                             kind="ExternalInput").ap() for k, x in arrays.items()}
    out = nc.dram_tensor("out", (GROUPS, P, GT, D), F32, kind="ExternalOutput").ap()
    whole_program(nc, aps, out)
    r = run_bass_kernel_spmd(nc, [{f"in_{k}": x for k, x in arrays.items()}], core_ids=[0])
    y = r.results[0]["out"]
    return y.transpose(0, 2, 1, 3).reshape(BATCH, SEQ, D)
```
